# Optimizing a Trainium2 kernel written in Bass

```python
import numpy as np
import jax
import jax.numpy as jnp

def _softmax(x, axis=-1):
    return jax.nn.softmax(x, axis=axis)

def _gelu(x):
    return jax.nn.gelu(x, approximate=True)

def _silu(x):
    return jax.nn.silu(x)

def _sigmoid(x):
    return jax.nn.sigmoid(x)

def _layernorm(x, axis=-1, eps=1e-05):
    m = jnp.mean(x, axis=axis, keepdims=True)
    v = jnp.var(x, axis=axis, keepdims=True)
    return (x - m) / jnp.sqrt(v + eps)

def _scatter_add(tgt, idx, src, axis=0):
    return tgt.at[idx].add(src)

def _segment_sum(src, seg, n):
    return jax.ops.segment_sum(src, seg, n)
kernel_name = 'mk_sandwich_d1_jaxref_r2_cee8a8'

def setup_inputs(seed: int=0):
    np.random.seed(seed)
    _w = jnp.asarray

    def _L0_attn_setup():
        import jax, jax.numpy as jnp
        import numpy as np
        EPS = 1e-12

        def _l2norm(t, axis=-1):
            return t / jnp.maximum(jnp.linalg.norm(t, axis=axis, keepdims=True), EPS)

        def _selective_scan(u, delta, A, Bm, Cm, D):
            uT = u.transpose(2, 0, 1)
            dT = delta.transpose(2, 0, 1)
            BT = Bm.transpose(2, 0, 1)
            CT = Cm.transpose(2, 0, 1)
            h0 = jnp.zeros(u.shape[:2] + (A.shape[1],), u.dtype)

            def step(h, inp):
                u_t, d_t, b_t, c_t = inp
                dA = jnp.exp(d_t[..., None] * A)
                h = dA * h + (d_t * u_t)[..., None] * b_t[:, None, :]
                y = jnp.einsum('bdn,bn->bd', h, c_t)
                return (h, y)
            _, ys = jax.lax.scan(step, h0, (uT, dT, BT, CT))
            y = ys.transpose(1, 2, 0)
            return y + D[None, :, None] * u
        key = jax.random.key(seed)
        ks = jax.random.split(key, 8)
        B, N, d_inner, d_state, dt_rank, K = (8, 1024, 512, 16, 32, 8)
        x = jax.random.normal(ks[0], (B, N, d_inner), jnp.float32)
        means = jax.random.normal(ks[1], (K, d_inner), jnp.float32)
        prompt_weight = jax.random.normal(ks[2], (d_state, d_inner), jnp.float32) * d_inner ** (-0.5)
        x_proj_weight = jax.random.normal(ks[3], (dt_rank + 2 * d_state, d_inner), jnp.float32) * d_inner ** (-0.5)
        dt_init_std = dt_rank ** (-0.5)
        dt_projs_weight = jax.random.uniform(ks[4], (d_inner, dt_rank), jnp.float32, -dt_init_std, dt_init_std)
        dt = jnp.exp(jax.random.uniform(ks[5], (d_inner,), jnp.float32) * (np.log(0.1) - np.log(0.001)) + np.log(0.001))
        dt = jnp.clip(dt, 0.0001, None)
        dt_projs_bias = dt + jnp.log(-jnp.expm1(-dt))
        A_logs = jnp.log(jnp.broadcast_to(jnp.arange(1, d_state + 1, dtype=jnp.float32), (d_inner, d_state)))
        Ds = jnp.ones((d_inner,), jnp.float32)
        return {'x': x, 'means': means, 'prompt_weight': prompt_weight, 'x_proj_weight': x_proj_weight, 'dt_projs_weight': dt_projs_weight, 'dt_projs_bias': dt_projs_bias, 'A_logs': A_logs, 'Ds': Ds}
    _L0_attn_in = _L0_attn_setup()

    def _L0_ffn_setup():
        import jax, jax.numpy as jnp
        import numpy as np
        DIM = 512
        NUM_HEAVY = 512
        N_ITERS = 50
        EPS = 1.0
        FETCH_K_RATIO = 9.0 / 8.0

        def rms_norm(x, gamma):
            norm = jnp.maximum(jnp.linalg.norm(x, axis=-1, keepdims=True), 1e-12)
            return x / norm * x.shape[-1] ** 0.5 * gamma

        def feed_forward(x, gamma, w1, b1, w2, b2):
            h = jax.nn.gelu(rms_norm(x, gamma) @ w1 + b1, approximate=False)
            return h @ w2 + b2

        def coor_descent(s, k, n_iters, eps):
            logk = jnp.log(jnp.asarray(k, dtype=s.dtype))

            def step(ab, _):
                a, b = ab
                sb = (s + b) / eps
                a = eps * (logk - jax.scipy.special.logsumexp(sb, axis=-1, keepdims=True))
                b = -jax.nn.relu(s + a)
                return ((a, b), None)
            a0 = jnp.zeros_like(s[..., :1])
            b0 = -s
            (a, b), _ = jax.lax.scan(step, (a0, b0), None, length=n_iters)
            return jnp.exp((s + a + b) / eps)
        key = jax.random.key(seed)
        ks = jax.random.split(key, 8)
        b, n, d = (4, 4096, DIM)
        dl, dh = (int(d * 0.5), d * 4)
        u = lambda k, shape, fan_in: jax.random.uniform(k, shape, jnp.float32, -1.0, 1.0) / np.sqrt(fan_in)
        return {'x': jax.random.normal(ks[0], (b, n, d), jnp.float32), 'routing_token': jax.random.normal(ks[1], (d,), jnp.float32), 'light_gamma': jnp.ones((d,), jnp.float32), 'light_w1': u(ks[2], (d, dl), d), 'light_b1': jnp.zeros((dl,), jnp.float32), 'light_w2': u(ks[3], (dl, d), dl), 'light_b2': jnp.zeros((d,), jnp.float32), 'heavy_gamma': jnp.ones((d,), jnp.float32), 'heavy_w1': u(ks[4], (d, dh), d), 'heavy_b1': jnp.zeros((dh,), jnp.float32), 'heavy_w2': u(ks[5], (dh, d), dh), 'heavy_b2': jnp.zeros((d,), jnp.float32)}
    _L0_ffn_in = _L0_ffn_setup()
    _d = {'L0_attn_x': _L0_attn_in['x'], 'L0_attn_means': _L0_attn_in['means'], 'L0_attn_prompt_weight': _L0_attn_in['prompt_weight'], 'L0_attn_x_proj_weight': _L0_attn_in['x_proj_weight'], 'L0_attn_dt_projs_weight': _L0_attn_in['dt_projs_weight'], 'L0_attn_dt_projs_bias': _L0_attn_in['dt_projs_bias'], 'L0_attn_A_logs': _L0_attn_in['A_logs'], 'L0_attn_Ds': _L0_attn_in['Ds'], 'L0_ffn_routing_token': _L0_ffn_in['routing_token'], 'L0_ffn_light_gamma': _L0_ffn_in['light_gamma'], 'L0_ffn_light_w1': _L0_ffn_in['light_w1'], 'L0_ffn_light_b1': _L0_ffn_in['light_b1'], 'L0_ffn_light_w2': _L0_ffn_in['light_w2'], 'L0_ffn_light_b2': _L0_ffn_in['light_b2'], 'L0_ffn_heavy_gamma': _L0_ffn_in['heavy_gamma'], 'L0_ffn_heavy_w1': _L0_ffn_in['heavy_w1'], 'L0_ffn_heavy_b1': _L0_ffn_in['heavy_b1'], 'L0_ffn_heavy_w2': _L0_ffn_in['heavy_w2'], 'L0_ffn_heavy_b2': _L0_ffn_in['heavy_b2']}
    _x0 = _d['L0_attn_x']
    _d['L0_attn_x'] = jax.random.normal(jax.random.fold_in(jax.random.key(seed), 1), (16, 1024, 512), dtype=_x0.dtype)
    del _x0
    return _d

def reference(L0_attn_x, L0_attn_means, L0_attn_prompt_weight, L0_attn_x_proj_weight, L0_attn_dt_projs_weight, L0_attn_dt_projs_bias, L0_attn_A_logs, L0_attn_Ds, L0_ffn_routing_token, L0_ffn_light_gamma, L0_ffn_light_w1, L0_ffn_light_b1, L0_ffn_light_w2, L0_ffn_light_b2, L0_ffn_heavy_gamma, L0_ffn_heavy_w1, L0_ffn_heavy_b1, L0_ffn_heavy_w2, L0_ffn_heavy_b2):

    def _L0_attn_ref(x, means, prompt_weight, x_proj_weight, dt_projs_weight, dt_projs_bias, A_logs, Ds):
        import jax, jax.numpy as jnp
        import numpy as np
        EPS = 1e-12

        def _l2norm(t, axis=-1):
            return t / jnp.maximum(jnp.linalg.norm(t, axis=axis, keepdims=True), EPS)

        def _selective_scan(u, delta, A, Bm, Cm, D):
            uT = u.transpose(2, 0, 1)
            dT = delta.transpose(2, 0, 1)
            BT = Bm.transpose(2, 0, 1)
            CT = Cm.transpose(2, 0, 1)
            h0 = jnp.zeros(u.shape[:2] + (A.shape[1],), u.dtype)

            def step(h, inp):
                u_t, d_t, b_t, c_t = inp
                dA = jnp.exp(d_t[..., None] * A)
                h = dA * h + (d_t * u_t)[..., None] * b_t[:, None, :]
                y = jnp.einsum('bdn,bn->bd', h, c_t)
                return (h, y)
            _, ys = jax.lax.scan(step, h0, (uT, dT, BT, CT))
            y = ys.transpose(1, 2, 0)
            return y + D[None, :, None] * u
        dt_rank = dt_projs_weight.shape[1]
        d_state = A_logs.shape[1]
        scores = jnp.einsum('bnd,kd->bnk', _l2norm(x), _l2norm(means))
        buckets = jnp.argmax(jax.lax.stop_gradient(scores), axis=-1)
        sort_idx = jnp.argsort(buckets, axis=-1, stable=True)
        inv_idx = jnp.argsort(sort_idx, axis=-1)
        xs = jnp.take_along_axis(x, sort_idx[..., None], axis=1)
        b_sorted = jnp.take_along_axis(buckets, sort_idx, axis=1)
        cluster_prompts = means @ prompt_weight.T
        prompt = cluster_prompts[b_sorted]
        u = xs.transpose(0, 2, 1)
        x_dbl = jnp.einsum('bdl,cd->bcl', u, x_proj_weight)
        dts = x_dbl[:, :dt_rank]
        Bm = x_dbl[:, dt_rank:dt_rank + d_state]
        Cm = x_dbl[:, dt_rank + d_state:] + prompt.transpose(0, 2, 1)
        delta = jax.nn.softplus(jnp.einsum('brl,dr->bdl', dts, dt_projs_weight) + dt_projs_bias[None, :, None])
        A = -jnp.exp(A_logs)
        y = _selective_scan(u, delta, A, Bm, Cm, Ds)
        y = y.transpose(0, 2, 1)
        out = jnp.take_along_axis(y, inv_idx[..., None], axis=1)
        return out

    def _L0_ffn_ref(x, routing_token, light_gamma, light_w1, light_b1, light_w2, light_b2, heavy_gamma, heavy_w1, heavy_b1, heavy_w2, heavy_b2):
        import jax, jax.numpy as jnp
        import numpy as np
        DIM = 512
        NUM_HEAVY = 512
        N_ITERS = 50
        EPS = 1.0
        FETCH_K_RATIO = 9.0 / 8.0

        def rms_norm(x, gamma):
            norm = jnp.maximum(jnp.linalg.norm(x, axis=-1, keepdims=True), 1e-12)
            return x / norm * x.shape[-1] ** 0.5 * gamma

        def feed_forward(x, gamma, w1, b1, w2, b2):
            h = jax.nn.gelu(rms_norm(x, gamma) @ w1 + b1, approximate=False)
            return h @ w2 + b2

        def coor_descent(s, k, n_iters, eps):
            logk = jnp.log(jnp.asarray(k, dtype=s.dtype))

            def step(ab, _):
                a, b = ab
                sb = (s + b) / eps
                a = eps * (logk - jax.scipy.special.logsumexp(sb, axis=-1, keepdims=True))
                b = -jax.nn.relu(s + a)
                return ((a, b), None)
            a0 = jnp.zeros_like(s[..., :1])
            b0 = -s
            (a, b), _ = jax.lax.scan(step, (a0, b0), None, length=n_iters)
            return jnp.exp((s + a + b) / eps)
        b, n, d = x.shape
        light_out = feed_forward(x, light_gamma, light_w1, light_b1, light_w2, light_b2)
        s = jnp.einsum('bnd,d->bn', x, routing_token)
        effective_k = min(NUM_HEAVY * FETCH_K_RATIO, n)
        scores = coor_descent(s, effective_k, N_ITERS, EPS)
        sel_scores, sel_idx = jax.lax.top_k(scores, NUM_HEAVY)
        sel_scores = sel_scores + jax.lax.stop_gradient(1.0 - sel_scores)
        routed = jnp.take_along_axis(x, sel_idx[..., None], axis=1)
        routed_out = feed_forward(routed, heavy_gamma, heavy_w1, heavy_b1, heavy_w2, heavy_b2)
        routed_out = routed_out * sel_scores[..., None]
        batch_idx = jnp.arange(b)[:, None]
        heavy_out = jnp.zeros_like(x).at[batch_idx, sel_idx].set(routed_out)
        return light_out + heavy_out
    x = L0_attn_x
    x = x + _layernorm(_L0_attn_ref(_layernorm(x, axis=-1), L0_attn_means, L0_attn_prompt_weight, L0_attn_x_proj_weight, L0_attn_dt_projs_weight, L0_attn_dt_projs_bias, L0_attn_A_logs, L0_attn_Ds), axis=-1)
    x = x + _layernorm(_L0_ffn_ref(_layernorm(x, axis=-1), L0_ffn_routing_token, L0_ffn_light_gamma, L0_ffn_light_w1, L0_ffn_light_b1, L0_ffn_light_w2, L0_ffn_light_b2, L0_ffn_heavy_gamma, L0_ffn_heavy_w1, L0_ffn_heavy_b1, L0_ffn_heavy_w2, L0_ffn_heavy_b2), axis=-1)
    return x

_drawn_inputs = setup_inputs


def setup_inputs(seed=0):
    import zlib

    import numpy as np

    out = dict(_drawn_inputs(seed))
    spreads = {'L0_attn_Ds': (1.0, 0.2),
     'L0_ffn_light_gamma': (1.0, 0.2),
     'L0_ffn_light_b1': (0.0, 0.1),
     'L0_ffn_light_b2': (0.0, 0.1),
     'L0_ffn_heavy_gamma': (1.0, 0.2),
     'L0_ffn_heavy_b1': (0.0, 0.1),
     'L0_ffn_heavy_b2': (0.0, 0.1)}
    factors = {}
    for name, (base, spread) in spreads.items():
        noise = np.random.default_rng([zlib.crc32(name.encode()), seed]).standard_normal(out[name].shape)
        drawn = base * np.exp(spread * noise) if base else spread * noise
        out[name] = jnp.asarray(drawn.astype(out[name].dtype))
    for name, factor in factors.items():
        out[name] = (out[name] * factor).astype(out[name].dtype)
    return out
```

```python
import math
from contextlib import ExitStack

import concourse.bass as bass
from concourse import mybir

P = 128
F32 = mybir.dt.float32
BF16 = mybir.dt.bfloat16
U32 = mybir.dt.uint32
I32 = mybir.dt.int32
ALU = mybir.AluOpType
ACT = mybir.ActivationFunctionType
AX = mybir.AxisListType.X

LN_EPS = 1e-5
NORM_EPS = 1e-12
NUM_HEAVY = 512
DESCENT_STEPS = 50
EFFECTIVE_K = 576.0
LOG_K = 6.356107660695891


def build(nc, x, means, means_t, prompt_t, w_x, w_c, w_dt_t, dt_bias, a_logs, ds,
          routing, l_gamma, l_w1, l_b1, l_w2, l_b2, h_gamma, h_w1, h_b1, h_w2, h_b2, out):
    B, L, D = x.shape
    NT = L // P
    ND = D // P
    K = means.shape[0]
    NS = w_c.shape[1]
    R = w_dt_t.shape[0]
    FL = l_w1.shape[1] // P
    FH = h_w1.shape[1] // P
    NJ = NUM_HEAVY // P
    PAIRS = B // 2
    KT = K * NT
    DT_ROW = 3 * 32
    SQRT_D = float(D) ** 0.5

    xs_dram = nc.dram_tensor("sorted_rows", [B * L, D], F32, kind="Internal").ap()
    ys_dram = nc.dram_tensor("sorted_outputs", [B * L, D], F32, kind="Internal").ap()
    xl_dram = nc.dram_tensor("residual_and_light", [B * L, 2 * D], F32, kind="Internal").ap()

    x_rows = x.rearrange("b (t p) d -> b p t d", p=P)
    xs_rows = xs_dram.rearrange("(b t p) d -> b p t d", p=P, t=NT)
    ys_rows = ys_dram.rearrange("(b t p) d -> b p t d", p=P, t=NT)
    xl_rows = xl_dram.rearrange("(b t p) d -> b p t d", p=P, t=NT)
    out_flat = out.rearrange("b l d -> (b l) d")
    out_rows = out.rearrange("b (t p) d -> b p t d", p=P)

    def row(view, b):
        return view[bass.ds(b, 1)].rearrange("a p t d -> (a p) t d")

    def at(i, h, per, k):
        return i * (2 * per) + (per * h + k)

    with ExitStack() as ctx:
        def sb(name, shape, dt=F32, c=ctx):
            return c.enter_context(nc.sbuf_tensor(name, shape, dt))

        def sem(name, c=ctx):
            return c.enter_context(nc.semaphore(name))

        gates = sem("gates_passed")

        def gate(eng, signal, value):
            eng.wait_ge(signal, value)
            eng.sem_inc(gates, 1)

        bank = [ctx.enter_context(nc.psum_tensor(f"bank{n}", [P, 512], F32)) for n in range(8)]

        ident = sb("ident", [P, P])
        ones = sb("ones", [P, P])
        positions = sb("positions", [P, (B + 2) * NT], U32)
        bounds = sb("bounds", [K, 2 * B])
        scores = sb("scores", [P, B * NT])
        half = sb("half", [P, NT])
        neg_half = sb("neg_half", [P, NT])
        mean_dirs = sb("mean_dirs", [P, ND, K])
        cluster_c = sb("cluster_c", [K, NS])
        zero_bias = sb("zero_bias", [P, 1])
        one_bias = sb("one_bias", [P, 1])

        with ExitStack() as c:
            means_sb = sb("means_sb", [K, D], c=c)
            means_sq = sb("means_sq", [K, D], c=c)
            mnorm = sb("mnorm", [K, 4], c=c)
            mhalf = sb("mhalf", [K, 1], c=c)
            means_ts = sb("means_ts", [P, ND, K], c=c)
            prompt_ts = sb("prompt_ts", [P, ND, NS], c=c)
            loads = sem("setup_loads", c)
            made = sem("setup_made", c)
            chain = sem("setup_chain", c)
            powered = sem("setup_powered", c)
            product = sem("setup_product", c)
            block = c.enter_context(nc.Block())

            @block.sync
            def _(sp):
                sp.dma_start(means_sb[:, :], means).then_inc(loads, 16)
                sp.dma_start(means_ts[:, :, :], means_t.rearrange("(c p) k -> p c k", p=P)).then_inc(loads, 16)
                sp.dma_start(prompt_ts[:, :, :], prompt_t.rearrange("(c p) n -> p c n", p=P)).then_inc(loads, 16)

            @block.gpsimd
            def _(pool):
                pool.memset(ident[:, :], 0.0).then_inc(made, 1)
                pool.memset(ones[:, :], 1.0).then_inc(made, 1)
                pool.memset(half[:, :], 0.5).then_inc(made, 1)
                pool.memset(neg_half[:, :], -0.5).then_inc(made, 1)
                pool.memset(mhalf[:, :], 0.5).then_inc(made, 1)
                pool.memset(positions[:, :], 0).then_inc(made, 1)
                pool.memset(zero_bias[:, :], 0.0).then_inc(made, 1)
                pool.memset(one_bias[:, :], 1.0).then_inc(made, 1)
                pool.wait_ge(made, 8)
                pool.affine_select(out=ident[:, :], in_=ident[:, :], compare_op=ALU.not_equal, fill=1.0,
                                   base=0, pattern=[[-1, P]], channel_multiplier=1).then_inc(made, 1)
                pool.wait_ge(chain, 2)
                pool.tensor_tensor(mnorm[:, 1:2], mnorm[:, 0:1], mhalf[:, :], ALU.pow).then_inc(powered, 1)

            @block.vector
            def _(dve):
                dve.wait_ge(loads, 48)
                dve.tensor_tensor(means_sq[:, :], means_sb[:, :], means_sb[:, :], ALU.mult).then_inc(chain, 1)
                dve.wait_ge(chain, 1)
                dve.tensor_reduce(mnorm[:, 0:1], means_sq[:, :], AX, ALU.add).then_inc(chain, 1)
                dve.wait_ge(powered, 1)
                dve.tensor_scalar(mnorm[:, 2:3], mnorm[:, 1:2], NORM_EPS, None, ALU.max).then_inc(chain, 1)
                dve.wait_ge(chain, 3)
                dve.reciprocal(mnorm[:, 3:4], mnorm[:, 2:3]).then_inc(chain, 1)
                dve.wait_ge(chain, 4)
                dve.tensor_scalar(means_sq[:, :], means_sb[:, :], mnorm[:, 3:4], None, ALU.mult).then_inc(chain, 1)
                dve.wait_ge(product, 1)
                dve.tensor_copy(mean_dirs[:, :, :].rearrange("p c k -> p (c k)"), bank[0][:, 0:ND * K]).then_inc(chain, 1)
                dve.wait_ge(product, 2)
                dve.tensor_copy(cluster_c[:, :], bank[1][0:K, 0:NS]).then_inc(chain, 1)

            @block.tensor
            def _(pe):
                pe.wait_ge(made, 9)
                pe.wait_ge(chain, 5)
                for c_ in range(ND):
                    last = pe.transpose(bank[0][:, c_ * K:(c_ + 1) * K], means_sq[:, c_ * P:(c_ + 1) * P],
                                        ident[0:K, 0:K])
                last.then_inc(product, 1)
                for c_ in range(ND):
                    last = pe.matmul(bank[1][0:K, 0:NS], means_ts[:, c_, :], prompt_ts[:, c_, :],
                                     start=(c_ == 0), stop=(c_ == ND - 1))
                last.then_inc(product, 1)

        with ExitStack() as c:
            xa = [sb(f"xa{n}", [P, NT, D], c=c) for n in range(2)]
            xt = [sb(f"xt{n}", [P, ND, P], c=c) for n in range(2)]
            stats = sb("stats", [P, NT, 6], c=c)
            moments = sb("moments", [P, NT, 2], c=c)
            var_eps = sb("var_eps", [P, NT], c=c)
            rstd = sb("rstd", [P, NT], c=c)
            std = sb("std", [P, NT], c=c)
            norm = sb("norm", [P, NT], c=c)
            rnorm = sb("rnorm", [P, NT], c=c)
            cosines = sb("cosines", [P, NT, K], c=c)
            best = sb("best", [P, NT], c=c)
            is_best = sb("is_best", [P, NT, K], c=c)
            candidate = sb("candidate", [P, NT, K], c=c)
            cluster = sb("cluster", [P, NT], c=c)
            cluster_ids = sb("cluster_ids", [P, NT, K], c=c)
            cluster_ids_m = sb("cluster_ids_m", [P, NT, K], c=c)
            ids_i = sb("ids_i", [P, NT, K], I32, c=c)
            onehot = sb("onehot", [P, K, NT], BF16, c=c)
            below = sb("below", [P, NT, K], BF16, c=c)
            upto = sb("upto", [P, NT, K], BF16, c=c)
            earlier = sb("earlier", [P, P], BF16, c=c)
            ones_b = sb("ones_b", [P, P], BF16, c=c)
            zeros = sb("zeros", [P, KT], c=c)
            totals = sb("totals", [P, KT], c=c)
            running = sb("running", [P, KT], c=c)
            before = sb("before", [P, KT], c=c)
            place = sb("place", [P, KT], c=c)
            chosen = sb("chosen", [P, KT], c=c)
            place_in_seq = sb("place_in_seq", [P, NT], c=c)
            first_row = sb("first_row", [P, 1], c=c)
            target = [sb(f"target{n}", [P, NT], U32, c=c) for n in range(2)]
            made = sem("sort_consts", c)
            loaded = [sem(f"sort_loaded{n}", c) for n in range(2)]
            stats_done = sem("sort_stats", c)
            moments_done = sem("sort_moments", c)
            var_done = sem("sort_var", c)
            pow_done = sem("sort_pow", c)
            normed = sem("sort_normed", c)
            turned = sem("sort_turned", c)
            turned_sb = sem("sort_turned_sb", c)
            cos_done = sem("sort_cosines", c)
            onehots = sem("sort_onehots", c)
            counted = sem("sort_counted", c)
            chain = sem("sort_chain", c)
            targets = sem("sort_targets", c)
            scattered = [sem(f"sort_scattered{n}", c) for n in range(2)]
            turn = bank[0:2]
            cos_ps = bank[2]
            count_ps = bank[3]
            block = c.enter_context(nc.Block())

            @block.sync
            def _(sp):
                for n in range(2):
                    sp.dma_start(xa[n][:, :, :], row(x_rows, n)).then_inc(loaded[n], 16)
                with sp.Fori(0, PAIRS - 1) as i:
                    for h in range(2):
                        sp.wait_ge(scattered[h], i * (16 * NT) + 16 * NT)
                        sp.dma_start(xa[h][:, :, :], row(x_rows, i * 2 + (2 + h))).then_inc(loaded[h], 16)

            @block.gpsimd
            def _(pool):
                pool.memset(earlier[:, :], 1.0).then_inc(made, 1)
                pool.memset(ones_b[:, :], 1.0).then_inc(made, 1)
                pool.memset(zeros[:, :], 0.0).then_inc(made, 1)
                pool.memset(first_row[:, :], 0.0).then_inc(made, 1)
                pool.iota(ids_i[:, :, :], pattern=[[0, NT], [1, K]], base=0, channel_multiplier=0).then_inc(made, 1)
                pool.wait_ge(made, 5)
                pool.affine_select(out=earlier[:, :], in_=earlier[:, :], compare_op=ALU.is_gt, fill=0.0,
                                   base=0, pattern=[[1, P]], channel_multiplier=-1).then_inc(made, 1)
                pool.tensor_copy(cluster_ids[:, :, :], ids_i[:, :, :]).then_inc(made, 1)
                pool.wait_ge(made, 7)
                pool.tensor_scalar(cluster_ids_m[:, :, :], cluster_ids[:, :, :], -float(K), None,
                                   ALU.add).then_inc(made, 1)
                with pool.Fori(0, PAIRS) as i:
                    for h in range(2):
                        pool.wait_ge(var_done, at(i, h, 1, 1))
                        pool.tensor_tensor(rstd[:, :], var_eps[:, :], neg_half[:, :], ALU.pow).then_inc(pow_done, 1)
                        pool.tensor_tensor(std[:, :], moments[:, :, 1], half[:, :], ALU.pow).then_inc(pow_done, 1)
                        gate(pool, targets, at(i, h, 1, 1))
                        for t in range(NT):
                            pool.indirect_dma_start(xs_dram, bass.IndirectOffsetOnAxis(target[h][:, t:t + 1], 0),
                                                    xa[h][:, t, :], None).then_inc(scattered[h], 16)
                for n in range(2):
                    pool.wait_ge(scattered[n], 16 * NT * PAIRS)

            @block.scalar
            def _(act):
                act.sem_inc(turned_sb, 2)
                with act.Fori(0, PAIRS) as i:
                    for h in range(2):
                        for t in range(NT):
                            act.wait_ge(turned, at(i, h, NT, t + 1))
                            act.wait_ge(cos_done, at(i, h, NT, t + 1))
                            act.activation(xt[t % 2][:, :, :].rearrange("p c q -> p (c q)"), turn[t % 2][:, :],
                                           ACT.Copy).then_inc(turned_sb, 1)

            @block.tensor
            def _(pe):
                pe.wait_ge(made, 8)
                pe.sem_inc(cos_done, 2)

                def turn_tile(i, h, t):
                    pe.wait_ge(normed, at(i, h, NT, t + 1))
                    pe.wait_ge(turned_sb, at(i, h, NT, t + 1))
                    for c_ in range(ND):
                        last = pe.transpose(turn[t % 2][:, c_ * P:(c_ + 1) * P], xa[h][:, t, c_ * P:(c_ + 1) * P],
                                            ident[:, :])
                    last.then_inc(turned, 1)

                def cos_tile(i, h, t):
                    pe.wait_ge(turned_sb, at(i, h, NT, t + 3))
                    for c_ in range(ND):
                        last = pe.matmul(cos_ps[:, t * K:(t + 1) * K], xt[t % 2][:, c_, :], mean_dirs[:, c_, :],
                                         start=(c_ == 0), stop=(c_ == ND - 1))
                    last.then_inc(cos_done, 1)

                with pe.Fori(0, PAIRS) as i:
                    for h in range(2):
                        for t in range(NT):
                            turn_tile(i, h, t)
                            if t:
                                cos_tile(i, h, t - 1)
                        cos_tile(i, h, NT - 1)
                        pe.wait_ge(onehots, at(i, h, 3, 3))
                        flat = onehot[:, :, :].rearrange("p k t -> p (k t)")
                        pe.matmul(count_ps[:, 0:KT], earlier[:, :], flat, start=True, stop=True)
                        pe.matmul(count_ps[:, KT:2 * KT], ones_b[:, :], flat, start=True, stop=True)
                        for e, mask in enumerate((below, upto)):
                            for t in range(NT):
                                last = pe.matmul(count_ps[0:K, 2 * KT + e:2 * KT + e + 1], mask[:, t, :],
                                                 ones_b[:, 0:1], start=(t == 0), stop=(t == NT - 1))
                        last.then_inc(counted, 1)

            @block.vector
            def _(dve):
                LINKS = 15
                dve.wait_ge(made, 8)
                with dve.Fori(0, PAIRS) as i:
                    for h in range(2):
                        links = [0]

                        def link(ins):
                            links[0] += 1
                            ins.then_inc(chain, 1)
                            dve.wait_ge(chain, at(i, h, LINKS, links[0]))

                        dve.wait_ge(loaded[h], i * 16 + 16)
                        for t in range(NT):
                            dve.bn_stats(stats[:, t, :], xa[h][:, t, :]).then_inc(stats_done, 1)
                        gate(dve, stats_done, at(i, h, NT, NT))
                        for t in range(NT):
                            dve.bn_aggr(moments[:, t, :], stats[:, t, :]).then_inc(moments_done, 1)
                        dve.wait_ge(moments_done, at(i, h, NT, NT))
                        dve.tensor_scalar(var_eps[:, :], moments[:, :, 1], LN_EPS, None, ALU.add).then_inc(var_done, 1)
                        dve.wait_ge(pow_done, at(i, h, 2, 2))
                        for t in range(NT):
                            dve.tensor_scalar(xa[h][:, t, :], xa[h][:, t, :], moments[:, t, 0:1], rstd[:, t:t + 1],
                                              ALU.subtract, ALU.mult).then_inc(normed, 1)
                        link(dve.scalar_tensor_tensor(out=norm[:, :], in0=std[:, :], scalar=SQRT_D, in1=rstd[:, :],
                                                      op0=ALU.mult, op1=ALU.mult))
                        link(dve.tensor_scalar(norm[:, :], norm[:, :], NORM_EPS, None, ALU.max))
                        link(dve.reciprocal(rnorm[:, :], norm[:, :]))
                        dve.wait_ge(cos_done, at(i, h, NT, NT + 2))
                        wide = [P, NT, K]
                        link(dve.tensor_tensor(cosines[:, :, :], cos_ps[:, 0:KT].rearrange("p (t k) -> p t k", k=K),
                                               rnorm[:, :].unsqueeze(2).to_broadcast(wide), ALU.mult))
                        link(dve.tensor_reduce(best[:, :], cosines[:, :, :], AX, ALU.max))
                        link(dve.tensor_tensor(is_best[:, :, :], cosines[:, :, :],
                                               best[:, :].unsqueeze(2).to_broadcast(wide), ALU.is_equal))
                        link(dve.scalar_tensor_tensor(out=candidate[:, :, :], in0=is_best[:, :, :], scalar=-float(K),
                                                      in1=cluster_ids[:, :, :], op0=ALU.mult, op1=ALU.add))
                        link(dve.tensor_reduce(cluster[:, :], candidate[:, :, :], AX, ALU.min))
                        mine = cluster[:, :].unsqueeze(2).to_broadcast(wide)
                        dve.tensor_tensor(onehot[:, :, :].rearrange("p k t -> p t k"), cluster_ids_m[:, :, :], mine,
                                          ALU.is_equal).then_inc(onehots, 1)
                        dve.tensor_tensor(below[:, :, :], cluster_ids_m[:, :, :], mine, ALU.is_gt).then_inc(onehots, 1)
                        dve.tensor_tensor(upto[:, :, :], cluster_ids_m[:, :, :], mine, ALU.is_ge).then_inc(onehots, 1)
                        dve.wait_ge(counted, at(i, h, 1, 1))
                        link(dve.tensor_copy(totals[:, :], count_ps[:, KT:2 * KT]))
                        link(dve.tensor_tensor_scan(running[:, :], totals[:, :], zeros[:, :], 0.0, ALU.add, ALU.add))
                        link(dve.tensor_tensor(before[:, :], running[:, :], totals[:, :], ALU.subtract))
                        link(dve.tensor_tensor(place[:, :], before[:, :], count_ps[:, 0:KT], ALU.add))
                        link(dve.tensor_tensor(chosen[:, :], place[:, :],
                                               onehot[:, :, :].rearrange("p k t -> p (k t)"), ALU.mult))
                        link(dve.tensor_reduce(place_in_seq[:, :], chosen[:, :].rearrange("p (k t) -> p t k", t=NT),
                                               AX, ALU.add))
                        col = (i * 2 + h) * NT
                        dve.tensor_scalar(positions[:, bass.ds(col, NT)], place_in_seq[:, :], first_row[:, :], None,
                                          ALU.add)
                        dve.tensor_scalar(bounds[:, bass.ds((i * 2 + h) * 2, 2)], count_ps[0:K, 2 * KT:2 * KT + 2],
                                          0.0, None, ALU.add)
                        dve.tensor_scalar(target[h][:, :], place_in_seq[:, :], first_row[:, :], None,
                                          ALU.add).then_inc(targets, 1)
                        dve.wait_ge(targets, at(i, h, 1, 1))
                        link(dve.tensor_scalar(first_row[:, :], first_row[:, :], float(L), None, ALU.add))
                        assert links[0] == LINKS, links[0]


        with ExitStack() as c:
            ITEMS = NS * ND
            acc = [sb(f"acc{n}", [P, NT, D], c=c) for n in range(2)]
            feat = [sb(f"feat{n}", [P, ND, L], c=c) for n in range(2)]
            delta = [sb(f"delta{n}", [P, ND, L], c=c) for n in range(2)]
            decay = [sb(f"decay{n}", [P, L], c=c) for n in range(4)]
            drive = [sb(f"drive{n}", [P, L], c=c) for n in range(4)]
            states = [sb(f"states{n}", [P, L], c=c) for n in range(2 * ND)]
            b_rows = [sb(f"b_rows{n}", [P, L], c=c) for n in range(2)]
            proj = sb("proj", [P, L], c=c)
            b_parts = sb("b_parts", [P, L], BF16, c=c)
            c_cols = [sb(f"c_cols{n}", [P, NT, NS], c=c) for n in range(2)]
            in_cluster = sb("in_cluster", [K, L], c=c)
            places = sb("places", [K, L], c=c)
            bound = sb("bound", [K, 2], c=c)
            wx = sb("wx", [P, ND, P], c=c)
            wc = sb("wc", [P, ND, NS], c=c)
            wdt = sb("wdt", [P, D], c=c)
            bias = sb("bias", [P, ND], c=c)
            a_neg = sb("a_neg", [P, ND, NS], c=c)
            d_row = sb("d_row", [P, D], c=c)
            select = sb("select", [P, NS, P], BF16, c=c)
            absz = [sb(f"absz{n}", [P, 512], c=c) for n in range(2)]
            soft = [sb(f"soft{n}", [P, 512], c=c) for n in range(2)]
            stats = sb("y_stats", [P, NT, 6], c=c)
            moments = sb("y_moments", [P, NT, 2], c=c)
            var_eps = sb("y_var_eps", [P, NT], c=c)
            rstd = sb("y_rstd", [P, NT], c=c)

            wloads = sem("scan_weights", c)
            made = sem("scan_consts", c)
            a_made = sem("scan_a", c)
            loaded = [sem(f"scan_loaded{n}", c) for n in range(2)]
            stored = [sem(f"scan_stored{n}", c) for n in range(2)]
            turned = sem("scan_turned", c)
            turned_out = sem("scan_turned_out", c)
            projected = sem("scan_projected", c)
            projected_out = sem("scan_projected_out", c)
            in_cluster_done = sem("scan_in_cluster", c)
            split = sem("scan_split", c)
            softs = sem("scan_softs", c)
            soft_steps = sem("scan_soft_steps", c)
            deltas = sem("scan_deltas", c)
            driven = sem("scan_feat_times_delta", c)
            skip_done = sem("scan_skip", c)
            b_spread = sem("scan_b_spread", c)
            b_ready = sem("scan_b_ready", c)
            decays = sem("scan_decays", c)
            drives = sem("scan_drives", c)
            scans = sem("scan_scans", c)
            states_turned = sem("scan_states_turned", c)
            added = sem("scan_added", c)
            stats_done = sem("scan_stats", c)
            moments_done = sem("scan_moments", c)
            var_done = sem("scan_var", c)
            pow_done = sem("scan_pow", c)
            normed = sem("scan_normed", c)
            chain = sem("scan_chain", c)
            turn = bank[0:2]
            b_ps = bank[2:4]
            state_ps = bank[4:6]
            proj_ps = bank[6]
            TURNS = NT + 2 * ND
            block = c.enter_context(nc.Block())

            @block.sync
            def _(sp):
                for dst, src in (
                    (wx[:, :, :], w_x.rearrange("(c p) m -> p c m", p=P)),
                    (wc[:, :, :], w_c.rearrange("(c p) m -> p c m", p=P)),
                    (wdt[DT_ROW:DT_ROW + R, :], w_dt_t),
                    (bias[:, :], dt_bias.rearrange("(c p) -> p c", p=P)),
                    (a_neg[:, :, :], a_logs.rearrange("(c p) n -> p c n", p=P)),
                    (d_row[:, :], ds.partition_broadcast(P)),
                ):
                    sp.dma_start(dst, src, allow_slow_non_contiguous=True).then_inc(wloads, 16)
                for n in range(2):
                    sp.dma_start(acc[n][:, :, :], row(xs_rows, n)).then_inc(loaded[n], 16)
                with sp.Fori(0, PAIRS - 1) as i:
                    for h in range(2):
                        sp.wait_ge(normed, at(i, h, NT, NT))
                        sp.dma_start(row(ys_rows, i * 2 + h), acc[h][:, :, :]).then_inc(stored[h], 16)
                        sp.wait_ge(stored[h], i * 16 + 16)
                        sp.dma_start(acc[h][:, :, :], row(xs_rows, i * 2 + (2 + h))).then_inc(loaded[h], 16)
                for h in range(2):
                    sp.wait_ge(normed, NT * (B - 1 + h))
                    sp.dma_start(row(ys_rows, B - 2 + h), acc[h][:, :, :]).then_inc(stored[h], 16)
                    sp.wait_ge(stored[h], 16 * PAIRS)

            @block.gpsimd
            def _(pool):
                pool.memset(select[:, :, :], 0.0).then_inc(made, 1)
                pool.memset(b_parts[:, :], 0.0).then_inc(made, 1)
                pool.iota(states[0][0:K, :].bitcast(I32), pattern=[[1, L]], base=0, channel_multiplier=0).then_inc(made, 1)
                pool.wait_ge(made, 3)
                pool.tensor_copy(places[:, :], states[0][0:K, :].bitcast(I32)).then_inc(made, 1)
                for part in range(3):
                    pool.affine_select(out=select[:, :, :], in_=select[:, :, :], compare_op=ALU.not_equal, fill=1.0,
                                       base=-32 * part, pattern=[[-1, NS], [0, P]],
                                       channel_multiplier=1).then_inc(made, 1)
                    pool.wait_ge(made, 5 + part)
                pool.sem_inc(drives, 2 * ND)
                with pool.Fori(0, PAIRS) as i:
                    for h in range(2):
                        for n in range(NS):
                            pool.wait_ge(b_ready, at(i, h, NS, n + 2))
                            for c_ in range(ND):
                                g = n * ND + c_
                                if n == 0:
                                    pool.wait_ge(driven, at(i, h, ND, c_ + 1))
                                pool.wait_ge(scans, at(i, h, ITEMS, g + 1))
                                pool.tensor_tensor(drive[g % 4][:, :], feat[h][:, c_, :], b_rows[n % 2][:, :],
                                                   ALU.mult).then_inc(drives, 1)
                        pool.wait_ge(var_done, at(i, h, 1, 1))
                        pool.tensor_tensor(rstd[:, :], var_eps[:, :], neg_half[:, :], ALU.pow).then_inc(pow_done, 1)

            @block.scalar
            def _(act):
                act.preload_act_table_set("natural_log_exp_and_others")
                act.wait_ge(wloads, 96)
                flat_a = a_neg[:, :, :].rearrange("p c n -> p (c n)")
                act.activation(flat_a, flat_a, ACT.Exp).then_inc(a_made, 1)
                act.wait_ge(a_made, 1)
                act.activation(flat_a, flat_a, ACT.Copy, scale=-1.0).then_inc(a_made, 1)
                act.wait_ge(a_made, 2)
                act.sem_inc(turned_out, 2)
                act.sem_inc(projected_out, 1)
                act.sem_inc(b_ready, 1)

                def spread(i, h, n):
                    act.wait_ge(b_spread, at(i, h, NS, n + 1))
                    act.wait_ge(drives, at(i, h, ITEMS, ND * (n + 1)))
                    for m in range(2):
                        last = act.activation(b_rows[n % 2][:, m * 512:(m + 1) * 512], b_ps[m][:, :], ACT.Copy)
                    last.then_inc(b_ready, 1)

                with act.Fori(0, PAIRS) as i:
                    for h in range(2):
                        act.wait_ge(drives, at(i, h, ITEMS, 2 * ND))
                        for t in range(NT):
                            act.wait_ge(turned, at(i, h, TURNS, t + 1))
                            act.activation(feat[h][:, :, t * P:(t + 1) * P],
                                           turn[t % 2][:, :].rearrange("p (c q) -> p c q", c=ND),
                                           ACT.Copy).then_inc(turned_out, 1)
                        for m in range(2):
                            act.wait_ge(projected, at(i, h, 3, m + 1))
                            act.activation(proj[:, m * 512:(m + 1) * 512], proj_ps[:, :], ACT.Copy)\
                               .then_inc(projected_out, 1)
                        act.wait_ge(projected, at(i, h, 3, 3))
                        act.activation(c_cols[h][:, :, :].rearrange("p t n -> p (t n)"), proj_ps[:, 0:NT * NS],
                                       ACT.Copy).then_inc(projected_out, 1)
                        for g in range(2 * ND):
                            c_, m = g // 2, g % 2
                            k = 3 * g
                            act.wait_ge(turned, at(i, h, TURNS, NT + g + 1))
                            act.activation(absz[g % 2][:, :], turn[g % 2][:, :], ACT.Abs,
                                           bias=bias[:, c_:c_ + 1]).then_inc(soft_steps, 1)
                            act.activation(delta[h][:, c_, m * 512:(m + 1) * 512], turn[g % 2][:, :], ACT.Relu,
                                           bias=bias[:, c_:c_ + 1]).then_inc(turned_out, 1)
                            act.wait_ge(soft_steps, at(i, h, 4 * ND, 2 * g + 1))
                            act.activation(absz[g % 2][:, :], absz[g % 2][:, :], ACT.Exp,
                                           scale=-1.0).then_inc(soft_steps, 1)
                            act.wait_ge(soft_steps, at(i, h, 4 * ND, 2 * g + 2))
                            act.wait_ge(deltas, at(i, h, 2 * ND, g + 1))
                            act.activation(soft[g % 2][:, :], absz[g % 2][:, :], ACT.Ln, bias=one_bias[:, :])\
                               .then_inc(softs, 1)
                        spread(i, h, 0)
                        for n in range(NS):
                            if n + 1 < NS:
                                spread(i, h, n + 1)
                            for c_ in range(ND):
                                g = n * ND + c_
                                if n == 0:
                                    act.wait_ge(deltas, at(i, h, 2 * ND, 2 * c_ + 2 + 2))
                                act.wait_ge(scans, at(i, h, ITEMS, g + 1))
                                act.activation(decay[g % 4][:, :], delta[h][:, c_, :], ACT.Exp,
                                               scale=a_neg[:, c_, n:n + 1]).then_inc(decays, 1)

            @block.tensor
            def _(pe):
                pe.wait_ge(made, 7)
                pe.wait_ge(wloads, 96)
                pe.sem_inc(states_turned, 2 * NT)

                def spread(i, h, n):
                    pe.wait_ge(b_ready, at(i, h, NS, n + 1))
                    for m in range(2):
                        last = pe.matmul(b_ps[m][:, :], select[:, n, :], b_parts[:, m * 512:(m + 1) * 512],
                                         start=True, stop=True)
                    last.then_inc(b_spread, 1)

                with pe.Fori(0, PAIRS) as i:
                    for h in range(2):
                        pe.wait_ge(loaded[h], i * 16 + 16)
                        for t in range(NT):
                            pe.wait_ge(turned_out, at(i, h, TURNS, t + 1))
                            for c_ in range(ND):
                                last = pe.transpose(turn[t % 2][:, c_ * P:(c_ + 1) * P],
                                                    acc[h][:, t, c_ * P:(c_ + 1) * P], ident[:, :])
                            last.then_inc(turned, 1)
                        pe.wait_ge(turned_out, at(i, h, TURNS, NT + 2))
                        for m in range(2):
                            pe.wait_ge(projected_out, at(i, h, 3, m + 1))
                            for c_ in range(ND):
                                last = pe.matmul(proj_ps[:, :], wx[:, c_, :], feat[h][:, c_, m * 512:(m + 1) * 512],
                                                 start=(c_ == 0), stop=(c_ == ND - 1))
                            last.then_inc(projected, 1)
                        pe.wait_ge(projected_out, at(i, h, 3, 3))
                        pe.wait_ge(in_cluster_done, at(i, h, 1, 1))
                        for t in range(NT):
                            for c_ in range(ND):
                                pe.matmul(proj_ps[:, t * NS:(t + 1) * NS], feat[h][:, c_, t * P:(t + 1) * P],
                                          wc[:, c_, :], start=(c_ == 0), stop=False)
                            last = pe.matmul(proj_ps[:, t * NS:(t + 1) * NS], in_cluster[:, t * P:(t + 1) * P],
                                             cluster_c[:, :], start=False, stop=True)
                        last.then_inc(projected, 1)
                        for g in range(2 * ND):
                            c_, m = g // 2, g % 2
                            pe.wait_ge(turned_out, at(i, h, TURNS, NT + g + 1))
                            pe.matmul(turn[g % 2][:, :], wdt[DT_ROW:DT_ROW + R, c_ * P:(c_ + 1) * P],
                                      proj[DT_ROW:DT_ROW + R, m * 512:(m + 1) * 512],
                                      start=True, stop=True).then_inc(turned, 1)
                        pe.wait_ge(split, at(i, h, 5, 5))
                        spread(i, h, 0)
                        spread(i, h, 1)
                        for n in range(NS):
                            if n + 2 < NS:
                                spread(i, h, n + 2)
                            pe.wait_ge(scans, at(i, h, ITEMS, ND * (n + 1) + 4))
                            for t in range(NT):
                                pe.wait_ge(added, at(i, h, NS * NT, n * NT + t + 1))
                                for c_ in range(ND):
                                    last = pe.transpose(state_ps[t % 2][:, c_ * P:(c_ + 1) * P],
                                                        states[(n % 2) * ND + c_][:, t * P:(t + 1) * P], ident[:, :])
                                last.then_inc(states_turned, 1)

            @block.vector
            def _(dve):
                LINKS = 3
                dve.wait_ge(made, 7)
                dve.wait_ge(wloads, 96)
                dve.sem_inc(deltas, 2)
                dve.sem_inc(scans, 4)
                dve.sem_inc(added, 2)

                def scan(i, h, n):
                    for c_ in range(ND):
                        g = n * ND + c_
                        if c_ == 0:
                            dve.wait_ge(states_turned, at(i, h, NS * NT, (n + 1) * NT))
                        dve.wait_ge(decays, at(i, h, ITEMS, g + 1))
                        dve.wait_ge(drives, at(i, h, ITEMS, g + 1) + 2 * ND)
                        dve.tensor_tensor_scan(states[(n % 2) * ND + c_][:, :], decay[g % 4][:, :],
                                               drive[g % 4][:, :], 0.0, ALU.mult, ALU.add).then_inc(scans, 1)

                def add(i, h, n):
                    dve.wait_ge(added, at(i, h, NS * NT, n * NT) + 2) if n else None
                    for t in range(NT):
                        dve.wait_ge(states_turned, at(i, h, NS * NT, n * NT + t + 1) + 2 * NT)
                        dve.scalar_tensor_tensor(out=acc[h][:, t, :], in0=state_ps[t % 2][:, :],
                                                 scalar=c_cols[h][:, t, n:n + 1], in1=acc[h][:, t, :],
                                                 op0=ALU.mult, op1=ALU.add).then_inc(added, 1)

                with dve.Fori(0, PAIRS) as i:
                    for h in range(2):
                        links = [0]

                        def link(ins):
                            links[0] += 1
                            ins.then_inc(chain, 1)
                            dve.wait_ge(chain, at(i, h, LINKS, links[0]))

                        link(dve.tensor_scalar(bound[:, :], bounds[:, bass.ds((i * 2 + h) * 2, 2)], 0.0, None, ALU.add))
                        link(dve.tensor_scalar(in_cluster[:, :], places[:, :], bound[:, 0:1], None, ALU.is_ge))
                        dve.scalar_tensor_tensor(out=in_cluster[:, :], in0=places[:, :], scalar=bound[:, 1:2],
                                                 in1=in_cluster[:, :], op0=ALU.is_lt, op1=ALU.mult)\
                           .then_inc(in_cluster_done, 1)
                        dve.wait_ge(projected_out, at(i, h, 3, 3))
                        dve.tensor_copy(b_parts[0:96, :], proj[0:96, :]).then_inc(split, 1)
                        dve.wait_ge(split, at(i, h, 5, 1))
                        dve.tensor_tensor(proj[0:64, :], proj[0:64, :], b_parts[0:64, :], ALU.subtract).then_inc(split, 1)
                        dve.wait_ge(split, at(i, h, 5, 2))
                        dve.tensor_copy(b_parts[0:64, :], proj[0:64, :]).then_inc(split, 1)
                        dve.wait_ge(split, at(i, h, 5, 3))
                        dve.tensor_tensor(proj[0:32, :], proj[0:32, :], b_parts[0:32, :], ALU.subtract).then_inc(split, 1)
                        dve.wait_ge(split, at(i, h, 5, 4))
                        dve.tensor_copy(b_parts[0:32, :], proj[0:32, :]).then_inc(split, 1)
                        for g in range(2 * ND):
                            c_, m = g // 2, g % 2
                            dve.wait_ge(softs, at(i, h, 2 * ND, g + 1))
                            piece = delta[h][:, c_, m * 512:(m + 1) * 512]
                            dve.tensor_tensor(piece, piece, soft[g % 2][:, :], ALU.add).then_inc(deltas, 1)
                            if m:
                                dve.wait_ge(deltas, at(i, h, 2 * ND, g + 1) + 2)
                                if g == 1:
                                    dve.wait_ge(projected, at(i, h, 3, 3))
                                dve.tensor_tensor(feat[h][:, c_, :], feat[h][:, c_, :], delta[h][:, c_, :],
                                                  ALU.mult).then_inc(driven, 1)
                        dve.wait_ge(turned, at(i, h, TURNS, NT))
                        link(dve.tensor_tensor(acc[h][:, :, :], acc[h][:, :, :],
                                               d_row[:, :].unsqueeze(1).to_broadcast([P, NT, D]), ALU.mult))
                        scan(i, h, 0)
                        for n in range(1, NS):
                            scan(i, h, n)
                            add(i, h, n - 1)
                        add(i, h, NS - 1)
                        dve.wait_ge(added, at(i, h, NS * NT, NS * NT) + 2)
                        for t in range(NT):
                            dve.bn_stats(stats[:, t, :], acc[h][:, t, :]).then_inc(stats_done, 1)
                        gate(dve, stats_done, at(i, h, NT, NT))
                        for t in range(NT):
                            dve.bn_aggr(moments[:, t, :], stats[:, t, :]).then_inc(moments_done, 1)
                        dve.wait_ge(moments_done, at(i, h, NT, NT))
                        dve.tensor_scalar(var_eps[:, :], moments[:, :, 1], LN_EPS, None, ALU.add).then_inc(var_done, 1)
                        dve.wait_ge(pow_done, at(i, h, 1, 1))
                        for t in range(NT):
                            dve.tensor_scalar(acc[h][:, t, :], acc[h][:, t, :], moments[:, t, 0:1], rstd[:, t:t + 1],
                                              ALU.subtract, ALU.mult).then_inc(normed, 1)
                        assert links[0] == LINKS, links[0]

        with ExitStack() as c:
            xr = [sb(f"xr{n}", [P, NT, D], c=c) for n in range(2)]
            both = [sb(f"both{n}", [P, NT, 2 * D], c=c) for n in range(2)]
            normed_x = sb("normed_x", [P, NT, D], c=c)
            xt = [sb(f"xt_l{n}", [P, ND, 512], c=c) for n in range(2)]
            hidden = [sb(f"hidden{n}", [P, FL, 512], c=c) for n in range(2)]
            w1 = sb("l_w1_sb", [P, ND, FL * P], c=c)
            w2 = sb("l_w2_sb", [P, FL, D], c=c)
            gamma = sb("l_gamma_sb", [P, ND], c=c)
            b1 = sb("l_b1_sb", [P, FL], c=c)
            b2 = sb("l_b2_sb", [P, D], c=c)
            route = sb("route_sb", [P, ND], c=c)
            stats = sb("x1_stats", [P, NT, 6], c=c)
            moments = sb("x1_moments", [P, NT, 2], c=c)
            var_eps = sb("x1_var_eps", [P, NT], c=c)
            rstd = sb("x1_rstd", [P, NT], c=c)
            std = sb("x1_std", [P, NT], c=c)
            norm = sb("x1_norm", [P, NT], c=c)
            rnorm = sb("x1_rnorm", [P, NT], c=c)
            scale = sb("x1_scale", [P, NT], c=c)
            o_stats = sb("lo_stats", [P, NT, 6], c=c)
            o_moments = sb("lo_moments", [P, NT, 2], c=c)
            o_var_eps = sb("lo_var_eps", [P, NT], c=c)
            o_rstd = sb("lo_rstd", [P, NT], c=c)
            index = [sb(f"index{n}", [P, NT], U32, c=c) for n in range(2)]

            wloads = sem("light_weights", c)
            folded = sem("light_gamma_folded", c)
            loaded = [sem(f"light_loaded{n}", c) for n in range(2)]
            gathered = [sem(f"light_gathered{n}", c) for n in range(2)]
            kept = [sem(f"light_kept{n}", c) for n in range(2)]
            written = [sem(f"light_written{n}", c) for n in range(2)]
            indexed = sem("light_indexed", c)
            summed = sem("light_summed", c)
            stats_done = sem("light_stats", c)
            moments_done = sem("light_moments", c)
            var_done = sem("light_var", c)
            pow_done = sem("light_pow", c)
            scaled = sem("light_scaled", c)
            normed = sem("light_normed", c)
            turned = sem("light_turned", c)
            turned_sb = sem("light_turned_sb", c)
            hidden_ps = sem("light_hidden_ps", c)
            hidden_sb = sem("light_hidden_sb", c)
            scored = sem("light_scored", c)
            light_ps = sem("light_out_ps", c)
            light_sb = sem("light_out_sb", c)
            light_n = sem("light_out_normed", c)
            out_ready = sem("light_out_ready", c)
            chain = sem("light_chain", c)
            turn = bank[0:2]
            hid = bank[2:4]
            lout = bank[4:6]
            score_ps = bank[6]
            G = NT // 4
            block = c.enter_context(nc.Block())

            @block.sync
            def _(sp):
                for dst, src in (
                    (w1[:, :, :], l_w1.rearrange("(c p) f -> p c f", p=P)),
                    (w2[:, :, :], l_w2.rearrange("(c p) f -> p c f", p=P)),
                    (gamma[:, :], l_gamma.rearrange("(c p) -> p c", p=P)),
                    (b1[:, :], l_b1.rearrange("(c p) -> p c", p=P)),
                    (b2[:, :], l_b2.partition_broadcast(P)),
                    (route[:, :], routing.rearrange("(c p) -> p c", p=P)),
                ):
                    sp.dma_start(dst, src, allow_slow_non_contiguous=True).then_inc(wloads, 16)
                for n in range(2):
                    sp.dma_start(xr[n][:, :, :], row(x_rows, n)).then_inc(loaded[n], 16)

                def store(i, h, seq):
                    sp.wait_ge(light_sb, at(i, h, NT, NT) + 2)
                    sp.dma_start(row(xl_rows, seq), both[h][:, :, :]).then_inc(kept[h], 16)
                    sp.wait_ge(out_ready, at(i, h, NT, NT))
                    sp.dma_start(row(out_rows, seq), xr[h][:, :, :]).then_inc(written[h], 16)

                with sp.Fori(0, PAIRS - 1) as i:
                    for h in range(2):
                        store(i, h, i * 2 + h)
                        sp.wait_ge(written[h], i * 16 + 16)
                        sp.dma_start(xr[h][:, :, :], row(x_rows, i * 2 + (2 + h))).then_inc(loaded[h], 16)
                for h in range(2):
                    store(PAIRS - 1, h, B - 2 + h)
                for h in range(2):
                    sp.wait_ge(written[h], 16 * PAIRS)
                    sp.wait_ge(kept[h], 16 * PAIRS)

            @block.gpsimd
            def _(pool):
                def gather(h):
                    for t in range(NT):
                        pool.indirect_dma_start(both[h][:, t, 0:D], None, ys_dram,
                                                bass.IndirectOffsetOnAxis(index[h][:, t:t + 1], 0))\
                            .then_inc(gathered[h], 16)

                def powers(i, h):
                    pool.wait_ge(var_done, at(i, h, 2, 1))
                    pool.tensor_tensor(rstd[:, :], var_eps[:, :], neg_half[:, :], ALU.pow).then_inc(pow_done, 1)
                    pool.tensor_tensor(std[:, :], moments[:, :, 1], half[:, :], ALU.pow).then_inc(pow_done, 1)
                    pool.wait_ge(var_done, at(i, h, 2, 2))
                    pool.tensor_tensor(o_rstd[:, :], o_var_eps[:, :], neg_half[:, :], ALU.pow).then_inc(pow_done, 1)

                for n in range(2):
                    pool.wait_ge(indexed, n + 1)
                    gather(n)
                with pool.Fori(0, PAIRS - 1) as i:
                    for h in range(2):
                        powers(i, h)
                        pool.wait_ge(indexed, at(i, h, 1, 3))
                        pool.wait_ge(out_ready, at(i, h, NT, NT))
                        gate(pool, kept[h], i * 16 + 16)
                        gather(h)
                for h in range(2):
                    powers(PAIRS - 1, h)

            @block.scalar
            def _(act):
                act.sem_inc(turned_sb, 2)
                act.sem_inc(hidden_sb, 2)
                act.wait_ge(wloads, 96)
                with act.Fori(0, PAIRS) as i:
                    for h in range(2):
                        for g in range(G):
                            for q in range(4):
                                t = 4 * g + q
                                act.wait_ge(turned, at(i, h, NT, t + 1))
                                if q == 0:
                                    act.wait_ge(scored, at(i, h, G, g + 1))
                                act.activation(xt[g % 2][:, :, q * P:(q + 1) * P],
                                               turn[t % 2][:, :].rearrange("p (c q) -> p c q", c=ND),
                                               ACT.Copy).then_inc(turned_sb, 1)
                            for f in range(FL):
                                act.wait_ge(hidden_ps, at(i, h, G * FL, g * FL + f + 1))
                                if f == 0:
                                    act.wait_ge(light_ps, at(i, h, NT, 4 * g + 4))
                                act.activation(hidden[g % 2][:, f, :], hid[f % 2][:, :], ACT.Gelu,
                                               bias=b1[:, f:f + 1]).then_inc(hidden_sb, 1)

            @block.tensor
            def _(pe):
                pe.sem_inc(scored, 2)
                pe.sem_inc(light_ps, 8)
                pe.wait_ge(folded, ND)
                with pe.Fori(0, PAIRS) as i:
                    for h in range(2):
                        for g in range(G):
                            for t in range(4 * g, 4 * g + 4):
                                pe.wait_ge(normed, at(i, h, NT, t + 1))
                                pe.wait_ge(turned_sb, at(i, h, NT, t + 1))
                                for c_ in range(ND):
                                    last = pe.transpose(turn[t % 2][:, c_ * P:(c_ + 1) * P],
                                                        normed_x[:, t, c_ * P:(c_ + 1) * P], ident[:, :])
                                last.then_inc(turned, 1)
                            pe.wait_ge(turned_sb, at(i, h, NT, 4 * g + 4) + 2)
                            for f in range(FL):
                                pe.wait_ge(hidden_sb, at(i, h, G * FL, g * FL + f + 1))
                                for c_ in range(ND):
                                    last = pe.matmul(hid[f % 2][:, :], w1[:, c_, f * P:(f + 1) * P],
                                                     xt[g % 2][:, c_, :], start=(c_ == 0), stop=(c_ == ND - 1))
                                last.then_inc(hidden_ps, 1)
                            for t in range(4 * g, 4 * g + 4):
                                q = t % 4
                                for c_ in range(ND):
                                    last = pe.matmul(score_ps[:, t:t + 1], xt[g % 2][:, c_, q * P:(q + 1) * P],
                                                     route[:, c_:c_ + 1], start=(c_ == 0), stop=(c_ == ND - 1))
                            last.then_inc(scored, 1)
                            pe.wait_ge(hidden_sb, at(i, h, G * FL, g * FL + FL) + 2)
                            for t in range(4 * g, 4 * g + 4):
                                q = t % 4
                                pe.wait_ge(light_sb, at(i, h, NT, t + 1))
                                for f in range(FL):
                                    last = pe.matmul(lout[t % 2][:, :], hidden[g % 2][:, f, q * P:(q + 1) * P],
                                                     w2[:, f, :], start=(f == 0), stop=(f == FL - 1))
                                last.then_inc(light_ps, 1)

            @block.vector
            def _(dve):
                LINKS = 3
                dve.sem_inc(light_sb, 2)
                dve.wait_ge(wloads, 96)
                for c_ in range(ND):
                    dve.tensor_scalar(w1[:, c_, :], w1[:, c_, :], gamma[:, c_:c_ + 1], None, ALU.mult)\
                       .then_inc(folded, 1)
                for n in range(2):
                    dve.tensor_scalar(index[n][:, :], positions[:, n * NT:(n + 1) * NT], 0.0, None,
                                      ALU.add).then_inc(indexed, 1)
                with dve.Fori(0, PAIRS) as i:
                    for h in range(2):
                        links = [0]

                        def link(ins):
                            links[0] += 1
                            ins.then_inc(chain, 1)
                            dve.wait_ge(chain, at(i, h, LINKS, links[0]))

                        dve.wait_ge(loaded[h], i * 16 + 16)
                        dve.wait_ge(gathered[h], i * (16 * NT) + 16 * NT)
                        for t in range(NT):
                            dve.tensor_tensor(both[h][:, t, 0:D], both[h][:, t, 0:D], xr[h][:, t, :],
                                              ALU.add).then_inc(summed, 1)
                        for t in range(NT):
                            gate(dve, summed, at(i, h, NT, t + 1))
                            dve.bn_stats(stats[:, t, :], both[h][:, t, 0:D]).then_inc(stats_done, 1)
                        gate(dve, stats_done, at(i, h, 2 * NT, NT))
                        for t in range(NT):
                            dve.bn_aggr(moments[:, t, :], stats[:, t, :]).then_inc(moments_done, 1)
                        dve.wait_ge(moments_done, at(i, h, 2 * NT, NT))
                        dve.tensor_scalar(var_eps[:, :], moments[:, :, 1], LN_EPS, None, ALU.add).then_inc(var_done, 1)
                        dve.wait_ge(pow_done, at(i, h, 3, 2))
                        link(dve.scalar_tensor_tensor(out=norm[:, :], in0=std[:, :], scalar=SQRT_D, in1=rstd[:, :],
                                                      op0=ALU.mult, op1=ALU.mult))
                        link(dve.tensor_scalar(norm[:, :], norm[:, :], NORM_EPS, 1.0 / SQRT_D, ALU.max, ALU.mult))
                        link(dve.reciprocal(rnorm[:, :], norm[:, :]))
                        dve.tensor_tensor(scale[:, :], rstd[:, :], rnorm[:, :], ALU.mult).then_inc(scaled, 1)
                        dve.wait_ge(scaled, at(i, h, 1, 1))
                        for t in range(NT):
                            dve.tensor_scalar(normed_x[:, t, :], both[h][:, t, 0:D], moments[:, t, 0:1],
                                              scale[:, t:t + 1], ALU.subtract, ALU.mult).then_inc(normed, 1)
                        for t in range(NT):
                            dve.wait_ge(light_ps, at(i, h, NT, t + 1) + 8)
                            dve.tensor_tensor(both[h][:, t, D:2 * D], lout[t % 2][:, :], b2[:, :], ALU.add)\
                               .then_inc(light_sb, 1)
                        for t in range(NT):
                            gate(dve, light_sb, at(i, h, NT, t + 1) + 2)
                            dve.bn_stats(o_stats[:, t, :], both[h][:, t, D:2 * D]).then_inc(stats_done, 1)
                        gate(dve, stats_done, at(i, h, 2 * NT, 2 * NT))
                        for t in range(NT):
                            dve.bn_aggr(o_moments[:, t, :], o_stats[:, t, :]).then_inc(moments_done, 1)
                        dve.wait_ge(moments_done, at(i, h, 2 * NT, 2 * NT))
                        dve.tensor_scalar(o_var_eps[:, :], o_moments[:, :, 1], LN_EPS, None, ALU.add)\
                           .then_inc(var_done, 1)
                        dve.wait_ge(scored, at(i, h, G, G) + 2)
                        dve.tensor_tensor(scores[:, bass.ds((i * 2 + h) * NT, NT)], score_ps[:, 0:NT], norm[:, :],
                                          ALU.mult)
                        dve.tensor_scalar(index[h][:, :], positions[:, bass.ds((i * 2 + (2 + h)) * NT, NT)], 0.0,
                                          None, ALU.add).then_inc(indexed, 1)
                        dve.wait_ge(pow_done, at(i, h, 3, 3))
                        for t in range(NT):
                            dve.tensor_scalar(xr[h][:, t, :], both[h][:, t, D:2 * D], o_moments[:, t, 0:1],
                                              o_rstd[:, t:t + 1], ALU.subtract, ALU.mult).then_inc(light_n, 1)
                        for t in range(NT):
                            dve.wait_ge(light_n, at(i, h, NT, t + 1))
                            dve.tensor_tensor(xr[h][:, t, :], xr[h][:, t, :], both[h][:, t, 0:D],
                                              ALU.add).then_inc(out_ready, 1)
                        assert links[0] == LINKS, links[0]

        listed = sb("listed", [P, (B + 2) * NJ], U32)
        weights = sb("weights", [P, B * NJ])
        with ExitStack() as c:
            same = sb("same", [P, NT * B], c=c)
            prior = sb("prior", [P, NT * B], c=c)
            s_rows = sb("s_rows", [P, P], c=c)
            clipped = sb("clipped", [P, P], c=c)
            expd = sb("expd", [P, P], c=c)
            top = sb("top", [P, 1], c=c)
            top_row = sb("top_row", [1, B, NT], c=c)
            top_seq = sb("top_seq", [1, B], c=c)
            top_all = sb("top_all", [P, 1], c=c)
            cap = sb("cap", [P, 1], c=c)
            shift = sb("shift", [P, 1], c=c)
            part = sb("part", [P, 1], c=c)
            log_sum = sb("log_sum", [P, 1], c=c)
            gap = sb("gap", [P, P], c=c)
            better = sb("better", [P, P], c=c)
            equal = sb("equal", [P, P], c=c)
            count = sb("count", [P, 2], c=c)
            bit = sb("bit", [P, 1], I32, c=c)
            trial = sb("trial", [P, 1], I32, c=c)
            keep = sb("keep", [P, 1], I32, c=c)
            limit = sb("limit", [P, 1], I32, c=c)
            zeros = sb("zeros_r", [P, P], c=c)
            run_eq = sb("run_eq", [P, P], c=c)
            room = sb("room", [P, 1], c=c)
            picked = sb("picked", [P, P], c=c)
            slot = sb("slot", [P, P], c=c)
            straight = sb("straight", [P, P], c=c)
            slot_t = sb("slot_t", [P, P], c=c)
            tagged = sb("tagged", [P, NT * B, 2], c=c)
            row_i = sb("row_i", [P, NT * B], I32, c=c)
            slots_i = sb("slots_i", [P, NUM_HEAVY], I32, c=c)
            slots = sb("slots", [P, NUM_HEAVY], c=c)
            takes = [sb(f"takes{n}", [P, NUM_HEAVY], c=c) for n in range(2 * NT)]

            made = sem("route_consts", c)
            chain = sem("route_chain", c)
            pe_done = sem("route_pe", c)
            shifted = sem("route_shifted", c)
            expds = sem("route_expds", c)
            sums = sem("route_sums", c)
            logs = sem("route_logs", c)
            caps = sem("route_caps", c)
            gaps = sem("route_gaps", c)
            score_exp = sem("route_score_exp", c)
            counts = sem("route_counts", c)
            totals = sem("route_totals", c)
            limits = sem("route_limits", c)
            bits = sem("route_bits", c)
            taken = sem("route_taken", c)
            lists = sem("route_lists", c)
            block = c.enter_context(nc.Block())

            @block.gpsimd
            def _(pool):
                pool.memset(same[:, :], 1.0).then_inc(made, 1)
                pool.memset(listed[:, B * NJ:(B + 2) * NJ], 0)
                pool.memset(zeros[:, :], 0.0).then_inc(made, 1)
                pool.memset(limit[:, :], 0).then_inc(made, 1)
                pool.memset(bit[:, :], 1 << 30).then_inc(made, 1)
                pool.memset(cap[:, :], -(LOG_K - math.log(L))).then_inc(made, 1)
                pool.iota(slots_i[:, :], pattern=[[1, NUM_HEAVY]], base=0, channel_multiplier=0).then_inc(made, 1)
                pool.iota(row_i[:, :], pattern=[[P, NT * B]], base=0, channel_multiplier=1).then_inc(made, 1)
                pool.wait_ge(made, 7)
                v = same[:, :].rearrange("p (b t) -> p b t", t=NT)
                pool.affine_select(out=v, in_=v, compare_op=ALU.is_ge, fill=0.0, base=0,
                                   pattern=[[-NT, B], [0, NT]], channel_multiplier=1).then_inc(made, 1)
                pool.wait_ge(made, 8)
                pool.affine_select(out=v, in_=v, compare_op=ALU.is_ge, fill=0.0, base=NT - 1,
                                   pattern=[[NT, B], [0, NT]], channel_multiplier=-1).then_inc(made, 1)
                pool.wait_ge(made, 9)
                pool.affine_select(out=prior[:, :], in_=same[:, :], compare_op=ALU.is_gt, fill=0.0, base=0,
                                   pattern=[[1, NT * B]], channel_multiplier=-1).then_inc(made, 1)
                pool.tensor_copy(slots[:, :], slots_i[:, :]).then_inc(made, 1)
                pool.tensor_copy(tagged[:, :, 0], row_i[:, :]).then_inc(made, 1)

            @block.scalar
            def _(act):
                act.preload_act_table_set("natural_log_exp_and_others")
                with act.Fori(0, DESCENT_STEPS - 1) as j:
                    act.wait_ge(shifted, j * 2 + 2)
                    act.activation(expd[:, :], clipped[:, :], ACT.Exp, bias=shift[:, :],
                                   accum_out=part[:, :]).then_inc(expds, 1)
                    act.wait_ge(sums, j + 1)
                    act.activation(log_sum[:, :], bank[1][:, 0:1], ACT.Ln).then_inc(logs, 1)
                act.wait_ge(gaps, 2)
                act.activation(expd[:, :], clipped[:, :], ACT.Exp).then_inc(score_exp, 1)

            @block.tensor
            def _(pe):
                pe.wait_ge(made, 12)
                pe.transpose(bank[0][:, 0:P], scores[:, :], ident[:, :]).then_inc(pe_done, 1)
                pe.wait_ge(chain, 2)
                pe.transpose(bank[0][0:1, 0:P], top[:, :], ident[:, :]).then_inc(pe_done, 1)
                pe.wait_ge(chain, 4)
                pe.matmul(bank[0][:, 0:1], top_row[:, :, :].rearrange("p b t -> p (b t)"), ones[0:1, 0:1],
                          start=True, stop=True).then_inc(pe_done, 1)
                with pe.Fori(0, DESCENT_STEPS - 1) as j:
                    pe.wait_ge(expds, j + 1)
                    pe.matmul(bank[1][:, 0:1], same[:, :], part[:, :], start=True, stop=True).then_inc(sums, 1)
                with pe.Fori(0, 31) as j:
                    pe.wait_ge(counts, j + 1)
                    pe.matmul(bank[2][:, 0:1], same[:, :], count[:, 0:1], start=True, stop=True).then_inc(totals, 1)
                pe.wait_ge(counts, 33)
                pe.matmul(bank[2][:, 2:3], same[:, :], count[:, 0:1], start=True, stop=True)
                pe.matmul(bank[2][:, 3:4], prior[:, :], count[:, 1:2], start=True, stop=True).then_inc(pe_done, 1)
                pe.wait_ge(counts, 34)
                pe.matmul(bank[2][:, 4:5], prior[:, :], count[:, 0:1], start=True, stop=True).then_inc(pe_done, 1)
                pe.wait_ge(caps, DESCENT_STEPS + 1)
                pe.transpose(bank[3][:, 0:P], slot[:, :], ident[:, :])
                pe.transpose(bank[3][:, P:2 * P], straight[:, :], ident[:, :]).then_inc(pe_done, 1)
                pe.wait_ge(caps, DESCENT_STEPS + 2)
                for b in range(B):
                    pe.wait_ge(taken, NT * (b + 1))
                    for j in range(NJ):
                        for t in range(NT):
                            last = pe.matmul(bank[4 + j][:, 2 * b:2 * b + 2],
                                             takes[(b % 2) * NT + t][:, j * P:(j + 1) * P],
                                             tagged[:, b * NT + t, :], start=(t == 0), stop=(t == NT - 1))
                    last.then_inc(lists, 1)

            @block.vector
            def _(dve):
                links = [0]

                def link(ins):
                    links[0] += 1
                    ins.then_inc(chain, 1)
                    dve.wait_ge(chain, links[0])

                dve.wait_ge(made, 12)
                dve.wait_ge(pe_done, 1)
                link(dve.tensor_copy(s_rows[:, :], bank[0][:, 0:P]))
                link(dve.tensor_reduce(top[:, :], s_rows[:, :], AX, ALU.max))
                dve.wait_ge(pe_done, 2)
                link(dve.tensor_reduce(top_seq[:, :], bank[0][0:1, 0:P].rearrange("p (b t) -> p b t", t=NT), AX, ALU.max))
                link(dve.tensor_scalar(top_row[:, :, :], top_seq[:, :].unsqueeze(2).to_broadcast([1, B, NT]), 0.0, None,
                                       ALU.add))
                dve.wait_ge(pe_done, 3)
                dve.tensor_copy(top_all[:, :], bank[0][:, 0:1]).then_inc(caps, 1)
                dve.wait_ge(caps, 1)
                with dve.Fori(0, DESCENT_STEPS - 1) as j:
                    dve.tensor_scalar(shift[:, :], top_all[:, :], cap[:, :], -1.0, ALU.min, ALU.mult).then_inc(shifted, 1)
                    dve.tensor_scalar(clipped[:, :], s_rows[:, :], cap[:, :], None, ALU.min).then_inc(shifted, 1)
                    dve.wait_ge(logs, j + 1)
                    dve.tensor_scalar(cap[:, :], log_sum[:, :], shift[:, :], LOG_K, ALU.subtract, ALU.subtract)\
                       .then_inc(caps, 1)
                    gate(dve, caps, j + 2)
                dve.tensor_scalar(clipped[:, :], s_rows[:, :], cap[:, :], 0.0, ALU.subtract, ALU.min).then_inc(gaps, 1)
                dve.wait_ge(gaps, 1)
                dve.tensor_scalar(gap[:, :], clipped[:, :], -1.0, 104.0, ALU.mult, ALU.min).then_inc(gaps, 1)
                dve.wait_ge(gaps, 2)
                with dve.Fori(0, 31) as j:
                    dve.tensor_tensor(trial[:, :], limit[:, :], bit[:, :], ALU.bitwise_or).then_inc(limits, 1)
                    dve.wait_ge(limits, j * 3 + 1)
                    dve.tensor_scalar(better[:, :], gap[:, :], trial[:, :].bitcast(F32), 0.0, ALU.is_lt, ALU.add,
                                      accum_out=count[:, 0:1]).then_inc(counts, 1)
                    dve.wait_ge(totals, j + 1)
                    dve.tensor_scalar(keep[:, :], bank[2][:, 0:1], float(NUM_HEAVY), -1.0, ALU.is_lt, ALU.mult)\
                       .then_inc(limits, 1)
                    dve.wait_ge(limits, j * 3 + 2)
                    dve.tensor_tensor(keep[:, :], keep[:, :], bit[:, :], ALU.bitwise_and).then_inc(limits, 1)
                    dve.wait_ge(limits, j * 3 + 3)
                    dve.tensor_tensor(limit[:, :], limit[:, :], keep[:, :], ALU.bitwise_or)
                    dve.tensor_scalar(bit[:, :], bit[:, :], 1, None, ALU.logical_shift_right).then_inc(bits, 1)
                    gate(dve, bits, j + 1)
                edge = limit[:, :].bitcast(F32)
                dve.tensor_scalar(better[:, :], gap[:, :], edge, 0.0, ALU.is_lt, ALU.add,
                                  accum_out=count[:, 0:1]).then_inc(counts, 1)
                dve.tensor_scalar(equal[:, :], gap[:, :], edge, 0.0, ALU.is_equal, ALU.add,
                                  accum_out=count[:, 1:2]).then_inc(counts, 1)
                dve.wait_ge(counts, 33)
                link(dve.tensor_tensor_scan(run_eq[:, :], equal[:, :], zeros[:, :], 0.0, ALU.add, ALU.add))
                dve.wait_ge(pe_done, 4)
                link(dve.tensor_scalar(room[:, :], bank[2][:, 2:3], -1.0, float(NUM_HEAVY), ALU.mult, ALU.add))
                link(dve.tensor_tensor(room[:, :], room[:, :], bank[2][:, 3:4], ALU.subtract))
                link(dve.tensor_scalar(run_eq[:, :], run_eq[:, :], room[:, :], None, ALU.is_le))
                link(dve.tensor_tensor(run_eq[:, :], run_eq[:, :], equal[:, :], ALU.mult))
                link(dve.tensor_tensor(picked[:, :], run_eq[:, :], better[:, :], ALU.add))
                dve.tensor_reduce(count[:, 0:1], picked[:, :], AX, ALU.add).then_inc(counts, 1)
                link(dve.tensor_tensor_scan(slot[:, :], picked[:, :], zeros[:, :], 0.0, ALU.add, ALU.add))
                dve.wait_ge(pe_done, 5)
                link(dve.tensor_scalar(slot[:, :], slot[:, :], bank[2][:, 4:5], None, ALU.add))
                link(dve.tensor_tensor(slot[:, :], slot[:, :], picked[:, :], ALU.mult))
                link(dve.tensor_scalar(slot[:, :], slot[:, :], -1.0, None, ALU.add))
                dve.wait_ge(score_exp, 1)
                link(dve.tensor_scalar(straight[:, :], expd[:, :], -1.0, 1.0, ALU.mult, ALU.add))
                dve.tensor_tensor(straight[:, :], straight[:, :], expd[:, :], ALU.add).then_inc(caps, 1)
                dve.wait_ge(pe_done, 6)
                link(dve.tensor_copy(slot_t[:, :], bank[3][:, 0:P]))
                dve.tensor_copy(tagged[:, :, 1], bank[3][:, P:2 * P]).then_inc(caps, 1)
                for b in range(B):
                    if b >= 2:
                        dve.wait_ge(lists, b - 1)
                    for t in range(NT):
                        g = b * NT + t
                        dve.tensor_scalar(takes[(b % 2) * NT + t][:, :], slots[:, :], slot_t[:, g:g + 1], None,
                                          ALU.is_equal).then_inc(taken, 1)
                dve.wait_ge(lists, B)
                for j in range(NJ):
                    pairs = bank[4 + j][:, 0:2 * B].rearrange("p (b e) -> p b e", e=2)
                    dve.tensor_copy(listed[:, 0:B * NJ].rearrange("p (b j) -> p b j", j=NJ)[:, :, j], pairs[:, :, 0])
                    dve.tensor_copy(weights[:, :].rearrange("p (b j) -> p b j", j=NJ)[:, :, j], pairs[:, :, 1])

        with ExitStack() as c:
            both = [sb(f"h_both{n}", [P, NJ, 2 * D], c=c) for n in range(2)]
            normed_x = sb("h_normed_x", [P, NJ, D], c=c)
            xt = [sb(f"xt_h{n}", [P, ND, 512], c=c) for n in range(2)]
            hidden = [sb(f"h_hidden{n}", [P, 512], c=c) for n in range(4)]
            w1 = sb("h_w1_sb", [P, ND, FH * P], c=c)
            w2 = sb("h_w2_sb", [P, FH, D], c=c)
            gamma = sb("h_gamma_sb", [P, ND], c=c)
            b1 = sb("h_b1_sb", [P, FH], c=c)
            b2 = sb("h_b2_sb", [P, D], c=c)
            rows = [sb(f"rows{n}", [P, NJ], U32, c=c) for n in range(2)]
            weight = sb("weight", [P, NJ], c=c)
            stats = sb("h_stats", [P, NJ, 6], c=c)
            moments = sb("h_moments", [P, NJ, 2], c=c)
            var_eps = sb("h_var_eps", [P, NJ], c=c)
            rstd = sb("h_rstd", [P, NJ], c=c)
            std = sb("h_std", [P, NJ], c=c)
            norm = sb("h_norm", [P, NJ], c=c)
            rnorm = sb("h_rnorm", [P, NJ], c=c)
            scale = sb("h_scale", [P, NJ], c=c)
            o_stats = sb("ho_stats", [P, NJ, 6], c=c)
            o_moments = sb("ho_moments", [P, NJ, 2], c=c)
            o_var_eps = sb("ho_var_eps", [P, NJ], c=c)
            o_rstd = sb("ho_rstd", [P, NJ], c=c)
            mix = [sb(f"mix{n}", [P, NJ, D], c=c) for n in range(2)]

            wloads = sem("heavy_weights", c)
            folded = sem("heavy_gamma_folded", c)
            indexed = sem("heavy_indexed", c)
            gathered = [sem(f"heavy_gathered{n}", c) for n in range(2)]
            scattered = [sem(f"heavy_scattered{n}", c) for n in range(2)]
            stats_done = sem("heavy_stats", c)
            moments_done = sem("heavy_moments", c)
            var_done = sem("heavy_var", c)
            pow_done = sem("heavy_pow", c)
            scaled = sem("heavy_scaled", c)
            normed = sem("heavy_normed", c)
            turned = sem("heavy_turned", c)
            turned_sb = sem("heavy_turned_sb", c)
            hidden_ps = sem("heavy_hidden_ps", c)
            hidden_sb = sem("heavy_hidden_sb", c)
            used = sem("heavy_hidden_used", c)
            weighed = sem("heavy_weighed", c)
            mixed = sem("heavy_mixed", c)
            out_n = sem("heavy_out_normed", c)
            out_ready = sem("heavy_out_ready", c)
            chain = sem("heavy_chain", c)
            turn = bank[0:2]
            hid = bank[2:4]
            outs = bank[4:8]
            block = c.enter_context(nc.Block())

            @block.sync
            def _(sp):
                for dst, src in (
                    (w1[:, :, :], h_w1.rearrange("(c p) f -> p c f", p=P)),
                    (w2[:, :, :], h_w2.rearrange("(c p) f -> p c f", p=P)),
                    (gamma[:, :], h_gamma.rearrange("(c p) -> p c", p=P)),
                    (b1[:, :], h_b1.rearrange("(c p) -> p c", p=P)),
                    (b2[:, :], h_b2.partition_broadcast(P)),
                ):
                    sp.dma_start(dst, src, allow_slow_non_contiguous=True).then_inc(wloads, 16)

            @block.gpsimd
            def _(pool):
                def gather(h):
                    for j in range(NJ):
                        pool.indirect_dma_start(both[h][:, j, :], None, xl_dram,
                                                bass.IndirectOffsetOnAxis(rows[h][:, j:j + 1], 0))\
                            .then_inc(gathered[h], 16)

                def finish(i, h):
                    pool.wait_ge(var_done, at(i, h, 2, 1))
                    pool.tensor_tensor(rstd[:, :], var_eps[:, :], neg_half[:, 0:NJ], ALU.pow).then_inc(pow_done, 1)
                    pool.tensor_tensor(std[:, :], moments[:, :, 1], half[:, 0:NJ], ALU.pow).then_inc(pow_done, 1)
                    pool.wait_ge(var_done, at(i, h, 2, 2))
                    pool.tensor_tensor(o_rstd[:, :], o_var_eps[:, :], neg_half[:, 0:NJ], ALU.pow).then_inc(pow_done, 1)
                    gate(pool, out_ready, at(i, h, NJ, NJ))
                    for j in range(NJ):
                        pool.indirect_dma_start(out_flat, bass.IndirectOffsetOnAxis(rows[h][:, j:j + 1], 0),
                                                mix[h][:, j, :], None).then_inc(scattered[h], 16)

                for n in range(2):
                    pool.wait_ge(indexed, n + 1)
                    gather(n)
                with pool.Fori(0, PAIRS - 1) as i:
                    for h in range(2):
                        finish(i, h)
                        gate(pool, indexed, at(i, h, 1, 3))
                        gather(h)
                for h in range(2):
                    finish(PAIRS - 1, h)
                for n in range(2):
                    pool.wait_ge(scattered[n], 16 * NJ * PAIRS)

            @block.scalar
            def _(act):
                act.sem_inc(turned_sb, 2)
                act.sem_inc(hidden_sb, 2)
                act.wait_ge(wloads, 80)
                with act.Fori(0, PAIRS) as i:
                    for h in range(2):
                        for j in range(NJ):
                            act.wait_ge(turned, at(i, h, NJ, j + 1))
                            act.activation(xt[h][:, :, j * P:(j + 1) * P],
                                           turn[j % 2][:, :].rearrange("p (c q) -> p c q", c=ND),
                                           ACT.Copy).then_inc(turned_sb, 1)
                        for f in range(FH):
                            act.wait_ge(hidden_ps, at(i, h, FH, f + 1))
                            act.wait_ge(used, at(i, h, FH, f + 1))
                            act.activation(hidden[f % 4][:, :], hid[f % 2][:, :], ACT.Gelu,
                                           bias=b1[:, f:f + 1]).then_inc(hidden_sb, 1)

            @block.tensor
            def _(pe):
                pe.sem_inc(used, 4)
                pe.wait_ge(folded, ND)

                def first(i, h, f):
                    pe.wait_ge(hidden_sb, at(i, h, FH, f + 1))
                    for c_ in range(ND):
                        last = pe.matmul(hid[f % 2][:, :], w1[:, c_, f * P:(f + 1) * P], xt[h][:, c_, :],
                                         start=(c_ == 0), stop=(c_ == ND - 1))
                    last.then_inc(hidden_ps, 1)

                def second(i, h, f):
                    pe.wait_ge(hidden_sb, at(i, h, FH, f + 1) + 2)
                    if f == 0:
                        pe.wait_ge(weighed, at(i, h, NJ, NJ))
                    for j in range(NJ):
                        last = pe.matmul(outs[j][:, :], hidden[f % 4][:, j * P:(j + 1) * P], w2[:, f, :],
                                         start=(f == 0), stop=(f == FH - 1))
                    last.then_inc(used, 1)

                with pe.Fori(0, PAIRS) as i:
                    for h in range(2):
                        for j in range(NJ):
                            pe.wait_ge(normed, at(i, h, NJ, j + 1))
                            pe.wait_ge(turned_sb, at(i, h, NJ, j + 1))
                            for c_ in range(ND):
                                last = pe.transpose(turn[j % 2][:, c_ * P:(c_ + 1) * P],
                                                    normed_x[:, j, c_ * P:(c_ + 1) * P], ident[:, :])
                            last.then_inc(turned, 1)
                        pe.wait_ge(turned_sb, at(i, h, NJ, NJ) + 2)
                        first(i, h, 0)
                        for f in range(1, FH):
                            first(i, h, f)
                            second(i, h, f - 1)
                        second(i, h, FH - 1)

            @block.vector
            def _(dve):
                LINKS = 4
                dve.sem_inc(weighed, NJ)
                dve.wait_ge(wloads, 80)
                for c_ in range(ND):
                    dve.tensor_scalar(w1[:, c_, :], w1[:, c_, :], gamma[:, c_:c_ + 1], None, ALU.mult)\
                       .then_inc(folded, 1)
                for n in range(2):
                    dve.tensor_scalar(rows[n][:, :], listed[:, n * NJ:(n + 1) * NJ], 0.0, None,
                                      ALU.add).then_inc(indexed, 1)
                with dve.Fori(0, PAIRS) as i:
                    for h in range(2):
                        links = [0]

                        def link(ins):
                            links[0] += 1
                            ins.then_inc(chain, 1)
                            dve.wait_ge(chain, at(i, h, LINKS, links[0]))

                        gate(dve, gathered[h], i * (16 * NJ) + 16 * NJ)
                        for j in range(NJ):
                            dve.bn_stats(stats[:, j, :], both[h][:, j, 0:D]).then_inc(stats_done, 1)
                        gate(dve, stats_done, at(i, h, 2 * NJ, NJ))
                        for j in range(NJ):
                            dve.bn_aggr(moments[:, j, :], stats[:, j, :]).then_inc(moments_done, 1)
                        dve.wait_ge(moments_done, at(i, h, 2 * NJ, NJ))
                        dve.tensor_scalar(var_eps[:, :], moments[:, :, 1], LN_EPS, None, ALU.add).then_inc(var_done, 1)
                        dve.wait_ge(pow_done, at(i, h, 3, 2))
                        link(dve.scalar_tensor_tensor(out=norm[:, :], in0=std[:, :], scalar=SQRT_D, in1=rstd[:, :],
                                                      op0=ALU.mult, op1=ALU.mult))
                        link(dve.tensor_scalar(norm[:, :], norm[:, :], NORM_EPS, 1.0 / SQRT_D, ALU.max, ALU.mult))
                        link(dve.reciprocal(rnorm[:, :], norm[:, :]))
                        dve.tensor_tensor(scale[:, :], rstd[:, :], rnorm[:, :], ALU.mult).then_inc(scaled, 1)
                        dve.wait_ge(scaled, at(i, h, 1, 1))
                        for j in range(NJ):
                            dve.tensor_scalar(normed_x[:, j, :], both[h][:, j, 0:D], moments[:, j, 0:1],
                                              scale[:, j:j + 1], ALU.subtract, ALU.mult).then_inc(normed, 1)
                        link(dve.tensor_scalar(weight[:, :], weights[:, bass.ds((i * 2 + h) * NJ, NJ)], 0.0, None,
                                               ALU.add))
                        dve.wait_ge(used, at(i, h, FH, FH) + 4)
                        for j in range(NJ):
                            dve.tensor_tensor(mix[h][:, j, :], outs[j][:, :], b2[:, :], ALU.add).then_inc(weighed, 1)
                        for j in range(NJ):
                            dve.wait_ge(weighed, at(i, h, NJ, j + 1) + NJ)
                            dve.scalar_tensor_tensor(out=mix[h][:, j, :], in0=mix[h][:, j, :],
                                                     scalar=weight[:, j:j + 1], in1=both[h][:, j, D:2 * D],
                                                     op0=ALU.mult, op1=ALU.add).then_inc(mixed, 1)
                        for j in range(NJ):
                            gate(dve, mixed, at(i, h, NJ, j + 1))
                            dve.bn_stats(o_stats[:, j, :], mix[h][:, j, :]).then_inc(stats_done, 1)
                        gate(dve, stats_done, at(i, h, 2 * NJ, 2 * NJ))
                        for j in range(NJ):
                            dve.bn_aggr(o_moments[:, j, :], o_stats[:, j, :]).then_inc(moments_done, 1)
                        dve.wait_ge(moments_done, at(i, h, 2 * NJ, 2 * NJ))
                        dve.tensor_scalar(o_var_eps[:, :], o_moments[:, :, 1], LN_EPS, None, ALU.add)\
                           .then_inc(var_done, 1)
                        dve.wait_ge(pow_done, at(i, h, 3, 3))
                        for j in range(NJ):
                            dve.tensor_scalar(mix[h][:, j, :], mix[h][:, j, :], o_moments[:, j, 0:1],
                                              o_rstd[:, j:j + 1], ALU.subtract, ALU.mult).then_inc(out_n, 1)
                        for j in range(NJ):
                            dve.wait_ge(out_n, at(i, h, NJ, j + 1))
                            dve.tensor_tensor(mix[h][:, j, :], mix[h][:, j, :], both[h][:, j, 0:D],
                                              ALU.add).then_inc(out_ready, 1)
                        dve.wait_ge(scattered[h], i * (16 * NJ) + 16 * NJ)
                        dve.tensor_scalar(rows[h][:, :], listed[:, bass.ds((i * 2 + (2 + h)) * NJ, NJ)], 0.0, None,
                                          ALU.add).then_inc(indexed, 1)
                        assert links[0] == LINKS, links[0]


def kernel(**inputs):
    import numpy as np
    import concourse.bacc as bacc
    from concourse.bass_utils import run_bass_kernel_spmd as run

    g = {k: np.asarray(v) for k, v in inputs.items()}
    x = g["L0_attn_x"]
    rank = g["L0_attn_dt_projs_weight"].shape[1]
    states = g["L0_attn_A_logs"].shape[1]
    proj = g["L0_attn_x_proj_weight"].T
    w_x = np.zeros((proj.shape[0], P), proj.dtype)
    for n in range(3):
        w_x[:, 32 * n:32 * n + states] = proj[:, rank:rank + states]
    w_x[:, 96:96 + rank] = proj[:, :rank]
    arrays = {
        "x": x, "means": g["L0_attn_means"], "means_t": g["L0_attn_means"].T,
        "prompt_t": g["L0_attn_prompt_weight"].T, "w_x": w_x, "w_c": proj[:, rank + states:],
        "w_dt_t": g["L0_attn_dt_projs_weight"].T, "dt_bias": g["L0_attn_dt_projs_bias"],
        "a_logs": g["L0_attn_A_logs"], "ds": g["L0_attn_Ds"],
        "routing": g["L0_ffn_routing_token"],
    }
    for side in ("light", "heavy"):
        for part in ("gamma", "w1", "b1", "w2", "b2"):
            arrays[f"{side[0]}_{part}"] = g[f"L0_ffn_{side}_{part}"]
    arrays = {k: np.ascontiguousarray(v) for k, v in arrays.items()}
    nc = bacc.Bacc("TRN2", target_bir_lowering=False, num_devices=1)
    args = {k: nc.dram_tensor(f"in_{k}", v.shape, mybir.dt.from_np(v.dtype), kind="ExternalInput").ap()
            for k, v in arrays.items()}
    out = nc.dram_tensor("out", x.shape, F32, kind="ExternalOutput").ap()
    build(nc, out=out, **args)
    result = run(nc, [{f"in_{k}": v for k, v in arrays.items()}], core_ids=[0])
    return result.results[0]["out"]
```

```python
import math
from contextlib import ExitStack

import concourse.bass as bass
from concourse import mybir

P = 128
F32 = mybir.dt.float32
F32R = mybir.dt.float32r
BF16 = mybir.dt.bfloat16
U32 = mybir.dt.uint32
I32 = mybir.dt.int32
ALU = mybir.AluOpType
ACT = mybir.ActivationFunctionType
AX = mybir.AxisListType.X

LN_EPS = 1e-5
NORM_EPS = 1e-12
NUM_HEAVY = 512
DESCENT_STEPS = 50
EFFECTIVE_K = 576.0
LOG_K = 6.356107660695891


def build(nc, x, means, means_t, prompt_t, w_x, w_c, w_dt_t, dt_bias, a_logs, ds,
          routing, l_gamma, l_w1, l_b1, l_w2, l_b2, h_gamma, h_w1, h_b1, h_w2, h_b2, out):
    B, L, D = x.shape
    NT = L // P
    ND = D // P
    K = means.shape[0]
    NS = w_c.shape[1]
    R = w_dt_t.shape[0]
    FL = l_w1.shape[1] // P
    FH = h_w1.shape[1] // P
    NJ = NUM_HEAVY // P
    PAIRS = B // 2
    KT = K * NT
    DT_ROW = 3 * 32
    SQRT_D = float(D) ** 0.5

    xs_dram = nc.dram_tensor("sorted_rows", [B * L, D], F32, kind="Internal").ap()
    ys_dram = nc.dram_tensor("sorted_outputs", [B * L, D], F32, kind="Internal").ap()
    xl_dram = nc.dram_tensor("residual_and_light", [B * L, 2 * D], F32, kind="Internal").ap()

    x_rows = x.rearrange("b (t p) d -> b p t d", p=P)
    xs_rows = xs_dram.rearrange("(b t p) d -> b p t d", p=P, t=NT)
    ys_rows = ys_dram.rearrange("(b t p) d -> b p t d", p=P, t=NT)
    xl_rows = xl_dram.rearrange("(b t p) d -> b p t d", p=P, t=NT)
    out_flat = out.rearrange("b l d -> (b l) d")
    out_rows = out.rearrange("b (t p) d -> b p t d", p=P)

    def row(view, b):
        return view[bass.ds(b, 1)].rearrange("a p t d -> (a p) t d")

    def at(i, h, per, k):
        return i * (2 * per) + (per * h + k)

    with ExitStack() as ctx:
        def sb(name, shape, dt=F32, c=ctx):
            return c.enter_context(nc.sbuf_tensor(name, shape, dt))

        def sem(name, c=ctx):
            return c.enter_context(nc.semaphore(name))

        gates = sem("gates_passed")

        def gate(eng, signal, value):
            eng.wait_ge(signal, value)
            eng.sem_inc(gates, 1)

        bank = [ctx.enter_context(nc.psum_tensor(f"bank{n}", [P, 512], F32)) for n in range(8)]

        ident = sb("ident", [P, P])
        ones = sb("ones", [P, P])
        positions = sb("positions", [P, (B + 2) * NT], U32)
        bounds = sb("bounds", [K, 2 * B])
        scores = sb("scores", [P, B * NT])
        half = sb("half", [P, NT])
        neg_half = sb("neg_half", [P, NT])
        mean_dirs = sb("mean_dirs", [P, ND, K])
        cluster_c = sb("cluster_c", [K, NS])
        zero_bias = sb("zero_bias", [P, 1])
        one_bias = sb("one_bias", [P, 1])

        with ExitStack() as c:
            means_sb = sb("means_sb", [K, D], c=c)
            means_sq = sb("means_sq", [K, D], c=c)
            mnorm = sb("mnorm", [K, 4], c=c)
            mhalf = sb("mhalf", [K, 1], c=c)
            means_ts = sb("means_ts", [P, ND, K], c=c)
            prompt_ts = sb("prompt_ts", [P, ND, NS], c=c)
            loads = sem("setup_loads", c)
            made = sem("setup_made", c)
            chain = sem("setup_chain", c)
            powered = sem("setup_powered", c)
            product = sem("setup_product", c)
            block = c.enter_context(nc.Block())

            @block.sync
            def _(sp):
                sp.dma_start(means_sb[:, :], means).then_inc(loads, 16)
                sp.dma_start(means_ts[:, :, :], means_t.rearrange("(c p) k -> p c k", p=P)).then_inc(loads, 16)
                sp.dma_start(prompt_ts[:, :, :], prompt_t.rearrange("(c p) n -> p c n", p=P)).then_inc(loads, 16)

            @block.gpsimd
            def _(pool):
                pool.memset(ident[:, :], 0.0).then_inc(made, 1)
                pool.memset(ones[:, :], 1.0).then_inc(made, 1)
                pool.memset(half[:, :], 0.5).then_inc(made, 1)
                pool.memset(neg_half[:, :], -0.5).then_inc(made, 1)
                pool.memset(mhalf[:, :], 0.5).then_inc(made, 1)
                pool.memset(positions[:, :], 0).then_inc(made, 1)
                pool.memset(zero_bias[:, :], 0.0).then_inc(made, 1)
                pool.memset(one_bias[:, :], 1.0).then_inc(made, 1)
                pool.wait_ge(made, 8)
                pool.affine_select(out=ident[:, :], in_=ident[:, :], compare_op=ALU.not_equal, fill=1.0,
                                   base=0, pattern=[[-1, P]], channel_multiplier=1).then_inc(made, 1)
                pool.wait_ge(chain, 2)
                pool.tensor_tensor(mnorm[:, 1:2], mnorm[:, 0:1], mhalf[:, :], ALU.pow).then_inc(powered, 1)

            @block.vector
            def _(dve):
                dve.wait_ge(loads, 48)
                dve.tensor_tensor(means_sq[:, :], means_sb[:, :], means_sb[:, :], ALU.mult).then_inc(chain, 1)
                dve.wait_ge(chain, 1)
                dve.tensor_reduce(mnorm[:, 0:1], means_sq[:, :], AX, ALU.add).then_inc(chain, 1)
                dve.wait_ge(powered, 1)
                dve.tensor_scalar(mnorm[:, 2:3], mnorm[:, 1:2], NORM_EPS, None, ALU.max).then_inc(chain, 1)
                dve.wait_ge(chain, 3)
                dve.reciprocal(mnorm[:, 3:4], mnorm[:, 2:3]).then_inc(chain, 1)
                dve.wait_ge(chain, 4)
                dve.tensor_scalar(means_sq[:, :], means_sb[:, :], mnorm[:, 3:4], None, ALU.mult).then_inc(chain, 1)
                dve.wait_ge(product, 1)
                dve.tensor_copy(mean_dirs[:, :, :].rearrange("p c k -> p (c k)"), bank[0][:, 0:ND * K]).then_inc(chain, 1)
                dve.wait_ge(product, 2)
                dve.tensor_copy(cluster_c[:, :], bank[1][0:K, 0:NS]).then_inc(chain, 1)

            @block.tensor
            def _(pe):
                pe.wait_ge(made, 9)
                pe.wait_ge(chain, 5)
                for c_ in range(ND):
                    last = pe.transpose(bank[0][:, c_ * K:(c_ + 1) * K], means_sq[:, c_ * P:(c_ + 1) * P],
                                        ident[0:K, 0:K])
                last.then_inc(product, 1)
                for c_ in range(ND):
                    last = pe.matmul(bank[1][0:K, 0:NS], means_ts[:, c_, :], prompt_ts[:, c_, :],
                                     start=(c_ == 0), stop=(c_ == ND - 1))
                last.then_inc(product, 1)

        with ExitStack() as c:
            xa = [sb(f"xa{n}", [P, NT, D], c=c) for n in range(2)]
            xt = [sb(f"xt{n}", [P, ND, P], c=c) for n in range(2)]
            stats = sb("stats", [P, NT, 6], c=c)
            moments = sb("moments", [P, NT, 2], c=c)
            var_eps = sb("var_eps", [P, NT], c=c)
            rstd = sb("rstd", [P, NT], c=c)
            std = sb("std", [P, NT], c=c)
            norm = sb("norm", [P, NT], c=c)
            rnorm = sb("rnorm", [P, NT], c=c)
            cosines = sb("cosines", [P, NT, K], c=c)
            best = sb("best", [P, NT], c=c)
            is_best = sb("is_best", [P, NT, K], c=c)
            candidate = sb("candidate", [P, NT, K], c=c)
            cluster = sb("cluster", [P, NT], c=c)
            cluster_ids = sb("cluster_ids", [P, NT, K], c=c)
            cluster_ids_m = sb("cluster_ids_m", [P, NT, K], c=c)
            ids_i = sb("ids_i", [P, NT, K], I32, c=c)
            onehot = sb("onehot", [P, K, NT], BF16, c=c)
            below = sb("below", [P, NT, K], BF16, c=c)
            upto = sb("upto", [P, NT, K], BF16, c=c)
            earlier = sb("earlier", [P, P], BF16, c=c)
            ones_b = sb("ones_b", [P, P], BF16, c=c)
            zeros = sb("zeros", [P, KT], c=c)
            totals = sb("totals", [P, KT], c=c)
            running = sb("running", [P, KT], c=c)
            before = sb("before", [P, KT], c=c)
            place = sb("place", [P, KT], c=c)
            chosen = sb("chosen", [P, KT], c=c)
            place_in_seq = sb("place_in_seq", [P, NT], c=c)
            first_row = sb("first_row", [P, 1], c=c)
            target = [sb(f"target{n}", [P, NT], U32, c=c) for n in range(2)]
            made = sem("sort_consts", c)
            loaded = [sem(f"sort_loaded{n}", c) for n in range(2)]
            stats_done = sem("sort_stats", c)
            moments_done = sem("sort_moments", c)
            var_done = sem("sort_var", c)
            pow_done = sem("sort_pow", c)
            normed = sem("sort_normed", c)
            turned = sem("sort_turned", c)
            turned_sb = sem("sort_turned_sb", c)
            cos_done = sem("sort_cosines", c)
            onehots = sem("sort_onehots", c)
            counted = sem("sort_counted", c)
            chain = sem("sort_chain", c)
            targets = sem("sort_targets", c)
            scattered = [sem(f"sort_scattered{n}", c) for n in range(2)]
            turn = bank[0:2]
            cos_ps = bank[2]
            count_ps = bank[3]
            block = c.enter_context(nc.Block())

            @block.sync
            def _(sp):
                for n in range(2):
                    sp.dma_start(xa[n][:, :, :], row(x_rows, n)).then_inc(loaded[n], 16)
                with sp.Fori(0, PAIRS - 1) as i:
                    for h in range(2):
                        sp.wait_ge(scattered[h], i * (16 * NT) + 16 * NT)
                        sp.dma_start(xa[h][:, :, :], row(x_rows, i * 2 + (2 + h))).then_inc(loaded[h], 16)

            @block.gpsimd
            def _(pool):
                pool.memset(earlier[:, :], 1.0).then_inc(made, 1)
                pool.memset(ones_b[:, :], 1.0).then_inc(made, 1)
                pool.memset(zeros[:, :], 0.0).then_inc(made, 1)
                pool.memset(first_row[:, :], 0.0).then_inc(made, 1)
                pool.iota(ids_i[:, :, :], pattern=[[0, NT], [1, K]], base=0, channel_multiplier=0).then_inc(made, 1)
                pool.wait_ge(made, 5)
                pool.affine_select(out=earlier[:, :], in_=earlier[:, :], compare_op=ALU.is_gt, fill=0.0,
                                   base=0, pattern=[[1, P]], channel_multiplier=-1).then_inc(made, 1)
                pool.tensor_copy(cluster_ids[:, :, :], ids_i[:, :, :]).then_inc(made, 1)
                pool.wait_ge(made, 7)
                pool.tensor_scalar(cluster_ids_m[:, :, :], cluster_ids[:, :, :], -float(K), None,
                                   ALU.add).then_inc(made, 1)
                with pool.Fori(0, PAIRS) as i:
                    for h in range(2):
                        pool.wait_ge(var_done, at(i, h, 1, 1))
                        pool.tensor_tensor(rstd[:, :], var_eps[:, :], neg_half[:, :], ALU.pow).then_inc(pow_done, 1)
                        pool.tensor_tensor(std[:, :], moments[:, :, 1], half[:, :], ALU.pow).then_inc(pow_done, 1)
                        gate(pool, targets, at(i, h, 1, 1))
                        for t in range(NT):
                            pool.indirect_dma_start(xs_dram, bass.IndirectOffsetOnAxis(target[h][:, t:t + 1], 0),
                                                    xa[h][:, t, :], None).then_inc(scattered[h], 16)
                for n in range(2):
                    pool.wait_ge(scattered[n], 16 * NT * PAIRS)

            @block.scalar
            def _(act):
                act.sem_inc(turned_sb, 2)
                with act.Fori(0, PAIRS) as i:
                    for h in range(2):
                        for t in range(NT):
                            act.wait_ge(turned, at(i, h, NT, t + 1))
                            act.wait_ge(cos_done, at(i, h, NT, t + 1))
                            act.activation(xt[t % 2][:, :, :].rearrange("p c q -> p (c q)"), turn[t % 2][:, :],
                                           ACT.Copy).then_inc(turned_sb, 1)

            @block.tensor
            def _(pe):
                pe.wait_ge(made, 8)
                pe.sem_inc(cos_done, 2)

                def turn_tile(i, h, t):
                    pe.wait_ge(normed, at(i, h, NT, t + 1))
                    pe.wait_ge(turned_sb, at(i, h, NT, t + 1))
                    for c_ in range(ND):
                        last = pe.transpose(turn[t % 2][:, c_ * P:(c_ + 1) * P], xa[h][:, t, c_ * P:(c_ + 1) * P],
                                            ident[:, :])
                    last.then_inc(turned, 1)

                def cos_tile(i, h, t):
                    pe.wait_ge(turned_sb, at(i, h, NT, t + 3))
                    for c_ in range(ND):
                        last = pe.matmul(cos_ps[:, t * K:(t + 1) * K], xt[t % 2][:, c_, :], mean_dirs[:, c_, :],
                                         start=(c_ == 0), stop=(c_ == ND - 1))
                    last.then_inc(cos_done, 1)

                with pe.Fori(0, PAIRS) as i:
                    for h in range(2):
                        for t in range(NT):
                            turn_tile(i, h, t)
                            if t:
                                cos_tile(i, h, t - 1)
                        cos_tile(i, h, NT - 1)
                        pe.wait_ge(onehots, at(i, h, 3, 3))
                        flat = onehot[:, :, :].rearrange("p k t -> p (k t)")
                        pe.matmul(count_ps[:, 0:KT], earlier[:, :], flat, start=True, stop=True)
                        pe.matmul(count_ps[:, KT:2 * KT], ones_b[:, :], flat, start=True, stop=True)
                        for e, mask in enumerate((below, upto)):
                            for t in range(NT):
                                last = pe.matmul(count_ps[0:K, 2 * KT + e:2 * KT + e + 1], mask[:, t, :],
                                                 ones_b[:, 0:1], start=(t == 0), stop=(t == NT - 1))
                        last.then_inc(counted, 1)

            @block.vector
            def _(dve):
                LINKS = 15
                dve.wait_ge(made, 8)
                with dve.Fori(0, PAIRS) as i:
                    for h in range(2):
                        links = [0]

                        def link(ins):
                            links[0] += 1
                            ins.then_inc(chain, 1)
                            dve.wait_ge(chain, at(i, h, LINKS, links[0]))

                        dve.wait_ge(loaded[h], i * 16 + 16)
                        for t in range(NT):
                            dve.bn_stats(stats[:, t, :], xa[h][:, t, :]).then_inc(stats_done, 1)
                        gate(dve, stats_done, at(i, h, NT, NT))
                        for t in range(NT):
                            dve.bn_aggr(moments[:, t, :], stats[:, t, :]).then_inc(moments_done, 1)
                        dve.wait_ge(moments_done, at(i, h, NT, NT))
                        dve.tensor_scalar(var_eps[:, :], moments[:, :, 1], LN_EPS, None, ALU.add).then_inc(var_done, 1)
                        dve.wait_ge(pow_done, at(i, h, 2, 2))
                        for t in range(NT):
                            dve.tensor_scalar(xa[h][:, t, :], xa[h][:, t, :], moments[:, t, 0:1], rstd[:, t:t + 1],
                                              ALU.subtract, ALU.mult).then_inc(normed, 1)
                        link(dve.scalar_tensor_tensor(out=norm[:, :], in0=std[:, :], scalar=SQRT_D, in1=rstd[:, :],
                                                      op0=ALU.mult, op1=ALU.mult))
                        link(dve.tensor_scalar(norm[:, :], norm[:, :], NORM_EPS, None, ALU.max))
                        link(dve.reciprocal(rnorm[:, :], norm[:, :]))
                        dve.wait_ge(cos_done, at(i, h, NT, NT + 2))
                        wide = [P, NT, K]
                        link(dve.tensor_tensor(cosines[:, :, :], cos_ps[:, 0:KT].rearrange("p (t k) -> p t k", k=K),
                                               rnorm[:, :].unsqueeze(2).to_broadcast(wide), ALU.mult))
                        link(dve.tensor_reduce(best[:, :], cosines[:, :, :], AX, ALU.max))
                        link(dve.tensor_tensor(is_best[:, :, :], cosines[:, :, :],
                                               best[:, :].unsqueeze(2).to_broadcast(wide), ALU.is_equal))
                        link(dve.scalar_tensor_tensor(out=candidate[:, :, :], in0=is_best[:, :, :], scalar=-float(K),
                                                      in1=cluster_ids[:, :, :], op0=ALU.mult, op1=ALU.add))
                        link(dve.tensor_reduce(cluster[:, :], candidate[:, :, :], AX, ALU.min))
                        mine = cluster[:, :].unsqueeze(2).to_broadcast(wide)
                        dve.tensor_tensor(onehot[:, :, :].rearrange("p k t -> p t k"), cluster_ids_m[:, :, :], mine,
                                          ALU.is_equal).then_inc(onehots, 1)
                        dve.tensor_tensor(below[:, :, :], cluster_ids_m[:, :, :], mine, ALU.is_gt).then_inc(onehots, 1)
                        dve.tensor_tensor(upto[:, :, :], cluster_ids_m[:, :, :], mine, ALU.is_ge).then_inc(onehots, 1)
                        dve.wait_ge(counted, at(i, h, 1, 1))
                        link(dve.tensor_copy(totals[:, :], count_ps[:, KT:2 * KT]))
                        link(dve.tensor_tensor_scan(running[:, :], totals[:, :], zeros[:, :], 0.0, ALU.add, ALU.add))
                        link(dve.tensor_tensor(before[:, :], running[:, :], totals[:, :], ALU.subtract))
                        link(dve.tensor_tensor(place[:, :], before[:, :], count_ps[:, 0:KT], ALU.add))
                        link(dve.tensor_tensor(chosen[:, :], place[:, :],
                                               onehot[:, :, :].rearrange("p k t -> p (k t)"), ALU.mult))
                        link(dve.tensor_reduce(place_in_seq[:, :], chosen[:, :].rearrange("p (k t) -> p t k", t=NT),
                                               AX, ALU.add))
                        col = (i * 2 + h) * NT
                        dve.tensor_scalar(positions[:, bass.ds(col, NT)], place_in_seq[:, :], first_row[:, :], None,
                                          ALU.add)
                        dve.tensor_scalar(bounds[:, bass.ds((i * 2 + h) * 2, 2)], count_ps[0:K, 2 * KT:2 * KT + 2],
                                          0.0, None, ALU.add)
                        dve.tensor_scalar(target[h][:, :], place_in_seq[:, :], first_row[:, :], None,
                                          ALU.add).then_inc(targets, 1)
                        dve.wait_ge(targets, at(i, h, 1, 1))
                        link(dve.tensor_scalar(first_row[:, :], first_row[:, :], float(L), None, ALU.add))
                        assert links[0] == LINKS, links[0]


        with ExitStack() as c:
            ITEMS = NS * ND
            raw = sb("raw", [P, NT, D], c=c)
            acc = [sb(f"acc{n}", [P, NT, D], c=c) for n in range(2)]
            feat = [sb(f"feat{n}", [P, ND, L], c=c) for n in range(2)]
            delta = [sb(f"delta{n}", [P, ND, L], c=c) for n in range(2)]
            decay = [sb(f"decay{n}", [P, L], c=c) for n in range(2)]
            drive = [sb(f"drive{n}", [P, L], c=c) for n in range(4)]
            states = [sb(f"states{n}", [P, L], c=c) for n in range(2 * ND)]
            b_rows = [sb(f"b_rows{n}", [P, L], c=c) for n in range(2)]
            proj = sb("proj", [P, L], c=c)
            b_parts = [sb(f"b_parts{n}", [P, L], BF16, c=c) for n in range(2)]
            c_cols = [sb(f"c_cols{n}", [P, NT, NS], c=c) for n in range(2)]
            places = sb("places", [K, L], c=c)
            bound = sb("bound", [K, 2], c=c)
            wx = sb("wx", [P, ND, P], c=c)
            wc = sb("wc", [P, ND, NS], c=c)
            wdt = sb("wdt", [P, D], c=c)
            bias = sb("bias", [P, ND], c=c)
            a_neg = sb("a_neg", [P, ND, NS], c=c)
            d_row = sb("d_row", [P, D], c=c)
            select = sb("select", [P, NS, P], BF16, c=c)
            pieces = sb("pieces", [P, 2, 512], c=c)
            soft = [pieces[:, n, :] for n in range(2)]
            in_cluster = pieces[0:K, :, :].rearrange("k m q -> k (m q)")
            stats = sb("y_stats", [P, NT, 6], c=c)
            moments = sb("y_moments", [P, NT, 2], c=c)
            var_eps = sb("y_var_eps", [P, NT], c=c)
            rstd = sb("y_rstd", [P, NT], c=c)

            wloads = sem("scan_weights", c)
            made = sem("scan_consts", c)
            a_made = sem("scan_a", c)
            loaded = sem("scan_loaded", c)
            stored = [sem(f"scan_stored{n}", c) for n in range(2)]
            turned = sem("scan_turned", c)
            turned_out = sem("scan_turned_out", c)
            in_cluster_done = sem("scan_in_cluster", c)
            split = sem("scan_split", c)
            softs = sem("scan_softs", c)
            soft_steps = sem("scan_soft_steps", c)
            deltas = sem("scan_deltas", c)
            driven = sem("scan_feat_times_delta", c)
            skipped = sem("scan_skip", c)
            b_spread = sem("scan_b_spread", c)
            b_ready = sem("scan_b_ready", c)
            decays = sem("scan_decays", c)
            drives = sem("scan_drives", c)
            scans = sem("scan_scans", c)
            states_turned = sem("scan_states_turned", c)
            added = sem("scan_added", c)
            stats_done = sem("scan_stats", c)
            moments_done = sem("scan_moments", c)
            var_done = sem("scan_var", c)
            pow_done = sem("scan_pow", c)
            normed = sem("scan_normed", c)
            chain = sem("scan_chain", c)
            turn = bank[0:2]
            b_ps = bank[2:4]
            state_ps = bank[4:8]
            BANKS = len(state_ps)
            HALVES = 2 * ND
            T_PROJ, T_C, T_DELTA = NT, NT + 2, NT + 4
            TURNS = NT + 4 + HALVES
            STEPS = [[0, 1], [2, 3], [4, 5], [6, 7], [T_PROJ], [T_PROJ + 1], [T_C, T_C + 1], [T_DELTA, T_DELTA + 1]]\
                + [[T_DELTA + g] for g in range(2, HALVES)]
            NORMALISE_STATE, SPLIT_STATE, SKIP_STATE = 4, 8, 5
            POWER_STATE = 2
            ACT_LAG = 2
            assert len(STEPS) + ACT_LAG <= NS
            block = c.enter_context(nc.Block())

            def all_sequences(eng, main):
                main(0, 0, True, False)
                main(0, 1, False, False)
                with eng.Fori(1, PAIRS - 1) as i:
                    for h in range(2):
                        main(i, h, False, False)
                main(PAIRS - 1, 0, False, False)
                main(PAIRS - 1, 1, False, True)

            @block.sync
            def _(sp):
                for dst, src in (
                    (wx[:, :, :], w_x.rearrange("(c p) m -> p c m", p=P)),
                    (wc[:, :, :], w_c.rearrange("(c p) m -> p c m", p=P)),
                    (wdt[DT_ROW:DT_ROW + R, :], w_dt_t),
                    (bias[:, :], dt_bias.rearrange("(c p) -> p c", p=P)),
                    (a_neg[:, :, :], a_logs.rearrange("(c p) n -> p c n", p=P)),
                    (d_row[:, :], ds.partition_broadcast(P)),
                ):
                    sp.dma_start(dst, src, allow_slow_non_contiguous=True).then_inc(wloads, 16)
                def main(i, h, first, last):
                    seq = i * 2 + h
                    if not last:
                        sp.wait_ge(skipped, at(i, h, 1, 1))
                        sp.dma_start(raw[:, :, :], row(xs_rows, i * 2 + (h + 1))).then_inc(loaded, 16)
                    if not first:
                        store(i, h, i * 2 + (h - 1))
                    if last:
                        store(i, h + 1, seq)

                def store(i, h, seq):
                    sp.wait_ge(normed, at(i, h, NT, 0))
                    sp.dma_start(row(ys_rows, seq), acc[(h + 1) % 2][:, :, :]).then_inc(stored[(h + 1) % 2], 16)

                sp.dma_start(raw[:, :, :], row(xs_rows, 0)).then_inc(loaded, 16)
                all_sequences(sp, main)
                for h in range(2):
                    sp.wait_ge(stored[h], 16 * PAIRS)

            @block.gpsimd
            def _(pool):
                pool.memset(select[:, :, :], 0.0).then_inc(made, 1)
                pool.memset(b_parts[0][:, :], 0.0).then_inc(made, 1)
                pool.memset(b_parts[1][:, :], 0.0).then_inc(made, 1)
                pool.iota(states[0][0:K, :].bitcast(I32), pattern=[[1, L]], base=0, channel_multiplier=0).then_inc(made, 1)
                pool.wait_ge(made, 4)
                pool.tensor_copy(places[:, :], states[0][0:K, :].bitcast(I32)).then_inc(made, 1)
                for part in range(3):
                    pool.affine_select(out=select[:, :, :], in_=select[:, :, :], compare_op=ALU.not_equal, fill=1.0,
                                       base=-32 * part, pattern=[[-1, NS], [0, P]],
                                       channel_multiplier=1).then_inc(made, 1)
                    pool.wait_ge(made, 6 + part)
                pool.sem_inc(drives, 2 * ND)

                def power(i, h):
                    pool.wait_ge(var_done, at(i, h, 1, 0))
                    pool.tensor_tensor(rstd[:, :], var_eps[:, :], neg_half[:, :], ALU.pow).then_inc(pow_done, 1)

                def main(i, h, first, last):
                    for n in range(NS):
                        pool.wait_ge(b_ready, at(i, h, NS, n + 2))
                        for c_ in range(ND):
                            g = n * ND + c_
                            if n == 0:
                                pool.wait_ge(driven, at(i, h, ND, c_ + 1))
                            pool.wait_ge(scans, at(i, h, ITEMS, g + 1))
                            pool.tensor_tensor(drive[g % 4][:, :], feat[h][:, c_, :], b_rows[n % 2][:, :],
                                               ALU.mult).then_inc(drives, 1)
                        if n == POWER_STATE and not first:
                            power(i, h)
                    if last:
                        power(i, h + 1)

                all_sequences(pool, main)

            @block.scalar
            def _(act):
                act.preload_act_table_set("natural_log_exp_and_others")
                act.wait_ge(wloads, 96)
                flat_a = a_neg[:, :, :].rearrange("p c n -> p (c n)")
                act.activation(flat_a, flat_a, ACT.Exp).then_inc(a_made, 1)
                act.wait_ge(a_made, 1)
                act.activation(flat_a, flat_a, ACT.Copy, scale=-1.0).then_inc(a_made, 1)
                act.wait_ge(a_made, 2)
                act.sem_inc(turned_out, 2)
                act.sem_inc(b_ready, 1)

                def spread(i, h, n):
                    act.wait_ge(b_spread, at(i, h, NS, n + 1))
                    act.wait_ge(drives, at(i, h, ITEMS, ND * (n + 1)))
                    for m in range(2):
                        last = act.activation(b_rows[n % 2][:, m * 512:(m + 1) * 512], b_ps[m][:, :], ACT.Copy)
                    last.then_inc(b_ready, 1)

                def item(i, h, k):
                    ps = turn[k % 2]
                    act.wait_ge(turned, at(i, h, TURNS, k + 1))
                    if k < T_PROJ:
                        act.activation(feat[h % 2][:, :, k * P:(k + 1) * P],
                                       ps[:, :].rearrange("p (c q) -> p c q", c=ND), ACT.Copy).then_inc(turned_out, 1)
                    elif k < T_C:
                        m = k - T_PROJ
                        act.activation(proj[:, m * 512:(m + 1) * 512], ps[:, :], ACT.Copy).then_inc(turned_out, 1)
                    elif k < T_DELTA:
                        m = (k - T_C) * (NT // 2)
                        act.activation(c_cols[h % 2][:, m:m + NT // 2, :].rearrange("p t n -> p (t n)"),
                                       ps[:, 0:NT // 2 * NS], ACT.Copy).then_inc(turned_out, 1)
                    else:
                        g = k - T_DELTA
                        c_, m = g // 2, g % 2
                        act.wait_ge(deltas, at(i, h, HALVES, g + 1))
                        act.activation(soft[g % 2], ps[:, :], ACT.Abs,
                                       bias=bias[:, c_:c_ + 1]).then_inc(soft_steps, 1)
                        act.activation(delta[h % 2][:, c_, m * 512:(m + 1) * 512], ps[:, :], ACT.Relu,
                                       bias=bias[:, c_:c_ + 1]).then_inc(turned_out, 1)
                        act.wait_ge(soft_steps, at(i, h, 2 * HALVES, 2 * g + 1))
                        act.activation(soft[g % 2], soft[g % 2], ACT.Exp, scale=-1.0).then_inc(soft_steps, 1)
                        act.wait_ge(soft_steps, at(i, h, 2 * HALVES, 2 * g + 2))
                        act.activation(soft[g % 2], soft[g % 2], ACT.Ln, bias=one_bias[:, :])\
                           .then_inc(softs, 1)

                def main(i, h, first, last):
                    for n in range(NS):
                        for c_ in range(ND):
                            g = n * ND + c_
                            if n == 0:
                                act.wait_ge(deltas, at(i, h, HALVES, 2 * c_ + 2) + 2)
                            act.wait_ge(scans, at(i, h, ITEMS, g + 3))
                            act.activation(decay[g % 2][:, :], delta[h][:, c_, :], ACT.Exp,
                                           scale=a_neg[:, c_, n:n + 1]).then_inc(decays, 1)
                            if c_ == 1 and (n + 1 < NS or not last):
                                spread(i, h, n + 1)
                            if c_ == 1 and not last and 0 <= n - ACT_LAG < len(STEPS):
                                for k in STEPS[n - ACT_LAG]:
                                    item(i, h + 1, k)

                for k in range(TURNS):
                    item(0, 0, k)
                spread(0, 0, 0)
                all_sequences(act, main)

            @block.tensor
            def _(pe):
                pe.wait_ge(made, 8)
                pe.wait_ge(wloads, 96)
                pe.sem_inc(states_turned, 2 * NT)

                def spread(i, h, n):
                    pe.wait_ge(b_ready, at(i, h, NS, n + 1))
                    if n % NS == 0:
                        pe.wait_ge(split, at(i, h + n // NS, 5, 5))
                    for m in range(2):
                        last = pe.matmul(b_ps[m][:, :], select[:, n % NS, :],
                                         b_parts[(h + n // NS) % 2][:, m * 512:(m + 1) * 512], start=True, stop=True)
                    last.then_inc(b_spread, 1)

                def item(i, h, k):
                    ps = turn[k % 2]
                    if k == 0:
                        pe.wait_ge(loaded, at(i, h, 16, 16))
                    pe.wait_ge(turned_out, at(i, h, TURNS, k + 1))
                    if k < T_PROJ:
                        for c_ in range(ND):
                            last = pe.transpose(ps[:, c_ * P:(c_ + 1) * P], raw[:, k, c_ * P:(c_ + 1) * P], ident[:, :])
                    elif k < T_C:
                        m = k - T_PROJ
                        pe.wait_ge(turned_out, at(i, h, TURNS, T_PROJ) + 2)
                        for c_ in range(ND):
                            last = pe.matmul(ps[:, :], wx[:, c_, :], feat[h % 2][:, c_, m * 512:(m + 1) * 512],
                                             start=(c_ == 0), stop=(c_ == ND - 1))
                    elif k < T_DELTA:
                        pe.wait_ge(in_cluster_done, at(i, h, 1, 1))
                        for q in range(NT // 2):
                            t = (k - T_C) * (NT // 2) + q
                            for c_ in range(ND):
                                pe.matmul(ps[:, q * NS:(q + 1) * NS], feat[h % 2][:, c_, t * P:(t + 1) * P],
                                          wc[:, c_, :], start=(c_ == 0), stop=False)
                            last = pe.matmul(ps[:, q * NS:(q + 1) * NS], in_cluster[:, t * P:(t + 1) * P],
                                             cluster_c[:, :], start=False, stop=True)
                    else:
                        g = k - T_DELTA
                        c_, m = g // 2, g % 2
                        pe.wait_ge(turned_out, at(i, h, TURNS, T_C) + 2)
                        last = pe.matmul(ps[:, :], wdt[DT_ROW:DT_ROW + R, c_ * P:(c_ + 1) * P],
                                         proj[DT_ROW:DT_ROW + R, m * 512:(m + 1) * 512], start=True, stop=True)
                    last.then_inc(turned, 1)

                def main(i, h, first, last):
                    for n in range(NS):
                        pe.wait_ge(scans, at(i, h, ITEMS, ND * (n + 1) + 4))
                        for t in range(NT):
                            pe.wait_ge(added, at(i, h, NS * NT, n * NT + t + 1))
                            for c_ in range(ND):
                                end = pe.transpose(state_ps[t % BANKS][:, c_ * P:(c_ + 1) * P],
                                                   states[(n % 2) * ND + c_][:, t * P:(t + 1) * P], ident[:, :])
                            end.then_inc(states_turned, 1)
                            if t == BANKS - 1:
                                if n + 2 < NS or not last:
                                    spread(i, h, n + 2)
                        if not last and n < len(STEPS):
                            for k in STEPS[n]:
                                item(i, h + 1, k)

                for k in range(TURNS):
                    item(0, 0, k)
                for n in range(2):
                    spread(0, 0, n)
                all_sequences(pe, main)

            @block.vector
            def _(dve):
                dve.wait_ge(made, 8)
                dve.wait_ge(wloads, 96)
                dve.sem_inc(deltas, 2)
                dve.sem_inc(scans, 4)
                dve.sem_inc(added, BANKS)

                def clusters(i, h):
                    dve.tensor_scalar(bound[:, :], bounds[:, bass.ds((i * 2 + h) * 2, 2)], 0.0, None,
                                      ALU.add).then_inc(chain, 1)
                    dve.wait_ge(chain, at(i, h, 2, 1))
                    dve.tensor_scalar(in_cluster, places[:, :], bound[:, 0:1], None, ALU.is_ge).then_inc(chain, 1)
                    dve.wait_ge(chain, at(i, h, 2, 2))
                    dve.scalar_tensor_tensor(out=in_cluster, in0=places[:, :], scalar=bound[:, 1:2],
                                             in1=in_cluster, op0=ALU.is_lt, op1=ALU.mult)\
                       .then_inc(in_cluster_done, 1)

                def split_b(i, h):
                    parts = b_parts[h % 2]
                    dve.wait_ge(turned_out, at(i, h, TURNS, T_C) + 2)
                    dve.tensor_copy(parts[0:96, :], proj[0:96, :]).then_inc(split, 1)
                    for n, rows in ((1, 64), (3, 32)):
                        dve.wait_ge(split, at(i, h, 5, n))
                        dve.tensor_tensor(proj[0:rows, :], proj[0:rows, :], parts[0:rows, :], ALU.subtract)\
                           .then_inc(split, 1)
                        dve.wait_ge(split, at(i, h, 5, n + 1))
                        dve.tensor_copy(parts[0:rows, :], proj[0:rows, :]).then_inc(split, 1)

                def step_size(i, h, g):
                    c_, m = g // 2, g % 2
                    dve.wait_ge(softs, at(i, h, HALVES, g + 1))
                    piece = delta[h % 2][:, c_, m * 512:(m + 1) * 512]
                    dve.tensor_tensor(piece, piece, soft[g % 2], ALU.add).then_inc(deltas, 1)
                    if m:
                        dve.wait_ge(turned, at(i, h, TURNS, T_DELTA))
                        dve.wait_ge(deltas, at(i, h, HALVES, g + 1) + 2)
                        dve.tensor_tensor(feat[h % 2][:, c_, :], feat[h % 2][:, c_, :], delta[h % 2][:, c_, :],
                                          ALU.mult).then_inc(driven, 1)

                def skip(i, h, wait_stored):
                    dve.wait_ge(turned, at(i, h, TURNS, T_PROJ))
                    if wait_stored:
                        dve.wait_ge(stored[h % 2], i * 16 + 16 * (h // 2))
                    dve.tensor_tensor(acc[h % 2][:, :, :], raw[:, :, :],
                                      d_row[:, :].unsqueeze(1).to_broadcast([P, NT, D]), ALU.mult).then_inc(skipped, 1)

                def scan(i, h, n, c_):
                    g = n * ND + c_
                    if c_ == 0:
                        dve.wait_ge(states_turned, at(i, h, NS * NT, (n + 1) * NT))
                    dve.wait_ge(decays, at(i, h, ITEMS, g + 1))
                    dve.wait_ge(drives, at(i, h, ITEMS, g + 1 + 2 * ND))
                    dve.tensor_tensor_scan(states[(n % 2) * ND + c_][:, :], decay[g % 2][:, :],
                                           drive[g % 4][:, :], 0.0, ALU.mult, ALU.add).then_inc(scans, 1)

                def add(i, h, n, c_):
                    if c_ == 0:
                        if n == 0:
                            dve.wait_ge(skipped, at(i, h, 1, 1))
                        else:
                            dve.wait_ge(added, at(i, h, NS * NT, n * NT + BANKS))
                    for t in range(c_ * NT // ND, (c_ + 1) * NT // ND):
                        dve.wait_ge(states_turned, at(i, h, NS * NT, n * NT + t + 1 + 2 * NT))
                        dve.scalar_tensor_tensor(out=acc[h % 2][:, t, :], in0=state_ps[t % BANKS][:, :],
                                                 scalar=c_cols[h % 2][:, t, n:n + 1], in1=acc[h % 2][:, t, :],
                                                 op0=ALU.mult, op1=ALU.add).then_inc(added, 1)

                def norm_stats(i, h):
                    mine = acc[(h + 1) % 2]
                    dve.wait_ge(added, at(i, h, NS * NT, BANKS))
                    for t in range(NT):
                        dve.bn_stats(stats[:, t, :], mine[:, t, :]).then_inc(stats_done, 1)
                    gate(dve, stats_done, at(i, h, NT, 0))
                    for t in range(NT):
                        dve.bn_aggr(moments[:, t, :], stats[:, t, :]).then_inc(moments_done, 1)
                    dve.wait_ge(moments_done, at(i, h, NT, 0))
                    dve.tensor_scalar(var_eps[:, :], moments[:, :, 1], LN_EPS, None, ALU.add).then_inc(var_done, 1)

                def normalise(i, h):
                    mine = acc[(h + 1) % 2]
                    dve.wait_ge(pow_done, at(i, h, 1, 0))
                    for t in range(NT):
                        dve.tensor_scalar(mine[:, t, :], mine[:, t, :], moments[:, t, 0:1], rstd[:, t:t + 1],
                                          ALU.subtract, ALU.mult).then_inc(normed, 1)

                def main(i, h, first, last):
                    for c_ in range(ND):
                        scan(i, h, 0, c_)
                        if not first:
                            add(i, h - 1, NS - 1, c_)
                    if not first:
                        norm_stats(i, h)
                    for n in range(1, NS):
                        for c_ in range(ND):
                            scan(i, h, n, c_)
                            add(i, h, n - 1, c_)
                        if n == NORMALISE_STATE and not first:
                            normalise(i, h)
                        if not last:
                            if n == 2:
                                clusters(i, h + 1)
                            if n == SPLIT_STATE:
                                split_b(i, h + 1)
                            k = n - ACT_LAG
                            if 0 <= k < len(STEPS) and STEPS[k][0] >= T_DELTA:
                                for item in STEPS[k]:
                                    step_size(i, h + 1, item - T_DELTA)
                            if n == SKIP_STATE:
                                skip(i, h + 1, not first)
                    if last:
                        for c_ in range(ND):
                            add(i, h, NS - 1, c_)
                        norm_stats(i, h + 1)
                        normalise(i, h + 1)

                clusters(0, 0)
                skip(0, 0, False)
                split_b(0, 0)
                for g in range(HALVES):
                    step_size(0, 0, g)
                all_sequences(dve, main)

        with ExitStack() as c:
            xr = [sb(f"xr{n}", [P, NT, D], c=c) for n in range(2)]
            both = [sb(f"both{n}", [P, NT, 2 * D], c=c) for n in range(2)]
            normed_x = sb("normed_x", [P, NT, D], c=c)
            xt = [sb(f"xt_l{n}", [P, ND, 512], c=c) for n in range(2)]
            hidden = [sb(f"hidden{n}", [P, FL, 512], c=c) for n in range(2)]
            w1 = sb("l_w1_sb", [P, ND, FL * P], c=c)
            w2 = sb("l_w2_sb", [P, FL, D], c=c)
            gamma = sb("l_gamma_sb", [P, ND], c=c)
            b1 = sb("l_b1_sb", [P, FL], c=c)
            b2 = sb("l_b2_sb", [P, D], c=c)
            route = sb("route_sb", [P, ND], c=c)
            stats = sb("x1_stats", [P, NT, 6], c=c)
            moments = sb("x1_moments", [P, NT, 2], c=c)
            var_eps = sb("x1_var_eps", [P, NT], c=c)
            rstd = sb("x1_rstd", [P, NT], c=c)
            std = sb("x1_std", [P, NT], c=c)
            norm = sb("x1_norm", [P, NT], c=c)
            rnorm = sb("x1_rnorm", [P, NT], c=c)
            scale = sb("x1_scale", [P, NT], c=c)
            o_stats = sb("lo_stats", [P, NT, 6], c=c)
            o_moments = sb("lo_moments", [P, NT, 2], c=c)
            o_var_eps = sb("lo_var_eps", [P, NT], c=c)
            o_rstd = sb("lo_rstd", [P, NT], c=c)
            index = [sb(f"index{n}", [P, NT], U32, c=c) for n in range(2)]

            wloads = sem("light_weights", c)
            folded = sem("light_gamma_folded", c)
            loaded = [sem(f"light_loaded{n}", c) for n in range(2)]
            gathered = [sem(f"light_gathered{n}", c) for n in range(2)]
            kept = [sem(f"light_kept{n}", c) for n in range(2)]
            written = [sem(f"light_written{n}", c) for n in range(2)]
            indexed = sem("light_indexed", c)
            summed = sem("light_summed", c)
            stats_done = sem("light_stats", c)
            moments_done = sem("light_moments", c)
            var_done = sem("light_var", c)
            pow_done = sem("light_pow", c)
            scaled = sem("light_scaled", c)
            normed = sem("light_normed", c)
            turned = sem("light_turned", c)
            turned_sb = sem("light_turned_sb", c)
            hidden_ps = sem("light_hidden_ps", c)
            hidden_sb = sem("light_hidden_sb", c)
            scored = sem("light_scored", c)
            light_ps = sem("light_out_ps", c)
            light_sb = sem("light_out_sb", c)
            light_n = sem("light_out_normed", c)
            out_ready = sem("light_out_ready", c)
            chain = sem("light_chain", c)
            turn = bank[0:2]
            hid = bank[2:4]
            lout = bank[4:6]
            score_ps = bank[6]
            G = NT // 4
            block = c.enter_context(nc.Block())

            @block.sync
            def _(sp):
                for dst, src in (
                    (w1[:, :, :], l_w1.rearrange("(c p) f -> p c f", p=P)),
                    (w2[:, :, :], l_w2.rearrange("(c p) f -> p c f", p=P)),
                    (gamma[:, :], l_gamma.rearrange("(c p) -> p c", p=P)),
                    (b1[:, :], l_b1.rearrange("(c p) -> p c", p=P)),
                    (b2[:, :], l_b2.partition_broadcast(P)),
                    (route[:, :], routing.rearrange("(c p) -> p c", p=P)),
                ):
                    sp.dma_start(dst, src, allow_slow_non_contiguous=True).then_inc(wloads, 16)
                for n in range(2):
                    sp.dma_start(xr[n][:, :, :], row(x_rows, n)).then_inc(loaded[n], 16)

                def store(i, h, seq):
                    sp.wait_ge(light_sb, at(i, h, NT, NT) + 2)
                    sp.dma_start(row(xl_rows, seq), both[h][:, :, :]).then_inc(kept[h], 16)
                    sp.wait_ge(out_ready, at(i, h, NT, NT))
                    sp.dma_start(row(out_rows, seq), xr[h][:, :, :]).then_inc(written[h], 16)

                with sp.Fori(0, PAIRS - 1) as i:
                    for h in range(2):
                        store(i, h, i * 2 + h)
                        sp.wait_ge(written[h], i * 16 + 16)
                        sp.dma_start(xr[h][:, :, :], row(x_rows, i * 2 + (2 + h))).then_inc(loaded[h], 16)
                for h in range(2):
                    store(PAIRS - 1, h, B - 2 + h)
                for h in range(2):
                    sp.wait_ge(written[h], 16 * PAIRS)
                    sp.wait_ge(kept[h], 16 * PAIRS)

            @block.gpsimd
            def _(pool):
                def gather(h):
                    for t in range(NT):
                        pool.indirect_dma_start(both[h][:, t, 0:D], None, ys_dram,
                                                bass.IndirectOffsetOnAxis(index[h][:, t:t + 1], 0))\
                            .then_inc(gathered[h], 16)

                def powers(i, h):
                    pool.wait_ge(var_done, at(i, h, 2, 1))
                    pool.tensor_tensor(rstd[:, :], var_eps[:, :], neg_half[:, :], ALU.pow).then_inc(pow_done, 1)
                    pool.tensor_tensor(std[:, :], moments[:, :, 1], half[:, :], ALU.pow).then_inc(pow_done, 1)
                    pool.wait_ge(var_done, at(i, h, 2, 2))
                    pool.tensor_tensor(o_rstd[:, :], o_var_eps[:, :], neg_half[:, :], ALU.pow).then_inc(pow_done, 1)

                for n in range(2):
                    pool.wait_ge(indexed, n + 1)
                    gather(n)
                with pool.Fori(0, PAIRS - 1) as i:
                    for h in range(2):
                        powers(i, h)
                        pool.wait_ge(indexed, at(i, h, 1, 3))
                        pool.wait_ge(out_ready, at(i, h, NT, NT))
                        gate(pool, kept[h], i * 16 + 16)
                        gather(h)
                for h in range(2):
                    powers(PAIRS - 1, h)

            @block.scalar
            def _(act):
                act.sem_inc(turned_sb, 2)
                act.sem_inc(hidden_sb, 2)
                act.wait_ge(wloads, 96)
                with act.Fori(0, PAIRS) as i:
                    for h in range(2):
                        for g in range(G):
                            for q in range(4):
                                t = 4 * g + q
                                act.wait_ge(turned, at(i, h, NT, t + 1))
                                if q == 0:
                                    act.wait_ge(scored, at(i, h, G, g + 1))
                                act.activation(xt[g % 2][:, :, q * P:(q + 1) * P],
                                               turn[t % 2][:, :].rearrange("p (c q) -> p c q", c=ND),
                                               ACT.Copy).then_inc(turned_sb, 1)
                            for f in range(FL):
                                act.wait_ge(hidden_ps, at(i, h, G * FL, g * FL + f + 1))
                                if f == 0:
                                    act.wait_ge(light_ps, at(i, h, NT, 4 * g + 4))
                                act.activation(hidden[g % 2][:, f, :], hid[f % 2][:, :], ACT.Gelu,
                                               bias=b1[:, f:f + 1]).then_inc(hidden_sb, 1)

            @block.tensor
            def _(pe):
                pe.sem_inc(scored, 2)
                pe.sem_inc(light_ps, 8)
                pe.wait_ge(folded, ND)
                with pe.Fori(0, PAIRS) as i:
                    for h in range(2):
                        for g in range(G):
                            for t in range(4 * g, 4 * g + 4):
                                pe.wait_ge(normed, at(i, h, NT, t + 1))
                                pe.wait_ge(turned_sb, at(i, h, NT, t + 1))
                                for c_ in range(ND):
                                    last = pe.transpose(turn[t % 2][:, c_ * P:(c_ + 1) * P],
                                                        normed_x[:, t, c_ * P:(c_ + 1) * P], ident[:, :])
                                last.then_inc(turned, 1)
                            pe.wait_ge(turned_sb, at(i, h, NT, 4 * g + 4) + 2)
                            for f in range(FL):
                                pe.wait_ge(hidden_sb, at(i, h, G * FL, g * FL + f + 1))
                                for c_ in range(ND):
                                    last = pe.matmul(hid[f % 2][:, :], w1[:, c_, f * P:(f + 1) * P],
                                                     xt[g % 2][:, c_, :], start=(c_ == 0), stop=(c_ == ND - 1))
                                last.then_inc(hidden_ps, 1)
                            for t in range(4 * g, 4 * g + 4):
                                q = t % 4
                                for c_ in range(ND):
                                    last = pe.matmul(score_ps[:, t:t + 1], xt[g % 2][:, c_, q * P:(q + 1) * P],
                                                     route[:, c_:c_ + 1], start=(c_ == 0), stop=(c_ == ND - 1))
                            last.then_inc(scored, 1)
                            pe.wait_ge(hidden_sb, at(i, h, G * FL, g * FL + FL) + 2)
                            for t in range(4 * g, 4 * g + 4):
                                q = t % 4
                                pe.wait_ge(light_sb, at(i, h, NT, t + 1))
                                for f in range(FL):
                                    last = pe.matmul(lout[t % 2][:, :], hidden[g % 2][:, f, q * P:(q + 1) * P],
                                                     w2[:, f, :], start=(f == 0), stop=(f == FL - 1))
                                last.then_inc(light_ps, 1)

            @block.vector
            def _(dve):
                LINKS = 3
                dve.sem_inc(light_sb, 2)
                dve.wait_ge(wloads, 96)
                for c_ in range(ND):
                    dve.tensor_scalar(w1[:, c_, :], w1[:, c_, :], gamma[:, c_:c_ + 1], None, ALU.mult)\
                       .then_inc(folded, 1)
                for n in range(2):
                    dve.tensor_scalar(index[n][:, :], positions[:, n * NT:(n + 1) * NT], 0.0, None,
                                      ALU.add).then_inc(indexed, 1)
                with dve.Fori(0, PAIRS) as i:
                    for h in range(2):
                        links = [0]

                        def link(ins):
                            links[0] += 1
                            ins.then_inc(chain, 1)
                            dve.wait_ge(chain, at(i, h, LINKS, links[0]))

                        dve.wait_ge(loaded[h], i * 16 + 16)
                        dve.wait_ge(gathered[h], i * (16 * NT) + 16 * NT)
                        for t in range(NT):
                            dve.tensor_tensor(both[h][:, t, 0:D], both[h][:, t, 0:D], xr[h][:, t, :],
                                              ALU.add).then_inc(summed, 1)
                        for t in range(NT):
                            gate(dve, summed, at(i, h, NT, t + 1))
                            dve.bn_stats(stats[:, t, :], both[h][:, t, 0:D]).then_inc(stats_done, 1)
                        gate(dve, stats_done, at(i, h, 2 * NT, NT))
                        for t in range(NT):
                            dve.bn_aggr(moments[:, t, :], stats[:, t, :]).then_inc(moments_done, 1)
                        dve.wait_ge(moments_done, at(i, h, 2 * NT, NT))
                        dve.tensor_scalar(var_eps[:, :], moments[:, :, 1], LN_EPS, None, ALU.add).then_inc(var_done, 1)
                        dve.wait_ge(pow_done, at(i, h, 3, 2))
                        link(dve.scalar_tensor_tensor(out=norm[:, :], in0=std[:, :], scalar=SQRT_D, in1=rstd[:, :],
                                                      op0=ALU.mult, op1=ALU.mult))
                        link(dve.tensor_scalar(norm[:, :], norm[:, :], NORM_EPS, 1.0 / SQRT_D, ALU.max, ALU.mult))
                        link(dve.reciprocal(rnorm[:, :], norm[:, :]))
                        dve.tensor_tensor(scale[:, :], rstd[:, :], rnorm[:, :], ALU.mult).then_inc(scaled, 1)
                        dve.wait_ge(scaled, at(i, h, 1, 1))
                        for t in range(NT):
                            dve.tensor_scalar(normed_x[:, t, :], both[h][:, t, 0:D], moments[:, t, 0:1],
                                              scale[:, t:t + 1], ALU.subtract, ALU.mult).then_inc(normed, 1)
                        for t in range(NT):
                            dve.wait_ge(light_ps, at(i, h, NT, t + 1) + 8)
                            dve.tensor_tensor(both[h][:, t, D:2 * D], lout[t % 2][:, :], b2[:, :], ALU.add)\
                               .then_inc(light_sb, 1)
                        for t in range(NT):
                            gate(dve, light_sb, at(i, h, NT, t + 1) + 2)
                            dve.bn_stats(o_stats[:, t, :], both[h][:, t, D:2 * D]).then_inc(stats_done, 1)
                        gate(dve, stats_done, at(i, h, 2 * NT, 2 * NT))
                        for t in range(NT):
                            dve.bn_aggr(o_moments[:, t, :], o_stats[:, t, :]).then_inc(moments_done, 1)
                        dve.wait_ge(moments_done, at(i, h, 2 * NT, 2 * NT))
                        dve.tensor_scalar(o_var_eps[:, :], o_moments[:, :, 1], LN_EPS, None, ALU.add)\
                           .then_inc(var_done, 1)
                        dve.wait_ge(scored, at(i, h, G, G) + 2)
                        dve.tensor_tensor(scores[:, bass.ds((i * 2 + h) * NT, NT)], score_ps[:, 0:NT], norm[:, :],
                                          ALU.mult)
                        dve.tensor_scalar(index[h][:, :], positions[:, bass.ds((i * 2 + (2 + h)) * NT, NT)], 0.0,
                                          None, ALU.add).then_inc(indexed, 1)
                        dve.wait_ge(pow_done, at(i, h, 3, 3))
                        for t in range(NT):
                            dve.tensor_scalar(xr[h][:, t, :], both[h][:, t, D:2 * D], o_moments[:, t, 0:1],
                                              o_rstd[:, t:t + 1], ALU.subtract, ALU.mult).then_inc(light_n, 1)
                        for t in range(NT):
                            dve.wait_ge(light_n, at(i, h, NT, t + 1))
                            dve.tensor_tensor(xr[h][:, t, :], xr[h][:, t, :], both[h][:, t, 0:D],
                                              ALU.add).then_inc(out_ready, 1)
                        assert links[0] == LINKS, links[0]

        listed = sb("listed", [P, (B + 2) * NJ], U32)
        weights = sb("weights", [P, B * NJ])
        with ExitStack() as c:
            same = sb("same", [P, NT * B], c=c)
            prior = sb("prior", [P, NT * B], c=c)
            s_rows = sb("s_rows", [P, P], c=c)
            clipped = sb("clipped", [P, P], c=c)
            expd = sb("expd", [P, P], c=c)
            top = sb("top", [P, 1], c=c)
            top_row = sb("top_row", [1, B, NT], c=c)
            top_seq = sb("top_seq", [1, B], c=c)
            top_all = sb("top_all", [P, 1], c=c)
            cap = sb("cap", [P, 1], c=c)
            shift = sb("shift", [P, 1], c=c)
            part = sb("part", [P, 1], c=c)
            log_sum = sb("log_sum", [P, 1], c=c)
            gap = sb("gap", [P, P], c=c)
            better = sb("better", [P, P], c=c)
            equal = sb("equal", [P, P], c=c)
            count = sb("count", [P, 2], c=c)
            bit = sb("bit", [P, 1], I32, c=c)
            trial = sb("trial", [P, 1], I32, c=c)
            keep = sb("keep", [P, 1], I32, c=c)
            limit = sb("limit", [P, 1], I32, c=c)
            zeros = sb("zeros_r", [P, P], c=c)
            run_eq = sb("run_eq", [P, P], c=c)
            room = sb("room", [P, 1], c=c)
            picked = sb("picked", [P, P], c=c)
            slot = sb("slot", [P, P], c=c)
            straight = sb("straight", [P, P], c=c)
            slot_t = sb("slot_t", [P, P], c=c)
            tagged = sb("tagged", [P, NT * B, 2], c=c)
            row_i = sb("row_i", [P, NT * B], I32, c=c)
            slots_i = sb("slots_i", [P, NUM_HEAVY], I32, c=c)
            slots = sb("slots", [P, NUM_HEAVY], c=c)
            takes = [sb(f"takes{n}", [P, NUM_HEAVY], c=c) for n in range(2 * NT)]

            made = sem("route_consts", c)
            chain = sem("route_chain", c)
            pe_done = sem("route_pe", c)
            shifted = sem("route_shifted", c)
            expds = sem("route_expds", c)
            sums = sem("route_sums", c)
            logs = sem("route_logs", c)
            caps = sem("route_caps", c)
            gaps = sem("route_gaps", c)
            score_exp = sem("route_score_exp", c)
            counts = sem("route_counts", c)
            totals = sem("route_totals", c)
            limits = sem("route_limits", c)
            bits = sem("route_bits", c)
            taken = sem("route_taken", c)
            lists = sem("route_lists", c)
            block = c.enter_context(nc.Block())

            @block.gpsimd
            def _(pool):
                pool.memset(same[:, :], 1.0).then_inc(made, 1)
                pool.memset(listed[:, B * NJ:(B + 2) * NJ], 0)
                pool.memset(zeros[:, :], 0.0).then_inc(made, 1)
                pool.memset(limit[:, :], 0).then_inc(made, 1)
                pool.memset(bit[:, :], 1 << 30).then_inc(made, 1)
                pool.memset(cap[:, :], -(LOG_K - math.log(L))).then_inc(made, 1)
                pool.iota(slots_i[:, :], pattern=[[1, NUM_HEAVY]], base=0, channel_multiplier=0).then_inc(made, 1)
                pool.iota(row_i[:, :], pattern=[[P, NT * B]], base=0, channel_multiplier=1).then_inc(made, 1)
                pool.wait_ge(made, 7)
                v = same[:, :].rearrange("p (b t) -> p b t", t=NT)
                pool.affine_select(out=v, in_=v, compare_op=ALU.is_ge, fill=0.0, base=0,
                                   pattern=[[-NT, B], [0, NT]], channel_multiplier=1).then_inc(made, 1)
                pool.wait_ge(made, 8)
                pool.affine_select(out=v, in_=v, compare_op=ALU.is_ge, fill=0.0, base=NT - 1,
                                   pattern=[[NT, B], [0, NT]], channel_multiplier=-1).then_inc(made, 1)
                pool.wait_ge(made, 9)
                pool.affine_select(out=prior[:, :], in_=same[:, :], compare_op=ALU.is_gt, fill=0.0, base=0,
                                   pattern=[[1, NT * B]], channel_multiplier=-1).then_inc(made, 1)
                pool.tensor_copy(slots[:, :], slots_i[:, :]).then_inc(made, 1)
                pool.tensor_copy(tagged[:, :, 0], row_i[:, :]).then_inc(made, 1)

            @block.scalar
            def _(act):
                act.preload_act_table_set("natural_log_exp_and_others")
                with act.Fori(0, DESCENT_STEPS - 1) as j:
                    act.wait_ge(shifted, j * 2 + 2)
                    act.activation(expd[:, :], clipped[:, :], ACT.Exp, bias=shift[:, :],
                                   accum_out=part[:, :]).then_inc(expds, 1)
                    act.wait_ge(sums, j + 1)
                    act.activation(log_sum[:, :], bank[1][:, 0:1], ACT.Ln).then_inc(logs, 1)
                act.wait_ge(gaps, 2)
                act.activation(expd[:, :], clipped[:, :], ACT.Exp).then_inc(score_exp, 1)

            @block.tensor
            def _(pe):
                pe.wait_ge(made, 12)
                pe.transpose(bank[0][:, 0:P], scores[:, :], ident[:, :]).then_inc(pe_done, 1)
                pe.wait_ge(chain, 2)
                pe.transpose(bank[0][0:1, 0:P], top[:, :], ident[:, :]).then_inc(pe_done, 1)
                pe.wait_ge(chain, 4)
                pe.matmul(bank[0][:, 0:1], top_row[:, :, :].rearrange("p b t -> p (b t)"), ones[0:1, 0:1],
                          start=True, stop=True).then_inc(pe_done, 1)
                with pe.Fori(0, DESCENT_STEPS - 1) as j:
                    pe.wait_ge(expds, j + 1)
                    pe.matmul(bank[1][:, 0:1], same[:, :], part[:, :], start=True, stop=True).then_inc(sums, 1)
                with pe.Fori(0, 31) as j:
                    pe.wait_ge(counts, j + 1)
                    pe.matmul(bank[2][:, 0:1], same[:, :], count[:, 0:1], start=True, stop=True).then_inc(totals, 1)
                pe.wait_ge(counts, 33)
                pe.matmul(bank[2][:, 2:3], same[:, :], count[:, 0:1], start=True, stop=True)
                pe.matmul(bank[2][:, 3:4], prior[:, :], count[:, 1:2], start=True, stop=True).then_inc(pe_done, 1)
                pe.wait_ge(counts, 34)
                pe.matmul(bank[2][:, 4:5], prior[:, :], count[:, 0:1], start=True, stop=True).then_inc(pe_done, 1)
                pe.wait_ge(caps, DESCENT_STEPS + 1)
                pe.transpose(bank[3][:, 0:P], slot[:, :], ident[:, :])
                pe.transpose(bank[3][:, P:2 * P], straight[:, :], ident[:, :]).then_inc(pe_done, 1)
                pe.wait_ge(caps, DESCENT_STEPS + 2)
                for b in range(B):
                    pe.wait_ge(taken, NT * (b + 1))
                    for j in range(NJ):
                        for t in range(NT):
                            last = pe.matmul(bank[4 + j][:, 2 * b:2 * b + 2],
                                             takes[(b % 2) * NT + t][:, j * P:(j + 1) * P],
                                             tagged[:, b * NT + t, :], start=(t == 0), stop=(t == NT - 1))
                    last.then_inc(lists, 1)

            @block.vector
            def _(dve):
                links = [0]

                def link(ins):
                    links[0] += 1
                    ins.then_inc(chain, 1)
                    dve.wait_ge(chain, links[0])

                dve.wait_ge(made, 12)
                dve.wait_ge(pe_done, 1)
                link(dve.tensor_copy(s_rows[:, :], bank[0][:, 0:P]))
                link(dve.tensor_reduce(top[:, :], s_rows[:, :], AX, ALU.max))
                dve.wait_ge(pe_done, 2)
                link(dve.tensor_reduce(top_seq[:, :], bank[0][0:1, 0:P].rearrange("p (b t) -> p b t", t=NT), AX, ALU.max))
                link(dve.tensor_scalar(top_row[:, :, :], top_seq[:, :].unsqueeze(2).to_broadcast([1, B, NT]), 0.0, None,
                                       ALU.add))
                dve.wait_ge(pe_done, 3)
                dve.tensor_copy(top_all[:, :], bank[0][:, 0:1]).then_inc(caps, 1)
                dve.wait_ge(caps, 1)
                with dve.Fori(0, DESCENT_STEPS - 1) as j:
                    dve.tensor_scalar(shift[:, :], top_all[:, :], cap[:, :], -1.0, ALU.min, ALU.mult).then_inc(shifted, 1)
                    dve.tensor_scalar(clipped[:, :], s_rows[:, :], cap[:, :], None, ALU.min).then_inc(shifted, 1)
                    dve.wait_ge(logs, j + 1)
                    dve.tensor_scalar(cap[:, :], log_sum[:, :], shift[:, :], LOG_K, ALU.subtract, ALU.subtract)\
                       .then_inc(caps, 1)
                    gate(dve, caps, j + 2)
                dve.tensor_scalar(clipped[:, :], s_rows[:, :], cap[:, :], 0.0, ALU.subtract, ALU.min).then_inc(gaps, 1)
                dve.wait_ge(gaps, 1)
                dve.tensor_scalar(gap[:, :], clipped[:, :], -1.0, 104.0, ALU.mult, ALU.min).then_inc(gaps, 1)
                dve.wait_ge(gaps, 2)
                with dve.Fori(0, 31) as j:
                    dve.tensor_tensor(trial[:, :], limit[:, :], bit[:, :], ALU.bitwise_or).then_inc(limits, 1)
                    dve.wait_ge(limits, j * 3 + 1)
                    dve.tensor_scalar(better[:, :], gap[:, :], trial[:, :].bitcast(F32), 0.0, ALU.is_lt, ALU.add,
                                      accum_out=count[:, 0:1]).then_inc(counts, 1)
                    dve.wait_ge(totals, j + 1)
                    dve.tensor_scalar(keep[:, :], bank[2][:, 0:1], float(NUM_HEAVY), -1.0, ALU.is_lt, ALU.mult)\
                       .then_inc(limits, 1)
                    dve.wait_ge(limits, j * 3 + 2)
                    dve.tensor_tensor(keep[:, :], keep[:, :], bit[:, :], ALU.bitwise_and).then_inc(limits, 1)
                    dve.wait_ge(limits, j * 3 + 3)
                    dve.tensor_tensor(limit[:, :], limit[:, :], keep[:, :], ALU.bitwise_or)
                    dve.tensor_scalar(bit[:, :], bit[:, :], 1, None, ALU.logical_shift_right).then_inc(bits, 1)
                    gate(dve, bits, j + 1)
                edge = limit[:, :].bitcast(F32)
                dve.tensor_scalar(better[:, :], gap[:, :], edge, 0.0, ALU.is_lt, ALU.add,
                                  accum_out=count[:, 0:1]).then_inc(counts, 1)
                dve.tensor_scalar(equal[:, :], gap[:, :], edge, 0.0, ALU.is_equal, ALU.add,
                                  accum_out=count[:, 1:2]).then_inc(counts, 1)
                dve.wait_ge(counts, 33)
                link(dve.tensor_tensor_scan(run_eq[:, :], equal[:, :], zeros[:, :], 0.0, ALU.add, ALU.add))
                dve.wait_ge(pe_done, 4)
                link(dve.tensor_scalar(room[:, :], bank[2][:, 2:3], -1.0, float(NUM_HEAVY), ALU.mult, ALU.add))
                link(dve.tensor_tensor(room[:, :], room[:, :], bank[2][:, 3:4], ALU.subtract))
                link(dve.tensor_scalar(run_eq[:, :], run_eq[:, :], room[:, :], None, ALU.is_le))
                link(dve.tensor_tensor(run_eq[:, :], run_eq[:, :], equal[:, :], ALU.mult))
                link(dve.tensor_tensor(picked[:, :], run_eq[:, :], better[:, :], ALU.add))
                dve.tensor_reduce(count[:, 0:1], picked[:, :], AX, ALU.add).then_inc(counts, 1)
                link(dve.tensor_tensor_scan(slot[:, :], picked[:, :], zeros[:, :], 0.0, ALU.add, ALU.add))
                dve.wait_ge(pe_done, 5)
                link(dve.tensor_scalar(slot[:, :], slot[:, :], bank[2][:, 4:5], None, ALU.add))
                link(dve.tensor_tensor(slot[:, :], slot[:, :], picked[:, :], ALU.mult))
                link(dve.tensor_scalar(slot[:, :], slot[:, :], -1.0, None, ALU.add))
                dve.wait_ge(score_exp, 1)
                link(dve.tensor_scalar(straight[:, :], expd[:, :], -1.0, 1.0, ALU.mult, ALU.add))
                dve.tensor_tensor(straight[:, :], straight[:, :], expd[:, :], ALU.add).then_inc(caps, 1)
                dve.wait_ge(pe_done, 6)
                link(dve.tensor_copy(slot_t[:, :], bank[3][:, 0:P]))
                dve.tensor_copy(tagged[:, :, 1], bank[3][:, P:2 * P]).then_inc(caps, 1)
                for b in range(B):
                    if b >= 2:
                        dve.wait_ge(lists, b - 1)
                    for t in range(NT):
                        g = b * NT + t
                        dve.tensor_scalar(takes[(b % 2) * NT + t][:, :], slots[:, :], slot_t[:, g:g + 1], None,
                                          ALU.is_equal).then_inc(taken, 1)
                dve.wait_ge(lists, B)
                for j in range(NJ):
                    pairs = bank[4 + j][:, 0:2 * B].rearrange("p (b e) -> p b e", e=2)
                    dve.tensor_copy(listed[:, 0:B * NJ].rearrange("p (b j) -> p b j", j=NJ)[:, :, j], pairs[:, :, 0])
                    dve.tensor_copy(weights[:, :].rearrange("p (b j) -> p b j", j=NJ)[:, :, j], pairs[:, :, 1])

        with ExitStack() as c:
            both = [sb(f"h_both{n}", [P, NJ, 2 * D], c=c) for n in range(2)]
            normed_x = sb("h_normed_x", [P, NJ, D], c=c)
            w1_hi = sb("h_w1_hi", [P, ND, FH * P], F32R, c=c)
            w1_lo = sb("h_w1_lo", [P, ND, FH * P], F32R, c=c)
            w2_hi = sb("h_w2_hi", [P, FH, D], F32R, c=c)
            w2_lo = sb("h_w2_lo", [P, FH, D], F32R, c=c)
            xt_hi = sb("h_xt_hi", [P, ND, 512], F32R, c=c)
            xt_lo = sb("h_xt_lo", [P, ND, 512], F32R, c=c)
            hidden = [sb(f"h_hidden{n}", [P, 512], c=c) for n in range(2)]
            hidden_hi = [sb(f"h_hidden_hi{n}", [P, 512], F32R, c=c) for n in range(2)]
            hidden_lo = [sb(f"h_hidden_lo{n}", [P, 512], F32R, c=c) for n in range(2)]
            gamma = sb("h_gamma_sb", [P, ND], c=c)
            b1 = sb("h_b1_sb", [P, FH], c=c)
            b2 = sb("h_b2_sb", [P, D], c=c)
            rows = [sb(f"rows{n}", [P, NJ], U32, c=c) for n in range(2)]
            weight = [sb(f"weight{n}", [P, NJ], c=c) for n in range(2)]
            stats = sb("h_stats", [P, NJ, 6], c=c)
            moments = sb("h_moments", [P, NJ, 2], c=c)
            var_eps = sb("h_var_eps", [P, NJ], c=c)
            rstd = sb("h_rstd", [P, NJ], c=c)
            std = sb("h_std", [P, NJ], c=c)
            norm = sb("h_norm", [P, NJ], c=c)
            rnorm = sb("h_rnorm", [P, NJ], c=c)
            scale = sb("h_scale", [P, NJ], c=c)
            o_stats = sb("ho_stats", [P, NJ, 6], c=c)
            o_moments = sb("ho_moments", [P, NJ, 2], c=c)
            o_var_eps = sb("ho_var_eps", [P, NJ], c=c)
            o_rstd = sb("ho_rstd", [P, NJ], c=c)

            staged = [sem(f"heavy_staged{n}", c) for n in range(2)]
            small = sem("heavy_small_weights", c)
            folded = sem("heavy_gamma_folded", c)
            w_hi = sem("heavy_weights_hi", c)
            w_lo = sem("heavy_weights_lo", c)
            indexed = sem("heavy_indexed", c)
            gathered = [sem(f"heavy_gathered{n}", c) for n in range(2)]
            scattered = [sem(f"heavy_scattered{n}", c) for n in range(2)]
            stats_done = sem("heavy_stats", c)
            moments_done = sem("heavy_moments", c)
            var_done = sem("heavy_var", c)
            pow_done = sem("heavy_pow", c)
            scaled = sem("heavy_scaled", c)
            normed = sem("heavy_normed", c)
            based = sem("heavy_light_and_bias", c)
            turned = sem("heavy_turned", c)
            turned_hi = sem("heavy_turned_hi", c)
            turned_lo = sem("heavy_turned_lo", c)
            hidden_ps = sem("heavy_hidden_ps", c)
            activated = sem("heavy_activated", c)
            his = sem("heavy_hidden_hi", c)
            los = sem("heavy_hidden_lo", c)
            used = sem("heavy_hidden_used", c)
            mixed = sem("heavy_mixed", c)
            o_stats_done = sem("heavy_out_stats", c)
            o_moments_done = sem("heavy_out_moments", c)
            o_var_done = sem("heavy_out_var", c)
            o_pow_done = sem("heavy_out_pow", c)
            out_n = sem("heavy_out_normed", c)
            out_ready = sem("heavy_out_ready", c)
            chain = sem("heavy_chain", c)
            turn = bank[0:2]
            hid = bank[2:4]
            outs = bank[4:8]
            STATS_OUT, FINISH, INDEX, STATS_IN, PREPARE = 1, 3, 5, 10, 12
            W_STAGES = 4
            halves = [both[n][:, :, :].rearrange("p j d -> p (j d)") for n in range(2)]
            w_parts = []
            for hi, lo in ((w1_hi, w1_lo), (w2_hi, w2_lo)):
                for m in range(2):
                    k = hi.shape[1] // 2
                    w_parts.append([w[:, m * k:(m + 1) * k, :].rearrange("p a b -> p (a b)") for w in (hi, lo)])
            block = c.enter_context(nc.Block())

            def all_sequences(eng, main):
                main(0, 0, True, False)
                main(0, 1, False, False)
                with eng.Fori(1, PAIRS - 1) as i:
                    for h in range(2):
                        main(i, h, False, False)
                main(PAIRS - 1, 0, False, False)
                main(PAIRS - 1, 1, False, True)

            @block.sync
            def _(sp):
                for dst, src in (
                    (gamma[:, :], h_gamma.rearrange("(c p) -> p c", p=P)),
                    (b1[:, :], h_b1.rearrange("(c p) -> p c", p=P)),
                    (b2[:, :], h_b2.partition_broadcast(P)),
                ):
                    sp.dma_start(dst, src, allow_slow_non_contiguous=True).then_inc(small, 16)
                views = [w.rearrange("(c p) f -> p c f", p=P) for w in (h_w1, h_w2)]
                for s in range(W_STAGES):
                    if s >= 2:
                        sp.wait_ge(w_lo, s - 1)
                    view = views[s // 2]
                    k = view.shape[1] // 2
                    sp.dma_start(halves[s % 2].rearrange("p (c f) -> p c f", c=k),
                                 view[:, (s % 2) * k:(s % 2 + 1) * k, :]).then_inc(staged[s % 2], 16)

            @block.gpsimd
            def _(pool):
                def gather(i, h):
                    gate(pool, indexed, at(i, h, 1, 1))
                    for j in range(NJ):
                        pool.indirect_dma_start(both[h % 2][:, j, :], None, xl_dram,
                                                bass.IndirectOffsetOnAxis(rows[h % 2][:, j:j + 1], 0))\
                            .then_inc(gathered[h % 2], 16)

                def powers(i, h):
                    pool.wait_ge(var_done, at(i, h, 1, 1))
                    pool.tensor_tensor(rstd[:, :], var_eps[:, :], neg_half[:, 0:NJ], ALU.pow).then_inc(pow_done, 1)
                    pool.tensor_tensor(std[:, :], moments[:, :, 1], half[:, 0:NJ], ALU.pow).then_inc(pow_done, 1)

                def out_power(i, h):
                    pool.wait_ge(o_var_done, at(i, h, 1, 0))
                    pool.tensor_tensor(o_rstd[:, :], o_var_eps[:, :], neg_half[:, 0:NJ], ALU.pow).then_inc(o_pow_done, 1)
                    gate(pool, out_ready, at(i, h, NJ, 0))
                    n = (h + 1) % 2
                    for j in range(NJ):
                        pool.indirect_dma_start(out_flat, bass.IndirectOffsetOnAxis(rows[n][:, j:j + 1], 0),
                                                both[n][:, j, D:2 * D], None).then_inc(scattered[n], 16)

                def main(i, h, first, last):
                    if not first:
                        out_power(i, h)
                    if not last:
                        gather(i, h + 1)
                        powers(i, h + 1)
                    else:
                        out_power(i, h + 1)

                pool.wait_ge(w_lo, W_STAGES)
                gather(0, 0)
                powers(0, 0)
                all_sequences(pool, main)
                for n in range(2):
                    pool.wait_ge(scattered[n], 16 * NJ * PAIRS)

            @block.scalar
            def _(act):
                act.wait_ge(small, 48)
                for s in range(W_STAGES):
                    act.wait_ge(staged[s % 2], 16 * (s // 2) + 16)
                    if s < 2:
                        for m in range(ND // 2):
                            piece = halves[s][:, m * FH * P:(m + 1) * FH * P]
                            c_ = s * (ND // 2) + m
                            act.activation(piece, piece, ACT.Copy, scale=gamma[:, c_:c_ + 1]).then_inc(folded, 1)
                        act.wait_ge(folded, (s + 1) * (ND // 2))
                    act.activation(w_parts[s][0], halves[s % 2], ACT.Copy).then_inc(w_hi, 1)

                def turn_hi(i, h, j):
                    act.wait_ge(turned, at(i, h, NJ, j + 1))
                    act.activation(xt_hi[:, :, j * P:(j + 1) * P], turn[j % 2][:, :].rearrange("p (c q) -> p c q", c=ND),
                                   ACT.Copy).then_inc(turned_hi, 1)

                def main(i, h, first, last):
                    for f in range(FH):
                        act.wait_ge(hidden_ps, at(i, h, FH, f + 1))
                        act.wait_ge(los, at(i, h, FH, f + 1))
                        act.activation(hidden[f % 2][:, :], hid[f % 2][:, :], ACT.Gelu,
                                       bias=b1[:, f:f + 1]).then_inc(activated, 1)
                        act.wait_ge(activated, at(i, h, FH, f + 1) + 2)
                        act.wait_ge(used, at(i, h, FH, f + 1))
                        act.activation(hidden_hi[f % 2][:, :], hidden[f % 2][:, :], ACT.Copy).then_inc(his, 1)
                    if not last:
                        for j in range(NJ):
                            turn_hi(i, h + 1, j)

                act.sem_inc(activated, 2)
                for j in range(NJ):
                    turn_hi(0, 0, j)
                all_sequences(act, main)

            @block.tensor
            def _(pe):
                def product(ps, lhs, rhs, steps):
                    count = 0
                    for a, b in steps:
                        for x_, y_ in ((0, 0), (0, 1), (1, 0)):
                            count += 1
                            last = pe.matmul(ps, a[x_], b[y_], start=lhs and count == 1,
                                             stop=rhs and count == 3 * len(steps))
                    return last

                def turn_tile(i, h, j):
                    pe.wait_ge(normed, at(i, h, NJ, j + 1))
                    pe.wait_ge(turned_lo, at(i, h, NJ, j + 1))
                    for c_ in range(ND):
                        last = pe.transpose(turn[j % 2][:, c_ * P:(c_ + 1) * P],
                                            normed_x[:, j, c_ * P:(c_ + 1) * P], ident[:, :])
                    last.then_inc(turned, 1)

                def first_layer(i, h, f):
                    if f == 0:
                        pe.wait_ge(turned_lo, at(i, h, NJ, NJ) + 2)
                    pe.wait_ge(activated, at(i, h, FH, f + 1))
                    cols = slice(f * P, (f + 1) * P)
                    product(hid[f % 2][:, :], True, True,
                            [((w1_hi[:, c_, cols], w1_lo[:, c_, cols]), (xt_hi[:, c_, :], xt_lo[:, c_, :]))
                             for c_ in range(ND)]).then_inc(hidden_ps, 1)

                def second_layer(i, h, f):
                    pe.wait_ge(los, at(i, h, FH, f + 1) + 2)
                    if f == 0:
                        pe.wait_ge(mixed, at(i, h, NJ, NJ))
                    for j in range(NJ):
                        cols = slice(j * P, (j + 1) * P)
                        last = product(outs[j][:, :], f == 0, f == FH - 1,
                                       [((hidden_hi[f % 2][:, cols], hidden_lo[f % 2][:, cols]),
                                         (w2_hi[:, f, :], w2_lo[:, f, :]))])
                    last.then_inc(used, 1)

                def main(i, h, first, last):
                    for f in range(FH + 2):
                        if f < FH:
                            first_layer(i, h, f)
                        if not last and FH - 1 <= f <= FH:
                            for j in ((0, 1), (2, 3))[f - (FH - 1)]:
                                turn_tile(i, h + 1, j)
                        if f >= 2:
                            second_layer(i, h, f - 2)

                pe.sem_inc(used, 2)
                pe.wait_ge(w_lo, W_STAGES)
                for j in range(NJ):
                    turn_tile(0, 0, j)
                all_sequences(pe, main)

            @block.vector
            def _(dve):
                def index(i, h):
                    dve.tensor_scalar(rows[h % 2][:, :], listed[:, bass.ds((i * 2 + h) * NJ, NJ)], 0.0, None,
                                      ALU.add).then_inc(indexed, 1)

                def stats_in(i, h):
                    mine = both[h % 2]
                    gate(dve, gathered[h % 2], i * (16 * NJ) + 16 * NJ * (h // 2 + 1))
                    for j in range(NJ):
                        dve.bn_stats(stats[:, j, :], mine[:, j, 0:D]).then_inc(stats_done, 1)
                    gate(dve, stats_done, at(i, h, NJ, NJ))
                    for j in range(NJ):
                        dve.bn_aggr(moments[:, j, :], stats[:, j, :]).then_inc(moments_done, 1)
                    dve.wait_ge(moments_done, at(i, h, NJ, NJ))
                    dve.tensor_scalar(var_eps[:, :], moments[:, :, 1], LN_EPS, None, ALU.add).then_inc(var_done, 1)

                def prepare(i, h):
                    mine = both[h % 2]
                    links = [0]

                    def link(ins):
                        links[0] += 1
                        ins.then_inc(chain, 1)
                        dve.wait_ge(chain, at(i, h, 4, links[0]))

                    dve.wait_ge(pow_done, at(i, h, 2, 2))
                    link(dve.scalar_tensor_tensor(out=norm[:, :], in0=std[:, :], scalar=SQRT_D, in1=rstd[:, :],
                                                  op0=ALU.mult, op1=ALU.mult))
                    link(dve.tensor_scalar(norm[:, :], norm[:, :], NORM_EPS, 1.0 / SQRT_D, ALU.max, ALU.mult))
                    link(dve.reciprocal(rnorm[:, :], norm[:, :]))
                    dve.tensor_tensor(scale[:, :], rstd[:, :], rnorm[:, :], ALU.mult).then_inc(scaled, 1)
                    dve.wait_ge(scaled, at(i, h, 1, 1))
                    for j in range(NJ):
                        dve.tensor_scalar(normed_x[:, j, :], mine[:, j, 0:D], moments[:, j, 0:1],
                                          scale[:, j:j + 1], ALU.subtract, ALU.mult).then_inc(normed, 1)
                    link(dve.tensor_scalar(weight[h % 2][:, :], weights[:, bass.ds((i * 2 + h) * NJ, NJ)], 0.0, None,
                                           ALU.add))
                    for j in range(NJ):
                        dve.scalar_tensor_tensor(out=mine[:, j, D:2 * D], in0=b2[:, :],
                                                 scalar=weight[h % 2][:, j:j + 1], in1=mine[:, j, D:2 * D],
                                                 op0=ALU.mult, op1=ALU.add).then_inc(based, 1)

                def turn_lo(i, h, j):
                    dve.wait_ge(turned_hi, at(i, h, NJ, j + 1))
                    dve.tensor_tensor(xt_lo[:, :, j * P:(j + 1) * P],
                                      turn[j % 2][:, :].rearrange("p (c q) -> p c q", c=ND),
                                      xt_hi[:, :, j * P:(j + 1) * P], ALU.subtract).then_inc(turned_lo, 1)

                def mix(i, h):
                    n = (h + 1) % 2
                    dve.wait_ge(based, at(i, h, NJ, 0))
                    dve.wait_ge(used, at(i, h, FH, 0) + 2)
                    for j in range(NJ):
                        dve.scalar_tensor_tensor(out=both[n][:, j, D:2 * D], in0=outs[j][:, :],
                                                 scalar=weight[n][:, j:j + 1], in1=both[n][:, j, D:2 * D],
                                                 op0=ALU.mult, op1=ALU.add).then_inc(mixed, 1)

                def stats_out(i, h):
                    n = (h + 1) % 2
                    gate(dve, mixed, at(i, h, NJ, NJ))
                    for j in range(NJ):
                        dve.bn_stats(o_stats[:, j, :], both[n][:, j, D:2 * D]).then_inc(o_stats_done, 1)
                    gate(dve, o_stats_done, at(i, h, NJ, 0))
                    for j in range(NJ):
                        dve.bn_aggr(o_moments[:, j, :], o_stats[:, j, :]).then_inc(o_moments_done, 1)
                    dve.wait_ge(o_moments_done, at(i, h, NJ, 0))
                    dve.tensor_scalar(o_var_eps[:, :], o_moments[:, :, 1], LN_EPS, None, ALU.add).then_inc(o_var_done, 1)

                def finish(i, h):
                    n = (h + 1) % 2
                    dve.wait_ge(o_pow_done, at(i, h, 1, 0))
                    for j in range(NJ):
                        dve.tensor_scalar(both[n][:, j, D:2 * D], both[n][:, j, D:2 * D], o_moments[:, j, 0:1],
                                          o_rstd[:, j:j + 1], ALU.subtract, ALU.mult).then_inc(out_n, 1)
                    for j in range(NJ):
                        dve.wait_ge(out_n, at(i, h, NJ, j + 1 - NJ))
                        dve.tensor_tensor(both[n][:, j, D:2 * D], both[n][:, j, D:2 * D], both[n][:, j, 0:D],
                                          ALU.add).then_inc(out_ready, 1)

                def main(i, h, first, last):
                    if not first:
                        mix(i, h)
                    for f in range(FH):
                        dve.wait_ge(his, at(i, h, FH, f + 1))
                        dve.tensor_tensor(hidden_lo[f % 2][:, :], hidden[f % 2][:, :], hidden_hi[f % 2][:, :],
                                          ALU.subtract).then_inc(los, 1)
                        if f == STATS_OUT and not first:
                            stats_out(i, h)
                        if f == FINISH and not first:
                            finish(i, h)
                        if f == INDEX and not last:
                            if not first:
                                n = (h + 1) % 2
                                dve.wait_ge(scattered[n], i * (16 * NJ) + 16 * NJ * ((h + 1) // 2))
                            index(i, h + 1)
                        if f == STATS_IN and not last:
                            stats_in(i, h + 1)
                        if f == PREPARE and not last:
                            prepare(i, h + 1)
                    if not last:
                        for j in range(NJ):
                            turn_lo(i, h + 1, j)
                    else:
                        mix(i, h + 1)
                        stats_out(i, h + 1)
                        finish(i, h + 1)

                dve.sem_inc(turned_lo, 2)
                dve.sem_inc(los, 2)
                dve.sem_inc(mixed, NJ)
                index(0, 0)
                for s in range(W_STAGES):
                    dve.wait_ge(w_hi, s + 1)
                    dve.tensor_tensor(w_parts[s][1], halves[s % 2], w_parts[s][0], ALU.subtract).then_inc(w_lo, 1)
                stats_in(0, 0)
                prepare(0, 0)
                for j in range(NJ):
                    turn_lo(0, 0, j)
                all_sequences(dve, main)


def kernel(**inputs):
    import numpy as np
    import concourse.bacc as bacc
    from concourse.bass_utils import run_bass_kernel_spmd as run

    g = {k: np.asarray(v) for k, v in inputs.items()}
    x = g["L0_attn_x"]
    rank = g["L0_attn_dt_projs_weight"].shape[1]
    states = g["L0_attn_A_logs"].shape[1]
    proj = g["L0_attn_x_proj_weight"].T
    w_x = np.zeros((proj.shape[0], P), proj.dtype)
    for n in range(3):
        w_x[:, 32 * n:32 * n + states] = proj[:, rank:rank + states]
    w_x[:, 96:96 + rank] = proj[:, :rank]
    arrays = {
        "x": x, "means": g["L0_attn_means"], "means_t": g["L0_attn_means"].T,
        "prompt_t": g["L0_attn_prompt_weight"].T, "w_x": w_x, "w_c": proj[:, rank + states:],
        "w_dt_t": g["L0_attn_dt_projs_weight"].T, "dt_bias": g["L0_attn_dt_projs_bias"],
        "a_logs": g["L0_attn_A_logs"], "ds": g["L0_attn_Ds"],
        "routing": g["L0_ffn_routing_token"],
    }
    for side in ("light", "heavy"):
        for part in ("gamma", "w1", "b1", "w2", "b2"):
            arrays[f"{side[0]}_{part}"] = g[f"L0_ffn_{side}_{part}"]
    arrays = {k: np.ascontiguousarray(v) for k, v in arrays.items()}
    nc = bacc.Bacc("TRN2", target_bir_lowering=False, num_devices=1)
    args = {k: nc.dram_tensor(f"in_{k}", v.shape, mybir.dt.from_np(v.dtype), kind="ExternalInput").ap()
            for k, v in arrays.items()}
    out = nc.dram_tensor("out", x.shape, F32, kind="ExternalOutput").ap()
    build(nc, out=out, **args)
    result = run(nc, [{f"in_{k}": v for k, v in arrays.items()}], core_ids=[0])
    return result.results[0]["out"]
```

```python
import math
from contextlib import ExitStack

import concourse.bass as bass
from concourse import mybir

P = 128
F32 = mybir.dt.float32
F32R = mybir.dt.float32r
BF16 = mybir.dt.bfloat16
U32 = mybir.dt.uint32
I32 = mybir.dt.int32
ALU = mybir.AluOpType
ACT = mybir.ActivationFunctionType
AX = mybir.AxisListType.X

LN_EPS = 1e-5
NORM_EPS = 1e-12
NUM_HEAVY = 512
DESCENT_STEPS = 50
EFFECTIVE_K = 576.0
LOG_K = 6.356107660695891


def build(nc, x, means, means_t, prompt_t, w_x, w_dt_t, dt_bias, a_logs, ds,
          routing, l_gamma, l_w1, l_b1, l_w2, l_b2, h_gamma, h_w1, h_b1, h_w2, h_b2, out):
    B, L, D = x.shape
    NT = L // P
    ND = D // P
    K = means.shape[0]
    NS = a_logs.shape[1]
    R = w_dt_t.shape[0]
    FL = l_w1.shape[1] // P
    FH = h_w1.shape[1] // P
    NJ = NUM_HEAVY // P
    PAIRS = B // 2
    KT = K * NT
    DT_ROW = 3 * 32
    C_ROW = 2 * 32 + NS
    SQRT_D = float(D) ** 0.5

    xs_dram = nc.dram_tensor("sorted_rows", [B * L, D], F32, kind="Internal").ap()
    ys_dram = nc.dram_tensor("sorted_outputs", [B * L, D], F32, kind="Internal").ap()
    xl_dram = nc.dram_tensor("residual_and_light", [B * L, 2 * D], F32, kind="Internal").ap()

    x_rows = x.rearrange("b (t p) d -> b p t d", p=P)
    xs_rows = xs_dram.rearrange("(b t p) d -> b p t d", p=P, t=NT)
    ys_rows = ys_dram.rearrange("(b t p) d -> b p t d", p=P, t=NT)
    xl_rows = xl_dram.rearrange("(b t p) d -> b p t d", p=P, t=NT)
    out_flat = out.rearrange("b l d -> (b l) d")
    out_rows = out.rearrange("b (t p) d -> b p t d", p=P)

    def row(view, b):
        return view[bass.ds(b, 1)].rearrange("a p t d -> (a p) t d")

    def at(i, h, per, k):
        return i * (2 * per) + (per * h + k)

    def all_sequences(eng, main):
        main(0, 0, True, False)
        main(0, 1, False, False)
        with eng.Fori(1, PAIRS - 1) as i:
            for h in range(2):
                main(i, h, False, False)
        main(PAIRS - 1, 0, False, False)
        main(PAIRS - 1, 1, False, True)

    with ExitStack() as ctx:
        def sb(name, shape, dt=F32, c=ctx):
            return c.enter_context(nc.sbuf_tensor(name, shape, dt))

        def sem(name, c=ctx):
            return c.enter_context(nc.semaphore(name))

        gates = sem("gates_passed")

        def gate(eng, signal, value):
            eng.wait_ge(signal, value)
            eng.sem_inc(gates, 1)

        bank = [ctx.enter_context(nc.psum_tensor(f"bank{n}", [P, 512], F32)) for n in range(8)]

        ident = sb("ident", [P, P])
        ones = sb("ones", [P, P])
        positions = sb("positions", [P, (B + 2) * NT], U32)
        bounds = sb("bounds", [K, 2 * B])
        scores = sb("scores", [P, B * NT])
        half = sb("half", [P, NT])
        neg_half = sb("neg_half", [P, NT])
        mean_dirs = sb("mean_dirs", [P, ND, K])
        cluster_c = sb("cluster_c", [K, P])
        zero_bias = sb("zero_bias", [P, 1])
        one_bias = sb("one_bias", [P, 1])

        with ExitStack() as c:
            means_sb = sb("means_sb", [K, D], c=c)
            means_sq = sb("means_sq", [K, D], c=c)
            mnorm = sb("mnorm", [K, 4], c=c)
            mhalf = sb("mhalf", [K, 1], c=c)
            means_ts = sb("means_ts", [P, ND, K], c=c)
            prompt_ts = sb("prompt_ts", [P, ND, NS], c=c)
            loads = sem("setup_loads", c)
            made = sem("setup_made", c)
            chain = sem("setup_chain", c)
            powered = sem("setup_powered", c)
            product = sem("setup_product", c)
            block = c.enter_context(nc.Block())

            @block.sync
            def _(sp):
                sp.dma_start(means_sb[:, :], means).then_inc(loads, 16)
                sp.dma_start(means_ts[:, :, :], means_t.rearrange("(c p) k -> p c k", p=P)).then_inc(loads, 16)
                sp.dma_start(prompt_ts[:, :, :], prompt_t.rearrange("(c p) n -> p c n", p=P)).then_inc(loads, 16)

            @block.gpsimd
            def _(pool):
                pool.memset(ident[:, :], 0.0).then_inc(made, 1)
                pool.memset(ones[:, :], 1.0).then_inc(made, 1)
                pool.memset(half[:, :], 0.5).then_inc(made, 1)
                pool.memset(neg_half[:, :], -0.5).then_inc(made, 1)
                pool.memset(mhalf[:, :], 0.5).then_inc(made, 1)
                pool.memset(positions[:, :], 0).then_inc(made, 1)
                pool.memset(zero_bias[:, :], 0.0).then_inc(made, 1)
                pool.memset(one_bias[:, :], 1.0).then_inc(made, 1)
                pool.memset(cluster_c[:, :], 0.0).then_inc(made, 1)
                pool.wait_ge(made, 9)
                pool.affine_select(out=ident[:, :], in_=ident[:, :], compare_op=ALU.not_equal, fill=1.0,
                                   base=0, pattern=[[-1, P]], channel_multiplier=1).then_inc(made, 1)
                pool.wait_ge(chain, 2)
                pool.tensor_tensor(mnorm[:, 1:2], mnorm[:, 0:1], mhalf[:, :], ALU.pow).then_inc(powered, 1)

            @block.vector
            def _(dve):
                dve.wait_ge(loads, 48)
                dve.tensor_tensor(means_sq[:, :], means_sb[:, :], means_sb[:, :], ALU.mult).then_inc(chain, 1)
                dve.wait_ge(chain, 1)
                dve.tensor_reduce(mnorm[:, 0:1], means_sq[:, :], AX, ALU.add).then_inc(chain, 1)
                dve.wait_ge(powered, 1)
                dve.tensor_scalar(mnorm[:, 2:3], mnorm[:, 1:2], NORM_EPS, None, ALU.max).then_inc(chain, 1)
                dve.wait_ge(chain, 3)
                dve.reciprocal(mnorm[:, 3:4], mnorm[:, 2:3]).then_inc(chain, 1)
                dve.wait_ge(chain, 4)
                dve.tensor_scalar(means_sq[:, :], means_sb[:, :], mnorm[:, 3:4], None, ALU.mult).then_inc(chain, 1)
                dve.wait_ge(product, 1)
                dve.tensor_copy(mean_dirs[:, :, :].rearrange("p c k -> p (c k)"), bank[0][:, 0:ND * K]).then_inc(chain, 1)
                dve.wait_ge(product, 2)
                dve.tensor_copy(cluster_c[:, C_ROW:C_ROW + NS], bank[1][0:K, 0:NS]).then_inc(chain, 1)

            @block.tensor
            def _(pe):
                pe.wait_ge(made, 10)
                pe.wait_ge(chain, 5)
                for c_ in range(ND):
                    last = pe.transpose(bank[0][:, c_ * K:(c_ + 1) * K], means_sq[:, c_ * P:(c_ + 1) * P],
                                        ident[0:K, 0:K])
                last.then_inc(product, 1)
                for c_ in range(ND):
                    last = pe.matmul(bank[1][0:K, 0:NS], means_ts[:, c_, :], prompt_ts[:, c_, :],
                                     start=(c_ == 0), stop=(c_ == ND - 1))
                last.then_inc(product, 1)

        with ExitStack() as c:
            RING = 4
            xa = [sb(f"xa{n}", [P, NT, D], c=c) for n in range(RING)]
            HALF = NT // 2
            xt = [sb(f"xt{n}", [P, ND, HALF * P], c=c) for n in range(2)]
            means_wide = sb("means_wide", [P, ND, P], c=c)
            dirs = [sb(f"dirs{n}", [P, HALF * P], c=c) for n in range(2)]
            stats = sb("stats", [P, NT, 6], c=c)
            moments = sb("moments", [P, NT, 2], c=c)
            var_eps = sb("var_eps", [P, NT], c=c)
            rstd = sb("rstd", [P, NT], c=c)
            std = sb("std", [P, NT], c=c)
            norm = sb("norm", [P, NT], c=c)
            rnorm = sb("rnorm", [P, NT], c=c)
            cosines = sb("cosines", [P, NT, K], c=c)
            best = sb("best", [P, NT], c=c)
            is_best = sb("is_best", [P, NT, K], c=c)
            candidate = sb("candidate", [P, NT, K], c=c)
            cluster = sb("cluster", [P, NT], c=c)
            cluster_ids = sb("cluster_ids", [P, NT, K], c=c)
            cluster_ids_m = sb("cluster_ids_m", [P, NT, K], c=c)
            ids_i = sb("ids_i", [P, NT, K], I32, c=c)
            onehot = sb("onehot", [P, K, NT], BF16, c=c)
            below = sb("below", [P, NT, K], BF16, c=c)
            upto = sb("upto", [P, NT, K], BF16, c=c)
            earlier = sb("earlier", [P, P], BF16, c=c)
            ones_b = sb("ones_b", [P, P], BF16, c=c)
            zeros = sb("zeros", [P, KT], c=c)
            totals = sb("totals", [P, KT], c=c)
            running = sb("running", [P, KT], c=c)
            before = sb("before", [P, KT], c=c)
            place = sb("place", [P, KT], c=c)
            chosen = sb("chosen", [P, KT], c=c)
            place_in_seq = sb("place_in_seq", [P, NT], c=c)
            first_row = sb("first_row", [P, 1], c=c)
            target = [sb(f"target{n}", [P, NT], U32, c=c) for n in range(RING)]
            made = sem("sort_consts", c)
            loaded = [sem(f"sort_loaded{n}", c) for n in range(RING)]
            stats_done = sem("sort_stats", c)
            moments_done = sem("sort_moments", c)
            var_done = sem("sort_var", c)
            pow_done = sem("sort_pow", c)
            normed = sem("sort_normed", c)
            turned = sem("sort_turned", c)
            turned_sb = sem("sort_turned_sb", c)
            widened = sem("sort_means_wide", c)
            dirs_ps_done = sem("sort_dirs_ps", c)
            dirs_done = sem("sort_dirs", c)
            cos_done = sem("sort_cosines", c)
            onehots = sem("sort_onehots", c)
            counted = sem("sort_counted", c)
            norm_chain = sem("sort_norm_chain", c)
            best_chain = sem("sort_best_chain", c)
            place_chain = sem("sort_place_chain", c)
            targets = sem("sort_targets", c)
            scattered = [sem(f"sort_scattered{n}", c) for n in range(RING)]
            turn = bank[0:2]
            dirs_ps = bank[4:6]
            cos_ps = bank[6:8]
            count_ps = bank[3]
            block = c.enter_context(nc.Block())

            def nth(i, u, per, k):
                return i * (RING * per) + (per * u + k)

            def all_rounds(eng, main):
                for u in range(RING):
                    main(0, u, u, RING)
                with eng.Fori(1, B // RING - 1) as i:
                    for u in range(RING):
                        main(i, u, RING, RING)
                for u in range(RING):
                    main(B // RING - 1, u, RING, RING - 1 - u)

            @block.sync
            def _(sp):
                def main(i, u, before, left):
                    if left >= 3:
                        n = (u + 3) % RING
                        if before:
                            sp.wait_ge(scattered[n], i * (16 * NT) + 16 * NT * ((u - 1) // RING + 1))
                        sp.dma_start(xa[n][:, :, :], row(x_rows, i * RING + (u + 3))).then_inc(loaded[n], 16)

                for n in range(3):
                    sp.dma_start(xa[n][:, :, :], row(x_rows, n)).then_inc(loaded[n], 16)
                all_rounds(sp, main)

            @block.gpsimd
            def _(pool):
                pool.memset(earlier[:, :], 1.0).then_inc(made, 1)
                pool.memset(means_wide[:, :, :], 0.0).then_inc(made, 1)
                pool.memset(ones_b[:, :], 1.0).then_inc(made, 1)
                pool.memset(zeros[:, :], 0.0).then_inc(made, 1)
                pool.memset(first_row[:, :], 0.0).then_inc(made, 1)
                pool.iota(ids_i[:, :, :], pattern=[[0, NT], [1, K]], base=0, channel_multiplier=0).then_inc(made, 1)
                pool.wait_ge(made, 6)
                pool.affine_select(out=earlier[:, :], in_=earlier[:, :], compare_op=ALU.is_gt, fill=0.0,
                                   base=0, pattern=[[1, P]], channel_multiplier=-1).then_inc(made, 1)
                pool.tensor_copy(cluster_ids[:, :, :], ids_i[:, :, :]).then_inc(made, 1)
                pool.wait_ge(made, 8)
                pool.tensor_scalar(cluster_ids_m[:, :, :], cluster_ids[:, :, :], -float(K), None,
                                   ALU.add).then_inc(made, 1)

                def powers(i, u):
                    pool.wait_ge(var_done, nth(i, u, 1, 1))
                    pool.tensor_tensor(rstd[:, :], var_eps[:, :], neg_half[:, :], ALU.pow).then_inc(pow_done, 1)
                    pool.tensor_tensor(std[:, :], moments[:, :, 1], half[:, :], ALU.pow).then_inc(pow_done, 1)

                def main(i, u, before, left):
                    if left:
                        powers(i, u + 1)
                    gate(pool, targets, nth(i, u, 1, 1))
                    for t in range(NT):
                        pool.indirect_dma_start(xs_dram, bass.IndirectOffsetOnAxis(target[u][:, t:t + 1], 0),
                                                xa[u][:, t, :], None).then_inc(scattered[u], 16)

                powers(0, 0)
                all_rounds(pool, main)
                for n in range(RING):
                    pool.wait_ge(scattered[n], 16 * NT * B // RING)

            @block.scalar
            def _(act):
                act.sem_inc(turned_sb, 2)

                def turn_out(i, u):
                    for t in range(NT):
                        g, q = t // HALF, t % HALF
                        act.wait_ge(turned, nth(i, u, NT, t + 1))
                        act.activation(xt[g][:, :, q * P:(q + 1) * P],
                                       turn[t % 2][:, :].rearrange("p (c q) -> p c q", c=ND),
                                       ACT.Copy).then_inc(turned_sb, 1)
                        if t == HALF + 1:
                            dirs_out(i, u, 0)
                    dirs_out(i, u, 1)

                def dirs_out(i, u, g):
                    act.wait_ge(dirs_ps_done, nth(i, u, 2, g + 1))
                    act.activation(dirs[g][:, :], dirs_ps[g][:, :], ACT.Copy).then_inc(dirs_done, 1)

                def main(i, u, before, left):
                    if left:
                        turn_out(i, u + 1)

                turn_out(0, 0)
                all_rounds(act, main)

            @block.tensor
            def _(pe):
                pe.wait_ge(made, 9)
                pe.wait_ge(widened, 1)

                def turn_tile(i, u, t):
                    pe.wait_ge(normed, nth(i, u, NT, t + 1))
                    pe.wait_ge(turned_sb, nth(i, u, NT, t + 1))
                    for c_ in range(ND):
                        last = pe.transpose(turn[t % 2][:, c_ * P:(c_ + 1) * P],
                                            xa[u % RING][:, t, c_ * P:(c_ + 1) * P], ident[:, :])
                    last.then_inc(turned, 1)

                def dirs_of(i, u, g):
                    pe.wait_ge(turned_sb, nth(i, u, NT, (g + 1) * HALF) + 2)
                    for c_ in range(ND):
                        last = pe.matmul(dirs_ps[g][:, :], means_wide[:, c_, :], xt[g][:, c_, :],
                                         start=(c_ == 0), stop=(c_ == ND - 1))
                    last.then_inc(dirs_ps_done, 1)

                def cos_of(i, u, g):
                    pe.wait_ge(dirs_done, nth(i, u, 2, g + 1))
                    for q in range(HALF):
                        last = pe.transpose(cos_ps[g][:, q * P:(q + 1) * P], dirs[g][:, q * P:(q + 1) * P], ident[:, :])
                    last.then_inc(cos_done, 1)

                def cosines_of(i, u):
                    for t in range(NT):
                        turn_tile(i, u, t)
                        if t == HALF + 1:
                            dirs_of(i, u, 0)
                    cos_of(i, u, 0)
                    dirs_of(i, u, 1)
                    cos_of(i, u, 1)

                def main(i, u, before, left):
                    pe.wait_ge(onehots, nth(i, u, 3, 3))
                    flat = onehot[:, :, :].rearrange("p k t -> p (k t)")
                    pe.matmul(count_ps[:, 0:KT], earlier[:, :], flat, start=True, stop=True)
                    pe.matmul(count_ps[:, KT:2 * KT], ones_b[:, :], flat, start=True, stop=True)
                    for e, mask in enumerate((below, upto)):
                        for t in range(NT):
                            last = pe.matmul(count_ps[0:K, 2 * KT + e:2 * KT + e + 1], mask[:, t, :],
                                             ones_b[:, 0:1], start=(t == 0), stop=(t == NT - 1))
                    last.then_inc(counted, 1)
                    if left:
                        cosines_of(i, u + 1)

                cosines_of(0, 0)
                all_rounds(pe, main)

            @block.vector
            def _(dve):
                def linked(signal, per, i, u):
                    count = [0]

                    def link(ins):
                        count[0] += 1
                        ins.then_inc(signal, 1)
                        dve.wait_ge(signal, nth(i, u, per, count[0]))

                    return link

                def row_stats(i, u):
                    mine = xa[u % RING]
                    dve.wait_ge(loaded[u % RING], i * 16 + 16 * (u // RING + 1))
                    for t in range(NT):
                        dve.bn_stats(stats[:, t, :], mine[:, t, :]).then_inc(stats_done, 1)
                    gate(dve, stats_done, nth(i, u, NT, NT))
                    for t in range(NT):
                        dve.bn_aggr(moments[:, t, :], stats[:, t, :]).then_inc(moments_done, 1)
                    dve.wait_ge(moments_done, nth(i, u, NT, NT))
                    dve.tensor_scalar(var_eps[:, :], moments[:, :, 1], LN_EPS, None, ALU.add).then_inc(var_done, 1)

                def normalise(i, u):
                    mine = xa[u % RING]
                    link = linked(norm_chain, 3, i, u)
                    dve.wait_ge(pow_done, nth(i, u, 2, 2))
                    for t in range(NT):
                        dve.tensor_scalar(mine[:, t, :], mine[:, t, :], moments[:, t, 0:1], rstd[:, t:t + 1],
                                          ALU.subtract, ALU.mult).then_inc(normed, 1)
                    link(dve.scalar_tensor_tensor(out=norm[:, :], in0=std[:, :], scalar=SQRT_D, in1=rstd[:, :],
                                                  op0=ALU.mult, op1=ALU.mult))
                    link(dve.tensor_scalar(norm[:, :], norm[:, :], NORM_EPS, None, ALU.max))
                    link(dve.reciprocal(rnorm[:, :], norm[:, :]))

                def nearest(i, u):
                    link = linked(best_chain, 5, i, u)
                    dve.wait_ge(cos_done, nth(i, u, 2, 2))
                    wide = [P, NT, K]
                    for g in range(2):
                        tiles = slice(g * HALF, (g + 1) * HALF)
                        last = dve.tensor_tensor(cosines[:, tiles, :],
                                                 cos_ps[g][:, :].rearrange("p (t q) -> p t q", q=P)[:, :, 0:K],
                                                 rnorm[:, tiles].unsqueeze(2).to_broadcast([P, HALF, K]), ALU.mult)
                    link(last)
                    link(dve.tensor_reduce(best[:, :], cosines[:, :, :], AX, ALU.max))
                    link(dve.tensor_tensor(is_best[:, :, :], cosines[:, :, :],
                                           best[:, :].unsqueeze(2).to_broadcast(wide), ALU.is_equal))
                    link(dve.scalar_tensor_tensor(out=candidate[:, :, :], in0=is_best[:, :, :], scalar=-float(K),
                                                  in1=cluster_ids[:, :, :], op0=ALU.mult, op1=ALU.add))
                    link(dve.tensor_reduce(cluster[:, :], candidate[:, :, :], AX, ALU.min))
                    mine = cluster[:, :].unsqueeze(2).to_broadcast(wide)
                    dve.tensor_tensor(onehot[:, :, :].rearrange("p k t -> p t k"), cluster_ids_m[:, :, :], mine,
                                      ALU.is_equal).then_inc(onehots, 1)
                    dve.tensor_tensor(below[:, :, :], cluster_ids_m[:, :, :], mine, ALU.is_gt).then_inc(onehots, 1)
                    dve.tensor_tensor(upto[:, :, :], cluster_ids_m[:, :, :], mine, ALU.is_ge).then_inc(onehots, 1)

                def sorted_places(i, u):
                    link = linked(place_chain, 7, i, u)
                    dve.wait_ge(counted, nth(i, u, 1, 1))
                    link(dve.tensor_copy(totals[:, :], count_ps[:, KT:2 * KT]))
                    link(dve.tensor_tensor_scan(running[:, :], totals[:, :], zeros[:, :], 0.0, ALU.add, ALU.add))
                    link(dve.tensor_tensor(before[:, :], running[:, :], totals[:, :], ALU.subtract))
                    link(dve.tensor_tensor(place[:, :], before[:, :], count_ps[:, 0:KT], ALU.add))
                    link(dve.tensor_tensor(chosen[:, :], place[:, :],
                                           onehot[:, :, :].rearrange("p k t -> p (k t)"), ALU.mult))
                    link(dve.tensor_reduce(place_in_seq[:, :], chosen[:, :].rearrange("p (k t) -> p t k", t=NT),
                                           AX, ALU.add))
                    col = i * (RING * NT) + u * NT
                    dve.tensor_scalar(positions[:, bass.ds(col, NT)], place_in_seq[:, :], first_row[:, :], None,
                                      ALU.add)
                    dve.tensor_scalar(bounds[:, bass.ds(i * (RING * 2) + u * 2, 2)], count_ps[0:K, 2 * KT:2 * KT + 2],
                                      0.0, None, ALU.add)
                    dve.tensor_scalar(target[u][:, :], place_in_seq[:, :], first_row[:, :], None,
                                      ALU.add).then_inc(targets, 1)
                    dve.wait_ge(targets, nth(i, u, 1, 1))
                    link(dve.tensor_scalar(first_row[:, :], first_row[:, :], float(L), None, ALU.add))

                def main(i, u, before_, left):
                    if left:
                        row_stats(i, u + 1)
                    nearest(i, u)
                    if left:
                        normalise(i, u + 1)
                    sorted_places(i, u)

                dve.wait_ge(made, 9)
                dve.tensor_copy(means_wide[:, :, 0:K], mean_dirs[:, :, :]).then_inc(widened, 1)
                row_stats(0, 0)
                normalise(0, 0)
                all_rounds(dve, main)


        with ExitStack() as c:
            ITEMS = NS * ND
            raw = sb("raw", [P, NT, D], c=c)
            acc = [sb(f"acc{n}", [P, NT, D], c=c) for n in range(2)]
            feat = [sb(f"feat{n}", [P, ND, L], c=c) for n in range(2)]
            delta = [sb(f"delta{n}", [P, ND, L], c=c) for n in range(2)]
            decay = [sb(f"decay{n}", [P, L], c=c) for n in range(2)]
            drive = [sb(f"drive{n}", [P, L], c=c) for n in range(4)]
            states = [sb(f"states{n}", [P, L], c=c) for n in range(2 * ND)]
            b_rows = [sb(f"b_rows{n}", [P, L], c=c) for n in range(2)]
            proj = sb("proj", [P, L], c=c)
            b_parts = [sb(f"b_parts{n}", [P, L], BF16, c=c) for n in range(2)]
            c_cols = [sb(f"c_cols{n}", [P, NT, NS], c=c) for n in range(2)]
            places = sb("places", [K, L], c=c)
            bound = sb("bound", [K, 2], c=c)
            wx = sb("wx", [P, ND, P], c=c)
            wdt = sb("wdt", [P, D], c=c)
            bias = sb("bias", [P, ND], c=c)
            a_neg = sb("a_neg", [P, ND, NS], c=c)
            d_row = sb("d_row", [P, D], c=c)
            select = sb("select", [P, NS, P], BF16, c=c)
            pieces = sb("pieces", [P, 2, 512], c=c)
            soft = [pieces[:, n, :] for n in range(2)]
            in_cluster = pieces[0:K, :, :].rearrange("k m q -> k (m q)")
            stats = sb("y_stats", [P, NT, 6], c=c)
            moments = sb("y_moments", [P, NT, 2], c=c)
            var_eps = sb("y_var_eps", [P, NT], c=c)
            rstd = sb("y_rstd", [P, NT], c=c)
            shift = sb("y_shift", [P, NT], c=c)

            wloads = sem("scan_weights", c)
            made = sem("scan_consts", c)
            a_made = sem("scan_a", c)
            loaded = sem("scan_loaded", c)
            stored = [sem(f"scan_stored{n}", c) for n in range(2)]
            turned = sem("scan_turned", c)
            turned_out = sem("scan_turned_out", c)
            in_cluster_done = sem("scan_in_cluster", c)
            split = sem("scan_split", c)
            rests = sem("scan_rests", c)
            shifted = sem("scan_out_shift", c)
            softs = sem("scan_softs", c)
            soft_steps = sem("scan_soft_steps", c)
            deltas = sem("scan_deltas", c)
            driven = sem("scan_feat_times_delta", c)
            skipped = sem("scan_skip", c)
            b_spread = sem("scan_b_spread", c)
            b_ready = sem("scan_b_ready", c)
            decays = sem("scan_decays", c)
            drives = sem("scan_drives", c)
            scans = sem("scan_scans", c)
            states_turned = sem("scan_states_turned", c)
            added = sem("scan_added", c)
            stats_done = sem("scan_stats", c)
            moments_done = sem("scan_moments", c)
            var_done = sem("scan_var", c)
            pow_done = sem("scan_pow", c)
            normed = sem("scan_normed", c)
            chain = sem("scan_chain", c)
            turn = bank[0:2]
            b_ps = bank[2:4]
            state_ps = bank[4:8]
            BANKS = len(state_ps)
            HALVES = 2 * ND
            T_PROJ, T_C, T_DELTA = NT, NT + 2, NT + 4
            TURNS = NT + 4 + HALVES
            STEPS = [[0, 1], [2, 3], [4, 5], [6, 7], [T_PROJ], [T_PROJ + 1], [T_C, T_C + 1], [T_DELTA, T_DELTA + 1]]\
                + [[T_DELTA + g] for g in range(2, HALVES)]
            SKIP_STATE = 8
            NORMALISE_STATES = (4, 5)
            SPLIT_STATES = (9, 10, 11)
            POWER_STATE = 2
            ACT_LAG = 2
            assert len(STEPS) + ACT_LAG <= NS
            block = c.enter_context(nc.Block())

            @block.sync
            def _(sp):
                sp.dma_start(raw[:, :, :], row(xs_rows, 0)).then_inc(loaded, 16)
                for dst, src in (
                    (wx[:, :, :], w_x.rearrange("(c p) m -> p c m", p=P)),
                    (wdt[DT_ROW:DT_ROW + R, :], w_dt_t),
                    (bias[:, :], dt_bias.rearrange("(c p) -> p c", p=P)),
                    (a_neg[:, :, :], a_logs.rearrange("(c p) n -> p c n", p=P)),
                    (d_row[:, :], ds.partition_broadcast(P)),
                ):
                    sp.dma_start(dst, src, allow_slow_non_contiguous=True).then_inc(wloads, 16)

                def main(i, h, first, last):
                    seq = i * 2 + h
                    if not last:
                        sp.wait_ge(skipped, at(i, h, 1, 1))
                        sp.dma_start(raw[:, :, :], row(xs_rows, i * 2 + (h + 1))).then_inc(loaded, 16)
                    if not first:
                        store(i, h, i * 2 + (h - 1))
                    if last:
                        store(i, h + 1, seq)

                def store(i, h, seq):
                    sp.wait_ge(normed, at(i, h, NT, 0))
                    sp.dma_start(row(ys_rows, seq), acc[(h + 1) % 2][:, :, :]).then_inc(stored[(h + 1) % 2], 16)

                all_sequences(sp, main)
                for h in range(2):
                    sp.wait_ge(stored[h], 16 * PAIRS)

            @block.gpsimd
            def _(pool):
                pool.memset(select[:, :, :], 0.0).then_inc(made, 1)
                pool.memset(b_parts[0][:, :], 0.0).then_inc(made, 1)
                pool.memset(b_parts[1][:, :], 0.0).then_inc(made, 1)
                pool.iota(states[0][0:K, :].bitcast(I32), pattern=[[1, L]], base=0, channel_multiplier=0).then_inc(made, 1)
                pool.wait_ge(made, 4)
                pool.tensor_copy(places[:, :], states[0][0:K, :].bitcast(I32)).then_inc(made, 1)
                for part in range(3):
                    pool.affine_select(out=select[:, :, :], in_=select[:, :, :], compare_op=ALU.not_equal, fill=1.0,
                                       base=-32 * part, pattern=[[-1, NS], [0, P]],
                                       channel_multiplier=1).then_inc(made, 1)
                    pool.wait_ge(made, 6 + part)
                pool.sem_inc(drives, 2 * ND)

                def power(i, h):
                    pool.wait_ge(var_done, at(i, h, 1, 0))
                    pool.tensor_tensor(rstd[:, :], var_eps[:, :], neg_half[:, :], ALU.pow).then_inc(pow_done, 1)

                def main(i, h, first, last):
                    for n in range(NS):
                        pool.wait_ge(b_ready, at(i, h, NS, n + 2))
                        for c_ in range(ND):
                            g = n * ND + c_
                            if n == 0:
                                pool.wait_ge(driven, at(i, h, ND, c_ + 1))
                            pool.wait_ge(scans, at(i, h, ITEMS, g + 1))
                            pool.tensor_tensor(drive[g % 4][:, :], feat[h][:, c_, :], b_rows[n % 2][:, :],
                                               ALU.mult).then_inc(drives, 1)
                        if n == POWER_STATE and not first:
                            power(i, h)
                    if last:
                        power(i, h + 1)

                all_sequences(pool, main)

            @block.scalar
            def _(act):
                act.preload_act_table_set("natural_log_exp_and_others")
                act.sem_inc(turned_out, 2)
                act.sem_inc(b_ready, 1)

                def spread(i, h, n):
                    act.wait_ge(b_spread, at(i, h, NS, n + 1))
                    act.wait_ge(drives, at(i, h, ITEMS, ND * (n + 1)))
                    for m in range(2):
                        last = act.activation(b_rows[n % 2][:, m * 512:(m + 1) * 512], b_ps[m][:, :], ACT.Copy)
                    last.then_inc(b_ready, 1)

                def item(i, h, k):
                    ps = turn[k % 2]
                    act.wait_ge(turned, at(i, h, TURNS, k + 1))
                    if k < T_PROJ:
                        act.activation(feat[h % 2][:, :, k * P:(k + 1) * P],
                                       ps[:, :].rearrange("p (c q) -> p c q", c=ND), ACT.Copy).then_inc(turned_out, 1)
                    elif k < T_C:
                        m = k - T_PROJ
                        act.activation(proj[:, m * 512:(m + 1) * 512], ps[:, :], ACT.Copy).then_inc(turned_out, 1)
                    elif k < T_DELTA:
                        m = (k - T_C) * (NT // 2)
                        act.activation(c_cols[h % 2][:, m:m + NT // 2, :],
                                       ps[:, :].rearrange("p (t q) -> p t q", q=P)[:, :, C_ROW:C_ROW + NS],
                                       ACT.Copy).then_inc(turned_out, 1)
                    else:
                        g = k - T_DELTA
                        c_, m = g // 2, g % 2
                        act.wait_ge(deltas, at(i, h, HALVES, g + 1))
                        act.activation(soft[g % 2], ps[:, :], ACT.Abs,
                                       bias=bias[:, c_:c_ + 1]).then_inc(soft_steps, 1)
                        act.activation(delta[h % 2][:, c_, m * 512:(m + 1) * 512], ps[:, :], ACT.Relu,
                                       bias=bias[:, c_:c_ + 1]).then_inc(turned_out, 1)
                        act.wait_ge(soft_steps, at(i, h, 2 * HALVES, 2 * g + 1))
                        act.activation(soft[g % 2], soft[g % 2], ACT.Exp, scale=-1.0).then_inc(soft_steps, 1)
                        act.wait_ge(soft_steps, at(i, h, 2 * HALVES, 2 * g + 2))
                        act.activation(soft[g % 2], soft[g % 2], ACT.Ln, bias=one_bias[:, :])\
                           .then_inc(softs, 1)

                def split_b(i, h, n):
                    if n:
                        act.wait_ge(rests, at(i, h, 2, n))
                    rows = 96 - 32 * n
                    act.activation(b_parts[h % 2][0:rows, :], proj[0:rows, :], ACT.Copy).then_inc(split, 1)

                def normalise(i, h, m):
                    mine = acc[(h + 1) % 2]
                    act.wait_ge(shifted, at(i, h, 1, 0))
                    for t in range(m * NT // 2, (m + 1) * NT // 2):
                        act.activation(mine[:, t, :], mine[:, t, :], ACT.Identity, bias=shift[:, t:t + 1],
                                       scale=rstd[:, t:t + 1]).then_inc(normed, 1)

                def main(i, h, first, last):
                    before = not first
                    for n in range(NS):
                        for c_ in range(ND):
                            g = n * ND + c_
                            if n == 0:
                                act.wait_ge(deltas, at(i, h, HALVES, 2 * c_ + 2) + 2)
                            act.wait_ge(scans, at(i, h, ITEMS, g + 3))
                            act.activation(decay[g % 2][:, :], delta[h][:, c_, :], ACT.Exp,
                                           scale=a_neg[:, c_, n:n + 1]).then_inc(decays, 1)
                            if c_ == 1 and (n + 1 < NS or not last):
                                spread(i, h, n + 1)
                            if not last and 0 <= n - ACT_LAG < len(STEPS):
                                here = STEPS[n - ACT_LAG]
                                for k in {1: here[:1], ND - 1: here[1:]}.get(c_, []):
                                    item(i, h + 1, k)
                        if n in NORMALISE_STATES and before:
                            normalise(i, h, NORMALISE_STATES.index(n))
                        if n in SPLIT_STATES and not last:
                            split_b(i, h + 1, SPLIT_STATES.index(n))

                for k in range(T_PROJ):
                    item(0, 0, k)
                act.wait_ge(wloads, 80)
                flat_a = a_neg[:, :, :].rearrange("p c n -> p (c n)")
                act.activation(flat_a, flat_a, ACT.Exp).then_inc(a_made, 1)
                act.wait_ge(a_made, 1)
                act.activation(flat_a, flat_a, ACT.Copy, scale=-1.0).then_inc(a_made, 1)
                act.wait_ge(a_made, 2)
                for k in range(T_PROJ, T_DELTA):
                    item(0, 0, k)
                for n in range(3):
                    split_b(0, 0, n)
                for k in range(T_DELTA, TURNS):
                    item(0, 0, k)
                spread(0, 0, 0)
                all_sequences(act, main)
                for n in range(2):
                    normalise(PAIRS - 1, 2, n)

            @block.tensor
            def _(pe):
                pe.wait_ge(made, 8)
                pe.sem_inc(states_turned, 2 * NT)

                def spread(i, h, n):
                    pe.wait_ge(b_ready, at(i, h, NS, n + 1))
                    if n % NS == 0:
                        pe.wait_ge(split, at(i, h + n // NS, 3, 3))
                    for m in range(2):
                        last = pe.matmul(b_ps[m][:, :], select[:, n % NS, :],
                                         b_parts[(h + n // NS) % 2][:, m * 512:(m + 1) * 512], start=True, stop=True)
                    last.then_inc(b_spread, 1)

                def item(i, h, k):
                    ps = turn[k % 2]
                    if k == 0:
                        pe.wait_ge(loaded, at(i, h, 16, 16))
                    pe.wait_ge(turned_out, at(i, h, TURNS, k + 1))
                    if k < T_PROJ:
                        for c_ in range(ND):
                            last = pe.transpose(ps[:, c_ * P:(c_ + 1) * P], raw[:, k, c_ * P:(c_ + 1) * P], ident[:, :])
                    elif k < T_C:
                        m = k - T_PROJ
                        pe.wait_ge(turned_out, at(i, h, TURNS, T_PROJ) + 2)
                        for c_ in range(ND):
                            pe.matmul(ps[:, :], wx[:, c_, :], feat[h % 2][:, c_, m * 512:(m + 1) * 512],
                                      start=(c_ == 0), stop=False)
                        pe.wait_ge(in_cluster_done, at(i, h, 1, 1))
                        last = pe.matmul(ps[:, :], cluster_c[:, :], in_cluster[:, m * 512:(m + 1) * 512],
                                         start=False, stop=True)
                    elif k < T_DELTA:
                        pe.wait_ge(turned_out, at(i, h, TURNS, T_C) + 2)
                        for q in range(NT // 2):
                            t = (k - T_C) * (NT // 2) + q
                            last = pe.transpose(ps[:, q * P:(q + 1) * P], proj[:, t * P:(t + 1) * P], ident[:, :])
                    else:
                        g = k - T_DELTA
                        c_, m = g // 2, g % 2
                        pe.wait_ge(turned_out, at(i, h, TURNS, T_C) + 2)
                        last = pe.matmul(ps[:, :], wdt[DT_ROW:DT_ROW + R, c_ * P:(c_ + 1) * P],
                                         proj[DT_ROW:DT_ROW + R, m * 512:(m + 1) * 512], start=True, stop=True)
                    last.then_inc(turned, 1)

                def main(i, h, first, last):
                    for n in range(NS):
                        if n + 2 < NS or not last:
                            spread(i, h, n + 2)
                        pe.wait_ge(scans, at(i, h, ITEMS, ND * (n + 1) + 4))
                        for t in range(NT):
                            pe.wait_ge(added, at(i, h, NS * NT, n * NT + t + 1))
                            for c_ in range(ND):
                                end = pe.transpose(state_ps[t % BANKS][:, c_ * P:(c_ + 1) * P],
                                                   states[(n % 2) * ND + c_][:, t * P:(t + 1) * P], ident[:, :])
                            end.then_inc(states_turned, 1)
                        if not last and n < len(STEPS):
                            for k in STEPS[n]:
                                item(i, h + 1, k)

                for k in range(T_PROJ):
                    item(0, 0, k)
                pe.wait_ge(wloads, 80)
                for k in range(T_PROJ, TURNS):
                    item(0, 0, k)
                for n in range(2):
                    spread(0, 0, n)
                all_sequences(pe, main)

            @block.vector
            def _(dve):
                dve.wait_ge(made, 8)
                dve.sem_inc(deltas, 2)
                dve.sem_inc(scans, 4)
                dve.sem_inc(added, BANKS)

                def clusters(i, h):
                    dve.tensor_scalar(bound[:, :], bounds[:, bass.ds((i * 2 + h) * 2, 2)], 0.0, None,
                                      ALU.add).then_inc(chain, 1)
                    dve.wait_ge(chain, at(i, h, 2, 1))
                    dve.tensor_scalar(in_cluster, places[:, :], bound[:, 0:1], None, ALU.is_ge).then_inc(chain, 1)
                    dve.wait_ge(chain, at(i, h, 2, 2))
                    dve.scalar_tensor_tensor(out=in_cluster, in0=places[:, :], scalar=bound[:, 1:2],
                                             in1=in_cluster, op0=ALU.is_lt, op1=ALU.mult)\
                       .then_inc(in_cluster_done, 1)

                def take_rest(i, h, n):
                    rows = 64 - 32 * n
                    dve.wait_ge(split, at(i, h, 3, n + 1))
                    if n == 0:
                        dve.wait_ge(turned, at(i, h, TURNS, T_DELTA))
                    dve.tensor_tensor(proj[0:rows, :], proj[0:rows, :], b_parts[h % 2][0:rows, :], ALU.subtract)\
                       .then_inc(rests, 1)

                def step_size(i, h, g):
                    c_, m = g // 2, g % 2
                    dve.wait_ge(softs, at(i, h, HALVES, g + 1))
                    piece = delta[h % 2][:, c_, m * 512:(m + 1) * 512]
                    dve.tensor_tensor(piece, piece, soft[g % 2], ALU.add).then_inc(deltas, 1)
                    if m:
                        dve.wait_ge(turned, at(i, h, TURNS, T_DELTA))
                        dve.wait_ge(deltas, at(i, h, HALVES, g + 1) + 2)
                        dve.tensor_tensor(feat[h % 2][:, c_, :], feat[h % 2][:, c_, :], delta[h % 2][:, c_, :],
                                          ALU.mult).then_inc(driven, 1)

                def skip(i, h, wait_stored):
                    dve.wait_ge(turned, at(i, h, TURNS, T_PROJ))
                    if wait_stored:
                        dve.wait_ge(stored[h % 2], i * 16 + 16 * (h // 2))
                    dve.tensor_tensor(acc[h % 2][:, :, :], raw[:, :, :],
                                      d_row[:, :].unsqueeze(1).to_broadcast([P, NT, D]), ALU.mult).then_inc(skipped, 1)

                def scan(i, h, n, c_):
                    g = n * ND + c_
                    if c_ == 0:
                        dve.wait_ge(states_turned, at(i, h, NS * NT, (n + 1) * NT))
                    dve.wait_ge(decays, at(i, h, ITEMS, g + 1))
                    dve.wait_ge(drives, at(i, h, ITEMS, g + 1 + 2 * ND))
                    dve.tensor_tensor_scan(states[(n % 2) * ND + c_][:, :], decay[g % 2][:, :],
                                           drive[g % 4][:, :], 0.0, ALU.mult, ALU.add).then_inc(scans, 1)

                def add(i, h, n, c_):
                    if c_ == 0:
                        if n == 0:
                            dve.wait_ge(skipped, at(i, h, 1, 1))
                        else:
                            dve.wait_ge(added, at(i, h, NS * NT, n * NT + BANKS))
                    for t in range(c_ * NT // ND, (c_ + 1) * NT // ND):
                        dve.wait_ge(states_turned, at(i, h, NS * NT, n * NT + t + 1 + 2 * NT))
                        dve.scalar_tensor_tensor(out=acc[h % 2][:, t, :], in0=state_ps[t % BANKS][:, :],
                                                 scalar=c_cols[h % 2][:, t, n:n + 1], in1=acc[h % 2][:, t, :],
                                                 op0=ALU.mult, op1=ALU.add).then_inc(added, 1)

                def norm_stats(i, h):
                    mine = acc[(h + 1) % 2]
                    dve.wait_ge(added, at(i, h, NS * NT, BANKS))
                    for t in range(NT):
                        dve.bn_stats(stats[:, t, :], mine[:, t, :]).then_inc(stats_done, 1)
                    gate(dve, stats_done, at(i, h, NT, 0))
                    for t in range(NT):
                        dve.bn_aggr(moments[:, t, :], stats[:, t, :]).then_inc(moments_done, 1)
                    dve.wait_ge(moments_done, at(i, h, NT, 0))
                    dve.tensor_scalar(var_eps[:, :], moments[:, :, 1], LN_EPS, None, ALU.add).then_inc(var_done, 1)

                def out_shift(i, h):
                    dve.wait_ge(pow_done, at(i, h, 1, 0))
                    dve.scalar_tensor_tensor(out=shift[:, :], in0=moments[:, :, 0], scalar=-1.0, in1=rstd[:, :],
                                             op0=ALU.mult, op1=ALU.mult).then_inc(shifted, 1)

                def main(i, h, first, last):
                    for c_ in range(ND):
                        scan(i, h, 0, c_)
                        if not first:
                            add(i, h - 1, NS - 1, c_)
                    if not first:
                        norm_stats(i, h)
                    for n in range(1, NS):
                        for c_ in range(ND):
                            scan(i, h, n, c_)
                            add(i, h, n - 1, c_)
                        if n == POWER_STATE and not first:
                            out_shift(i, h)
                        if not last:
                            if n == 2:
                                clusters(i, h + 1)
                            if n in SPLIT_STATES[:2]:
                                take_rest(i, h + 1, SPLIT_STATES.index(n))
                            k = n - ACT_LAG
                            if 0 <= k < len(STEPS) and STEPS[k][0] >= T_DELTA:
                                for item in STEPS[k]:
                                    step_size(i, h + 1, item - T_DELTA)
                            if n == SKIP_STATE:
                                skip(i, h + 1, not first)
                    if last:
                        for c_ in range(ND):
                            add(i, h, NS - 1, c_)
                        norm_stats(i, h + 1)
                        out_shift(i, h + 1)

                clusters(0, 0)
                dve.wait_ge(wloads, 80)
                skip(0, 0, False)
                take_rest(0, 0, 0)
                take_rest(0, 0, 1)
                for g in range(HALVES):
                    step_size(0, 0, g)
                all_sequences(dve, main)

        with ExitStack() as c:
            T = 4
            U = B * NT // T
            RING = 4
            both = [sb(f"both{n}", [P, T, 2 * D], c=c) for n in range(RING)]
            ys = [sb(f"ys{n}", [P, T, D], c=c) for n in range(2)]
            result = [sb(f"result{n}", [P, T, D], c=c) for n in range(RING)]
            normed_x = [sb(f"normed_x{n}", [P, T, D], c=c) for n in range(2)]
            xt = [sb(f"xt_l{n}", [P, ND, T * P], c=c) for n in range(2)]
            hidden = [sb(f"hidden{n}", [P, FL, T * P], c=c) for n in range(2)]
            w1 = sb("l_w1_sb", [P, ND, FL * P], c=c)
            w2 = sb("l_w2_sb", [P, FL, D], c=c)
            gamma = sb("l_gamma_sb", [P, ND], c=c)
            b1 = sb("l_b1_sb", [P, FL], c=c)
            b2 = sb("l_b2_sb", [P, D], c=c)
            route = sb("route_sb", [P, D], c=c)
            product = sb("row_times_route", [P, T, D], c=c)
            dots = sb("dots", [P, T], c=c)
            stats = sb("x1_stats", [P, T, 6], c=c)
            moments = sb("x1_moments", [P, T, 2], c=c)
            var_eps = sb("x1_var_eps", [P, T], c=c)
            rstd = sb("x1_rstd", [P, T], c=c)
            std = sb("x1_std", [P, T], c=c)
            norm = [sb(f"x1_norm{n}", [P, T], c=c) for n in range(RING)]
            rnorm = sb("x1_rnorm", [P, T], c=c)
            scale = [sb(f"x1_scale{n}", [P, T], c=c) for n in range(2)]
            shift = [sb(f"x1_shift{n}", [P, T], c=c) for n in range(2)]
            o_stats = sb("lo_stats", [P, T, 6], c=c)
            o_moments = sb("lo_moments", [P, T, 2], c=c)
            o_var_eps = sb("lo_var_eps", [P, T], c=c)
            o_rstd = sb("lo_rstd", [P, T], c=c)
            o_shift = sb("lo_shift", [P, T], c=c)
            index = [sb(f"index{n}", [P, T], U32, c=c) for n in range(RING)]

            wloads = sem("light_weights", c)
            folded = sem("light_gamma_folded", c)
            loaded = [sem(f"light_loaded{n}", c) for n in range(RING)]
            gathered = [sem(f"light_gathered{n}", c) for n in range(2)]
            kept = [sem(f"light_kept{n}", c) for n in range(RING)]
            written = [sem(f"light_written{n}", c) for n in range(RING)]
            indexed = sem("light_indexed", c)
            summed = sem("light_summed", c)
            stats_done = sem("light_stats", c)
            moments_done = sem("light_moments", c)
            var_done = sem("light_var", c)
            pow_done = sem("light_pow", c)
            scaled = sem("light_scaled", c)
            normed = sem("light_normed", c)
            turned = sem("light_turned", c)
            turned_sb = sem("light_turned_sb", c)
            hidden_ps = sem("light_hidden_ps", c)
            hidden_sb = sem("light_hidden_sb", c)
            dotted = sem("light_dotted", c)
            light_ps = sem("light_out_ps", c)
            light_sb = sem("light_out_sb", c)
            o_stats_done = sem("light_out_stats", c)
            o_moments_done = sem("light_out_moments", c)
            o_var_done = sem("light_out_var", c)
            o_pow_done = sem("light_out_pow", c)
            o_shifted = sem("light_out_shift", c)
            light_n = sem("light_out_normed", c)
            out_ready = sem("light_out_ready", c)
            chain = sem("light_chain", c)
            turn = bank[0:2]
            hid = bank[2:4]
            lout = bank[4:8]
            x_units = x.rearrange("b (g t p) d -> (b g) p t d", t=T, p=P)
            out_units = out.rearrange("b (g t p) d -> (b g) p t d", t=T, p=P)
            xl_units = xl_dram.rearrange("(u t p) d -> u p t d", t=T, p=P)
            block = c.enter_context(nc.Block())

            def nth(i, u, per, k):
                return i * (RING * per) + (per * u + k)

            def dma(i, u, per):
                return i * (16 * per) + 16 * per * (u // RING + 1)

            def all_units(eng, main):
                for u in range(RING):
                    main(0, u, u, RING)
                with eng.Fori(1, U // RING - 1) as i:
                    for u in range(RING):
                        main(i, u, RING, RING)
                for u in range(RING):
                    main(U // RING - 1, u, RING, RING - 1 - u)

            @block.sync
            def _(sp):
                def load(i, u):
                    sp.dma_start(both[u % RING][:, :, 0:D], row(x_units, i * RING + u)).then_inc(loaded[u % RING], 16)

                for u in range(3):
                    load(0, u)
                for dst, src in (
                    (w1[:, :, :], l_w1.rearrange("(c p) f -> p c f", p=P)),
                    (w2[:, :, :], l_w2.rearrange("(c p) f -> p c f", p=P)),
                    (gamma[:, :], l_gamma.rearrange("(c p) -> p c", p=P)),
                    (b1[:, :], l_b1.rearrange("(c p) -> p c", p=P)),
                    (b2[:, :], l_b2.partition_broadcast(P)),
                    (route[:, :], routing.partition_broadcast(P)),
                ):
                    sp.dma_start(dst, src, allow_slow_non_contiguous=True).then_inc(wloads, 16)

                def write(i, u):
                    n = (u - 1) % RING
                    sp.wait_ge(out_ready, nth(i, u, 1, 0))
                    sp.dma_start(row(out_units, i * RING + (u - 1)), result[n][:, :, :]).then_inc(written[n], 16)

                def main(i, u, before, left):
                    if before:
                        write(i, u)
                    if left >= 3:
                        if before:
                            sp.wait_ge(kept[(u + 3) % RING], dma(i, u - 1, 1))
                        if before >= 2:
                            sp.wait_ge(written[(u + 2) % RING], dma(i, u - 2, 1))
                        load(i, u + 3)
                    sp.wait_ge(light_sb, nth(i, u, T, T) + T)
                    sp.dma_start(row(xl_units, i * RING + u), both[u][:, :, :]).then_inc(kept[u], 16)
                    if left == 0:
                        write(i, u + 1)

                all_units(sp, main)
                for n in range(RING):
                    sp.wait_ge(written[n], 16 * U // RING)
                    sp.wait_ge(kept[n], 16 * U // RING)

            @block.gpsimd
            def _(pool):
                def gather(i, u, reused):
                    gate(pool, indexed, nth(i, u, 1, 1))
                    if reused:
                        gate(pool, summed, nth(i, u, T, -T))
                    for t in range(T):
                        pool.indirect_dma_start(ys[u % 2][:, t, :], None, ys_dram,
                                                bass.IndirectOffsetOnAxis(index[u % RING][:, t:t + 1], 0))\
                            .then_inc(gathered[u % 2], 16)

                def powers(i, u):
                    pool.wait_ge(var_done, nth(i, u, 1, 1))
                    pool.tensor_tensor(rstd[:, :], var_eps[:, :], neg_half[:, 0:T], ALU.pow).then_inc(pow_done, 1)
                    pool.tensor_tensor(std[:, :], moments[:, :, 1], half[:, 0:T], ALU.pow).then_inc(pow_done, 1)

                def out_power(i, u):
                    pool.wait_ge(o_var_done, nth(i, u, 1, 0))
                    pool.tensor_tensor(o_rstd[:, :], o_var_eps[:, :], neg_half[:, 0:T], ALU.pow).then_inc(o_pow_done, 1)

                def finish(i, u):
                    n = (u - 1) % RING
                    pool.wait_ge(light_n, nth(i, u, T, 0))
                    pool.tensor_tensor(result[n][:, :, :], result[n][:, :, :], both[n][:, :, 0:D], ALU.add).then_inc(out_ready, 1)

                def main(i, u, before, left):
                    if before:
                        out_power(i, u)
                    if left >= 3:
                        gather(i, u + 3, True)
                    if left >= 2:
                        powers(i, u + 2)
                    if before:
                        finish(i, u)
                    if left == 0:
                        out_power(i, u + 1)
                        finish(i, u + 1)

                for u in range(2):
                    gather(0, u, False)
                for u in range(2):
                    powers(0, u)
                gather(0, 2, True)
                all_units(pool, main)

            @block.scalar
            def _(act):
                act.sem_inc(turned_sb, 2)
                act.sem_inc(hidden_sb, 2)

                def norm_in(i, u):
                    act.wait_ge(scaled, nth(i, u, 2, 2))
                    for t in range(T):
                        act.activation(normed_x[u % 2][:, t, :], both[u % RING][:, t, 0:D], ACT.Identity,
                                       bias=shift[u % 2][:, t:t + 1], scale=scale[u % 2][:, t:t + 1]).then_inc(normed, 1)

                def turn_out(i, u):
                    for t in range(T):
                        act.wait_ge(turned, nth(i, u, T, t + 1))
                        act.activation(xt[u % 2][:, :, t * P:(t + 1) * P],
                                       turn[t % 2][:, :].rearrange("p (c q) -> p c q", c=ND),
                                       ACT.Copy).then_inc(turned_sb, 1)

                def norm_out(i, u):
                    n = (u - 1) % RING
                    act.wait_ge(o_shifted, nth(i, u, 1, 0))
                    for t in range(T):
                        act.activation(result[n][:, t, :], both[n][:, t, D:2 * D], ACT.Identity,
                                       bias=o_shift[:, t:t + 1], scale=o_rstd[:, t:t + 1]).then_inc(light_n, 1)

                def main(i, u, before, left):
                    if before:
                        norm_out(i, u)
                    for f in range(FL):
                        act.wait_ge(hidden_ps, nth(i, u, FL, f + 1))
                        act.activation(hidden[u % 2][:, f, :], hid[f % 2][:, :], ACT.Gelu,
                                       bias=b1[:, f:f + 1]).then_inc(hidden_sb, 1)
                    if left >= 1:
                        turn_out(i, u + 1)
                    if left >= 2:
                        norm_in(i, u + 2)
                    if left == 0:
                        norm_out(i, u + 1)

                norm_in(0, 0)
                norm_in(0, 1)
                turn_out(0, 0)
                act.wait_ge(wloads, 96)
                all_units(act, main)

            @block.tensor
            def _(pe):
                def turn_tiles(i, u):
                    for t in range(T):
                        pe.wait_ge(normed, nth(i, u, T, t + 1))
                        pe.wait_ge(turned_sb, nth(i, u, T, t + 1))
                        for c_ in range(ND):
                            last = pe.transpose(turn[t % 2][:, c_ * P:(c_ + 1) * P],
                                                normed_x[u % 2][:, t, c_ * P:(c_ + 1) * P], ident[:, :])
                        last.then_inc(turned, 1)

                def main(i, u, before, left):
                    pe.wait_ge(turned_sb, nth(i, u, T, T) + 2)
                    for f in range(FL):
                        pe.wait_ge(hidden_sb, nth(i, u, FL, f + 1))
                        for c_ in range(ND):
                            last = pe.matmul(hid[f % 2][:, :], w1[:, c_, f * P:(f + 1) * P],
                                             xt[u % 2][:, c_, :], start=(c_ == 0), stop=(c_ == ND - 1))
                        last.then_inc(hidden_ps, 1)
                    if left >= 1:
                        turn_tiles(i, u + 1)
                    pe.wait_ge(hidden_sb, nth(i, u, FL, FL) + 2)
                    for t in range(T):
                        pe.wait_ge(light_sb, nth(i, u, T, t + 1))
                        for f in range(FL):
                            last = pe.matmul(lout[t][:, :], hidden[u % 2][:, f, t * P:(t + 1) * P],
                                             w2[:, f, :], start=(f == 0), stop=(f == FL - 1))
                        last.then_inc(light_ps, 1)

                turn_tiles(0, 0)
                pe.wait_ge(folded, ND)
                all_units(pe, main)

            @block.vector
            def _(dve):
                def places(i, u):
                    dve.tensor_scalar(index[u % RING][:, :], positions[:, bass.ds(i * (RING * T) + u * T, T)], 0.0,
                                      None, ALU.add).then_inc(indexed, 1)

                def sum_stats(i, u):
                    mine = both[u % RING]
                    dve.wait_ge(loaded[u % RING], dma(i, u, 1))
                    dve.wait_ge(gathered[u % 2], i * (16 * T * RING // 2) + 16 * T * (u // 2 + 1))
                    for t in range(T):
                        dve.tensor_tensor(mine[:, t, 0:D], mine[:, t, 0:D], ys[u % 2][:, t, :],
                                          ALU.add).then_inc(summed, 1)
                    for t in range(T):
                        gate(dve, summed, nth(i, u, T, t + 1))
                        dve.bn_stats(stats[:, t, :], mine[:, t, 0:D]).then_inc(stats_done, 1)
                    gate(dve, stats_done, nth(i, u, T, T))
                    for t in range(T):
                        dve.bn_aggr(moments[:, t, :], stats[:, t, :]).then_inc(moments_done, 1)
                    dve.wait_ge(moments_done, nth(i, u, T, T))
                    dve.tensor_scalar(var_eps[:, :], moments[:, :, 1], LN_EPS, None, ALU.add).then_inc(var_done, 1)

                def scales(i, u, reused):
                    if reused:
                        dve.wait_ge(normed, nth(i, u, T, -T))
                    links = [0]

                    def link(ins):
                        links[0] += 1
                        ins.then_inc(chain, 1)
                        dve.wait_ge(chain, nth(i, u, 3, links[0]))

                    mine = norm[u % RING]
                    dve.wait_ge(pow_done, nth(i, u, 2, 2))
                    link(dve.scalar_tensor_tensor(out=mine[:, :], in0=std[:, :], scalar=SQRT_D, in1=rstd[:, :],
                                                  op0=ALU.mult, op1=ALU.mult))
                    link(dve.tensor_scalar(mine[:, :], mine[:, :], NORM_EPS, 1.0 / SQRT_D, ALU.max, ALU.mult))
                    link(dve.reciprocal(rnorm[:, :], mine[:, :]))
                    dve.tensor_tensor(scale[u % 2][:, :], rstd[:, :], rnorm[:, :], ALU.mult).then_inc(scaled, 1)
                    dve.wait_ge(scaled, nth(i, u, 2, 1))
                    dve.scalar_tensor_tensor(out=shift[u % 2][:, :], in0=moments[:, :, 0], scalar=-1.0,
                                             in1=scale[u % 2][:, :], op0=ALU.mult, op1=ALU.mult).then_inc(scaled, 1)

                def route_dots(i, u):
                    for t in range(T):
                        dve.wait_ge(normed, nth(i, u, T, t + 1))
                        dve.scalar_tensor_tensor(out=product[:, t, :], in0=normed_x[u % 2][:, t, :], scalar=1.0,
                                                 in1=route[:, :], op0=ALU.mult, op1=ALU.mult,
                                                 accum_out=dots[:, t:t + 1]).then_inc(dotted, 1)

                def route_scores(i, u):
                    gate(dve, dotted, nth(i, u, T, T))
                    dve.tensor_tensor(scores[:, bass.ds(i * (RING * T) + u * T, T)], dots[:, :],
                                      norm[u % RING][:, :], ALU.mult)

                def out_shift(i, u):
                    dve.wait_ge(o_pow_done, nth(i, u, 1, 0))
                    dve.scalar_tensor_tensor(out=o_shift[:, :], in0=o_moments[:, :, 0], scalar=-1.0,
                                             in1=o_rstd[:, :], op0=ALU.mult, op1=ALU.mult).then_inc(o_shifted, 1)

                def main(i, u, before, left):
                    if before:
                        out_shift(i, u)
                    if left >= 3:
                        places(i, u + 3)
                    if left >= 2:
                        sum_stats(i, u + 2)
                    if left >= 1:
                        route_dots(i, u + 1)
                    if left >= 2:
                        scales(i, u + 2, True)
                    if left >= 1:
                        route_scores(i, u + 1)
                    mine = both[u % RING]
                    for t in range(T + 1):
                        if t < T:
                            dve.wait_ge(light_ps, nth(i, u, T, t + 1))
                            dve.tensor_tensor(mine[:, t, D:2 * D], lout[t][:, :], b2[:, :], ALU.add)\
                               .then_inc(light_sb, 1)
                        if t:
                            gate(dve, light_sb, nth(i, u, T, t) + T)
                            dve.bn_stats(o_stats[:, t - 1, :], mine[:, t - 1, D:2 * D]).then_inc(o_stats_done, 1)
                    gate(dve, o_stats_done, nth(i, u, T, T))
                    for t in range(T):
                        dve.bn_aggr(o_moments[:, t, :], o_stats[:, t, :]).then_inc(o_moments_done, 1)
                    dve.wait_ge(o_moments_done, nth(i, u, T, T))
                    dve.tensor_scalar(o_var_eps[:, :], o_moments[:, :, 1], LN_EPS, None, ALU.add).then_inc(o_var_done, 1)
                    if left == 0:
                        out_shift(i, u + 1)

                dve.sem_inc(light_sb, T)
                for u in range(3):
                    places(0, u)
                for u in range(2):
                    sum_stats(0, u)
                    scales(0, u, False)
                dve.wait_ge(wloads, 96)
                for c_ in range(ND):
                    dve.tensor_scalar(w1[:, c_, :], w1[:, c_, :], gamma[:, c_:c_ + 1], None, ALU.mult)\
                       .then_inc(folded, 1)
                route_dots(0, 0)
                route_scores(0, 0)
                all_units(dve, main)

        w1_hi = sb("h_w1_hi", [P, ND, FH * P], F32R)
        w1_lo = sb("h_w1_lo", [P, ND, FH * P], F32R)
        w2_hi = sb("h_w2_hi", [P, FH, D], F32R)
        w2_lo = sb("h_w2_lo", [P, FH, D], F32R)
        listed = sb("listed", [P, (B + 2) * NJ], U32)
        weights = sb("weights", [P, B * NJ])
        with ExitStack() as c:
            same = sb("same", [P, NT * B], c=c)
            prior = sb("prior", [P, NT * B], c=c)
            s_rows = sb("s_rows", [P, P], c=c)
            clipped = sb("clipped", [P, P], c=c)
            expd = sb("expd", [P, P], c=c)
            top = sb("top", [P, 1], c=c)
            top_row = sb("top_row", [1, B, NT], c=c)
            top_seq = sb("top_seq", [1, B], c=c)
            top_all = sb("top_all", [P, 1], c=c)
            cap = sb("cap", [P, 1], c=c)
            shift = sb("shift", [P, 1], c=c)
            part = sb("part", [P, 1], c=c)
            log_sum = sb("log_sum", [P, 1], c=c)
            gap = sb("gap", [P, P], c=c)
            better = sb("better", [P, P], c=c)
            equal = sb("equal", [P, P], c=c)
            count = sb("count", [P, 2], c=c)
            bit = sb("bit", [P, 1], I32, c=c)
            trial = sb("trial", [P, 1], I32, c=c)
            keep = sb("keep", [P, 1], I32, c=c)
            limit = sb("limit", [P, 1], I32, c=c)
            zeros = sb("zeros_r", [P, P], c=c)
            run_eq = sb("run_eq", [P, P], c=c)
            room = sb("room", [P, 1], c=c)
            picked = sb("picked", [P, P], c=c)
            slot = sb("slot", [P, P], c=c)
            straight = sb("straight", [P, P], c=c)
            slot_t = sb("slot_t", [P, P], c=c)
            TAGS = 5
            tagged = sb("tagged", [P, NT * B, TAGS], BF16, c=c)
            tile_row = sb("tile_row", [P, NT * B], I32, c=c)
            row_in_tile = sb("row_in_tile", [P, NT * B], I32, c=c)
            rest = [sb(f"weight_rest{n}", [P, P], c=c) for n in range(3)]
            found = sb("found", [P, NJ, B, TAGS], c=c)
            weight_sum = sb("weight_sum", [P, NJ, B], c=c)
            slots_i = sb("slots_i", [P, NUM_HEAVY], I32, c=c)
            slots = sb("slots", [P, NUM_HEAVY], c=c)
            takes = [sb(f"takes{n}", [P, NUM_HEAVY], BF16, c=c) for n in range(2 * NT)]

            W_STAGES = 2 * ND
            staging = [sb(f"w_staging{n}", [P, FH * P], c=c) for n in range(2)]
            gamma = sb("h_gamma_sb", [P, ND], c=c)
            w_parts = []
            for hi, lo in ((w1_hi, w1_lo), (w2_hi, w2_lo)):
                k = hi.shape[1] // ND
                for m in range(ND):
                    w_parts.append([w[:, m * k:(m + 1) * k, :].rearrange("p a b -> p (a b)") for w in (hi, lo)])

            gamma_loaded = sem("heavy_gamma_loaded", c)
            staged = [sem(f"heavy_staged{n}", c) for n in range(2)]
            folded = sem("heavy_gamma_folded", c)
            w_hi = sem("heavy_weights_hi", c)
            w_lo = sem("heavy_weights_lo", c)
            made = sem("route_consts", c)
            chain = sem("route_chain", c)
            pe_done = sem("route_pe", c)
            shifted = sem("route_shifted", c)
            expds = sem("route_expds", c)
            sums = sem("route_sums", c)
            logs = sem("route_logs", c)
            caps = sem("route_caps", c)
            gaps = sem("route_gaps", c)
            score_exp = sem("route_score_exp", c)
            counts = sem("route_counts", c)
            totals = sem("route_totals", c)
            limits = sem("route_limits", c)
            bits = sem("route_bits", c)
            taken = sem("route_taken", c)
            lists = sem("route_lists", c)
            block = c.enter_context(nc.Block())

            @block.sync
            def _(sp):
                sp.dma_start(gamma[:, :], h_gamma.rearrange("(c p) -> p c", p=P),
                             allow_slow_non_contiguous=True).then_inc(gamma_loaded, 16)
                views = [w.rearrange("(c p) f -> p c f", p=P) for w in (h_w1, h_w2)]
                for n in range(W_STAGES):
                    if n >= 2:
                        sp.wait_ge(w_lo, n - 1)
                    view = views[n // ND]
                    k = view.shape[1] // ND
                    sp.dma_start(staging[n % 2][:, :].rearrange("p (c f) -> p c f", c=k),
                                 view[:, (n % ND) * k:(n % ND + 1) * k, :]).then_inc(staged[n % 2], 16)

            @block.gpsimd
            def _(pool):
                pool.memset(same[:, :], 1.0).then_inc(made, 1)
                pool.memset(listed[:, B * NJ:(B + 2) * NJ], 0)
                pool.memset(zeros[:, :], 0.0).then_inc(made, 1)
                pool.memset(limit[:, :], 0).then_inc(made, 1)
                pool.memset(bit[:, :], 1 << 30).then_inc(made, 1)
                pool.memset(cap[:, :], -(LOG_K - math.log(L))).then_inc(made, 1)
                pool.iota(slots_i[:, :], pattern=[[1, NUM_HEAVY]], base=0, channel_multiplier=0).then_inc(made, 1)
                pool.iota(tile_row[:, :], pattern=[[P, NT * B]], base=0, channel_multiplier=0).then_inc(made, 1)
                pool.iota(row_in_tile[:, :], pattern=[[0, NT * B]], base=0, channel_multiplier=1).then_inc(made, 1)
                pool.wait_ge(made, 8)
                v = same[:, :].rearrange("p (b t) -> p b t", t=NT)
                pool.affine_select(out=v, in_=v, compare_op=ALU.is_ge, fill=0.0, base=0,
                                   pattern=[[-NT, B], [0, NT]], channel_multiplier=1).then_inc(made, 1)
                pool.wait_ge(made, 9)
                pool.affine_select(out=v, in_=v, compare_op=ALU.is_ge, fill=0.0, base=NT - 1,
                                   pattern=[[NT, B], [0, NT]], channel_multiplier=-1).then_inc(made, 1)
                pool.wait_ge(made, 10)
                pool.affine_select(out=prior[:, :], in_=same[:, :], compare_op=ALU.is_gt, fill=0.0, base=0,
                                   pattern=[[1, NT * B]], channel_multiplier=-1).then_inc(made, 1)
                pool.tensor_copy(slots[:, :], slots_i[:, :]).then_inc(made, 1)
                pool.tensor_copy(tagged[:, :, 0], tile_row[:, :]).then_inc(made, 1)
                pool.tensor_copy(tagged[:, :, 1], row_in_tile[:, :]).then_inc(made, 1)
                for n in range(W_STAGES):
                    pool.wait_ge(w_hi, n + 1)
                    pool.tensor_tensor(w_parts[n][1], staging[n % 2][:, :], w_parts[n][0], ALU.subtract).then_inc(w_lo, 1)

            @block.scalar
            def _(act):
                act.preload_act_table_set("natural_log_exp_and_others")
                with act.Fori(0, DESCENT_STEPS - 1) as j:
                    act.wait_ge(shifted, j * 2 + 2)
                    act.activation(expd[:, :], clipped[:, :], ACT.Exp, bias=shift[:, :],
                                   accum_out=part[:, :]).then_inc(expds, 1)
                    act.wait_ge(sums, j + 1)
                    act.activation(log_sum[:, :], bank[1][:, 0:1], ACT.Ln).then_inc(logs, 1)
                act.wait_ge(gaps, 2)
                act.activation(expd[:, :], clipped[:, :], ACT.Exp).then_inc(score_exp, 1)
                act.wait_ge(gamma_loaded, 16)
                for n in range(W_STAGES):
                    act.wait_ge(staged[n % 2], 16 * (n // 2) + 16)
                    if n < ND:
                        act.activation(staging[n % 2][:, :], staging[n % 2][:, :], ACT.Copy,
                                       scale=gamma[:, n:n + 1]).then_inc(folded, 1)
                        act.wait_ge(folded, n + 1)
                    act.activation(w_parts[n][0], staging[n % 2][:, :], ACT.Copy).then_inc(w_hi, 1)

            @block.tensor
            def _(pe):
                pe.wait_ge(made, 14)
                pe.transpose(bank[0][:, 0:P], scores[:, :], ident[:, :]).then_inc(pe_done, 1)
                pe.wait_ge(chain, 2)
                pe.transpose(bank[0][0:1, 0:P], top[:, :], ident[:, :]).then_inc(pe_done, 1)
                pe.wait_ge(chain, 4)
                pe.matmul(bank[0][:, 0:1], top_row[:, :, :].rearrange("p b t -> p (b t)"), ones[0:1, 0:1],
                          start=True, stop=True).then_inc(pe_done, 1)
                with pe.Fori(0, DESCENT_STEPS - 1) as j:
                    pe.wait_ge(expds, j + 1)
                    pe.matmul(bank[1][:, 0:1], same[:, :], part[:, :], start=True, stop=True).then_inc(sums, 1)
                with pe.Fori(0, 31) as j:
                    pe.wait_ge(counts, j + 1)
                    pe.matmul(bank[2][:, 0:1], same[:, :], count[:, 0:1], start=True, stop=True).then_inc(totals, 1)
                pe.wait_ge(counts, 33)
                pe.matmul(bank[2][:, 2:3], same[:, :], count[:, 0:1], start=True, stop=True)
                pe.matmul(bank[2][:, 3:4], prior[:, :], count[:, 1:2], start=True, stop=True).then_inc(pe_done, 1)
                pe.wait_ge(counts, 34)
                pe.matmul(bank[2][:, 4:5], prior[:, :], count[:, 0:1], start=True, stop=True).then_inc(pe_done, 1)
                pe.wait_ge(caps, DESCENT_STEPS + 1)
                pe.transpose(bank[3][:, 0:P], slot[:, :], ident[:, :])
                pe.transpose(bank[3][:, P:2 * P], straight[:, :], ident[:, :]).then_inc(pe_done, 1)
                pe.wait_ge(caps, DESCENT_STEPS + 2)
                for b in range(B):
                    pe.wait_ge(taken, NT * (b + 1))
                    for j in range(NJ):
                        for t in range(NT):
                            last = pe.matmul(bank[4 + j][:, TAGS * b:TAGS * (b + 1)],
                                             takes[(b % 2) * NT + t][:, j * P:(j + 1) * P],
                                             tagged[:, b * NT + t, :], start=(t == 0), stop=(t == NT - 1))
                    last.then_inc(lists, 1)

            @block.vector
            def _(dve):
                links = [0]

                def link(ins):
                    links[0] += 1
                    ins.then_inc(chain, 1)
                    dve.wait_ge(chain, links[0])

                dve.wait_ge(made, 14)
                dve.wait_ge(pe_done, 1)
                link(dve.tensor_copy(s_rows[:, :], bank[0][:, 0:P]))
                link(dve.tensor_reduce(top[:, :], s_rows[:, :], AX, ALU.max))
                dve.wait_ge(pe_done, 2)
                link(dve.tensor_reduce(top_seq[:, :], bank[0][0:1, 0:P].rearrange("p (b t) -> p b t", t=NT), AX, ALU.max))
                link(dve.tensor_scalar(top_row[:, :, :], top_seq[:, :].unsqueeze(2).to_broadcast([1, B, NT]), 0.0, None,
                                       ALU.add))
                dve.wait_ge(pe_done, 3)
                dve.tensor_copy(top_all[:, :], bank[0][:, 0:1]).then_inc(caps, 1)
                dve.wait_ge(caps, 1)
                with dve.Fori(0, DESCENT_STEPS - 1) as j:
                    dve.tensor_scalar(shift[:, :], top_all[:, :], cap[:, :], -1.0, ALU.min, ALU.mult).then_inc(shifted, 1)
                    dve.tensor_scalar(clipped[:, :], s_rows[:, :], cap[:, :], None, ALU.min).then_inc(shifted, 1)
                    dve.wait_ge(logs, j + 1)
                    dve.tensor_scalar(cap[:, :], log_sum[:, :], shift[:, :], LOG_K, ALU.subtract, ALU.subtract)\
                       .then_inc(caps, 1)
                    gate(dve, caps, j + 2)
                dve.tensor_scalar(clipped[:, :], s_rows[:, :], cap[:, :], 0.0, ALU.subtract, ALU.min).then_inc(gaps, 1)
                dve.wait_ge(gaps, 1)
                dve.tensor_scalar(gap[:, :], clipped[:, :], -1.0, 104.0, ALU.mult, ALU.min).then_inc(gaps, 1)
                dve.wait_ge(gaps, 2)
                with dve.Fori(0, 31) as j:
                    dve.tensor_tensor(trial[:, :], limit[:, :], bit[:, :], ALU.bitwise_or).then_inc(limits, 1)
                    dve.wait_ge(limits, j * 3 + 1)
                    dve.tensor_scalar(better[:, :], gap[:, :], trial[:, :].bitcast(F32), 0.0, ALU.is_lt, ALU.add,
                                      accum_out=count[:, 0:1]).then_inc(counts, 1)
                    dve.wait_ge(totals, j + 1)
                    dve.tensor_scalar(keep[:, :], bank[2][:, 0:1], float(NUM_HEAVY), -1.0, ALU.is_lt, ALU.mult)\
                       .then_inc(limits, 1)
                    dve.wait_ge(limits, j * 3 + 2)
                    dve.tensor_tensor(keep[:, :], keep[:, :], bit[:, :], ALU.bitwise_and).then_inc(limits, 1)
                    dve.wait_ge(limits, j * 3 + 3)
                    dve.tensor_tensor(limit[:, :], limit[:, :], keep[:, :], ALU.bitwise_or)
                    dve.tensor_scalar(bit[:, :], bit[:, :], 1, None, ALU.logical_shift_right).then_inc(bits, 1)
                    gate(dve, bits, j + 1)
                edge = limit[:, :].bitcast(F32)
                dve.tensor_scalar(better[:, :], gap[:, :], edge, 0.0, ALU.is_lt, ALU.add,
                                  accum_out=count[:, 0:1]).then_inc(counts, 1)
                dve.tensor_scalar(equal[:, :], gap[:, :], edge, 0.0, ALU.is_equal, ALU.add,
                                  accum_out=count[:, 1:2]).then_inc(counts, 1)
                dve.wait_ge(counts, 33)
                link(dve.tensor_tensor_scan(run_eq[:, :], equal[:, :], zeros[:, :], 0.0, ALU.add, ALU.add))
                dve.wait_ge(pe_done, 4)
                link(dve.tensor_scalar(room[:, :], bank[2][:, 2:3], -1.0, float(NUM_HEAVY), ALU.mult, ALU.add))
                link(dve.tensor_tensor(room[:, :], room[:, :], bank[2][:, 3:4], ALU.subtract))
                link(dve.tensor_scalar(run_eq[:, :], run_eq[:, :], room[:, :], None, ALU.is_le))
                link(dve.tensor_tensor(run_eq[:, :], run_eq[:, :], equal[:, :], ALU.mult))
                link(dve.tensor_tensor(picked[:, :], run_eq[:, :], better[:, :], ALU.add))
                dve.tensor_reduce(count[:, 0:1], picked[:, :], AX, ALU.add).then_inc(counts, 1)
                link(dve.tensor_tensor_scan(slot[:, :], picked[:, :], zeros[:, :], 0.0, ALU.add, ALU.add))
                dve.wait_ge(pe_done, 5)
                link(dve.tensor_scalar(slot[:, :], slot[:, :], bank[2][:, 4:5], None, ALU.add))
                link(dve.tensor_tensor(slot[:, :], slot[:, :], picked[:, :], ALU.mult))
                link(dve.tensor_scalar(slot[:, :], slot[:, :], -1.0, None, ALU.add))
                dve.wait_ge(score_exp, 1)
                link(dve.tensor_scalar(straight[:, :], expd[:, :], -1.0, 1.0, ALU.mult, ALU.add))
                dve.tensor_tensor(straight[:, :], straight[:, :], expd[:, :], ALU.add).then_inc(caps, 1)
                dve.wait_ge(pe_done, 6)
                link(dve.tensor_copy(slot_t[:, :], bank[3][:, 0:P]))
                link(dve.tensor_copy(rest[0][:, :], bank[3][:, P:2 * P]))
                for n in range(2):
                    link(dve.tensor_copy(tagged[:, :, 2 + n], rest[n][:, :]))
                    link(dve.tensor_tensor(rest[n + 1][:, :], rest[n][:, :], tagged[:, :, 2 + n], ALU.subtract))
                dve.tensor_copy(tagged[:, :, 4], rest[2][:, :]).then_inc(caps, 1)
                for b in range(B):
                    if b >= 2:
                        dve.wait_ge(lists, b - 1)
                    for t in range(NT):
                        g = b * NT + t
                        dve.tensor_scalar(takes[(b % 2) * NT + t][:, :], slots[:, :], slot_t[:, g:g + 1], None,
                                          ALU.is_equal).then_inc(taken, 1)
                dve.wait_ge(lists, B)
                for j in range(NJ):
                    copied = dve.tensor_copy(found[:, j, :, :].rearrange("p b e -> p (b e)"),
                                             bank[4 + j][:, 0:TAGS * B])
                link(copied)
                link(dve.tensor_tensor(weight_sum[:, :, :], found[:, :, :, 2], found[:, :, :, 3], ALU.add))
                for j in range(NJ):
                    dve.tensor_tensor(listed[:, 0:B * NJ].rearrange("p (b j) -> p b j", j=NJ)[:, :, j],
                                      found[:, j, :, 0], found[:, j, :, 1], ALU.add)
                    dve.tensor_tensor(weights[:, :].rearrange("p (b j) -> p b j", j=NJ)[:, :, j],
                                      weight_sum[:, j, :], found[:, j, :, 4], ALU.add)

        with ExitStack() as c:
            both = [sb(f"h_both{n}", [P, NJ, 2 * D], c=c) for n in range(2)]
            normed_x = sb("h_normed_x", [P, NJ, D], c=c)
            xt_hi = sb("h_xt_hi", [P, ND, 512], F32R, c=c)
            xt_lo = sb("h_xt_lo", [P, ND, 512], F32R, c=c)
            hidden = [sb(f"h_hidden{n}", [P, 512], c=c) for n in range(2)]
            hidden_hi = [sb(f"h_hidden_hi{n}", [P, 512], F32R, c=c) for n in range(2)]
            hidden_lo = [sb(f"h_hidden_lo{n}", [P, 512], F32R, c=c) for n in range(2)]
            b1 = sb("h_b1_sb", [P, FH], c=c)
            b2 = sb("h_b2_sb", [P, D], c=c)
            rows = [sb(f"rows{n}", [P, NJ], U32, c=c) for n in range(2)]
            weight = [sb(f"weight{n}", [P, NJ], c=c) for n in range(2)]
            stats = sb("h_stats", [P, NJ, 6], c=c)
            moments = sb("h_moments", [P, NJ, 2], c=c)
            var_eps = sb("h_var_eps", [P, NJ], c=c)
            rstd = sb("h_rstd", [P, NJ], c=c)
            std = sb("h_std", [P, NJ], c=c)
            norm = sb("h_norm", [P, NJ], c=c)
            rnorm = sb("h_rnorm", [P, NJ], c=c)
            scale = sb("h_scale", [P, NJ], c=c)
            o_stats = sb("ho_stats", [P, NJ, 6], c=c)
            o_moments = sb("ho_moments", [P, NJ, 2], c=c)
            o_var_eps = sb("ho_var_eps", [P, NJ], c=c)
            o_rstd = sb("ho_rstd", [P, NJ], c=c)

            small = sem("heavy_small_weights", c)
            indexed = sem("heavy_indexed", c)
            gathered = [sem(f"heavy_gathered{n}", c) for n in range(2)]
            scattered = [sem(f"heavy_scattered{n}", c) for n in range(2)]
            stats_done = sem("heavy_stats", c)
            moments_done = sem("heavy_moments", c)
            var_done = sem("heavy_var", c)
            pow_done = sem("heavy_pow", c)
            scaled = sem("heavy_scaled", c)
            normed = sem("heavy_normed", c)
            based = sem("heavy_light_and_bias", c)
            turned = sem("heavy_turned", c)
            turned_hi = sem("heavy_turned_hi", c)
            turned_lo = sem("heavy_turned_lo", c)
            hidden_ps = sem("heavy_hidden_ps", c)
            activated = sem("heavy_activated", c)
            his = sem("heavy_hidden_hi", c)
            los = sem("heavy_hidden_lo", c)
            used = sem("heavy_hidden_used", c)
            mixed = sem("heavy_mixed", c)
            o_stats_done = sem("heavy_out_stats", c)
            o_moments_done = sem("heavy_out_moments", c)
            o_var_done = sem("heavy_out_var", c)
            o_pow_done = sem("heavy_out_pow", c)
            out_n = sem("heavy_out_normed", c)
            out_ready = sem("heavy_out_ready", c)
            chain = sem("heavy_chain", c)
            turn = bank[0:2]
            hid = bank[2:4]
            outs = bank[4:8]
            STATS_OUT, FINISH, INDEX, STATS_IN, PREPARE = 1, 3, 5, 10, 12
            block = c.enter_context(nc.Block())

            @block.sync
            def _(sp):
                for dst, src in (
                    (b1[:, :], h_b1.rearrange("(c p) -> p c", p=P)),
                    (b2[:, :], h_b2.partition_broadcast(P)),
                ):
                    sp.dma_start(dst, src, allow_slow_non_contiguous=True).then_inc(small, 16)

            @block.gpsimd
            def _(pool):
                def gather(i, h):
                    gate(pool, indexed, at(i, h, 1, 1))
                    for j in range(NJ):
                        pool.indirect_dma_start(both[h % 2][:, j, :], None, xl_dram,
                                                bass.IndirectOffsetOnAxis(rows[h % 2][:, j:j + 1], 0))\
                            .then_inc(gathered[h % 2], 16)

                def powers(i, h):
                    pool.wait_ge(var_done, at(i, h, 1, 1))
                    pool.tensor_tensor(rstd[:, :], var_eps[:, :], neg_half[:, 0:NJ], ALU.pow).then_inc(pow_done, 1)
                    pool.tensor_tensor(std[:, :], moments[:, :, 1], half[:, 0:NJ], ALU.pow).then_inc(pow_done, 1)

                def out_power(i, h):
                    pool.wait_ge(o_var_done, at(i, h, 1, 0))
                    pool.tensor_tensor(o_rstd[:, :], o_var_eps[:, :], neg_half[:, 0:NJ], ALU.pow).then_inc(o_pow_done, 1)
                    gate(pool, out_ready, at(i, h, NJ, 0))
                    n = (h + 1) % 2
                    for j in range(NJ):
                        pool.indirect_dma_start(out_flat, bass.IndirectOffsetOnAxis(rows[n][:, j:j + 1], 0),
                                                both[n][:, j, D:2 * D], None).then_inc(scattered[n], 16)

                def main(i, h, first, last):
                    if not first:
                        out_power(i, h)
                    if not last:
                        gather(i, h + 1)
                        powers(i, h + 1)
                    else:
                        out_power(i, h + 1)

                gather(0, 0)
                powers(0, 0)
                all_sequences(pool, main)
                for n in range(2):
                    pool.wait_ge(scattered[n], 16 * NJ * PAIRS)

            @block.scalar
            def _(act):
                act.wait_ge(small, 32)

                def turn_hi(i, h, j):
                    act.wait_ge(turned, at(i, h, NJ, j + 1))
                    act.activation(xt_hi[:, :, j * P:(j + 1) * P], turn[j % 2][:, :].rearrange("p (c q) -> p c q", c=ND),
                                   ACT.Copy).then_inc(turned_hi, 1)

                def main(i, h, first, last):
                    for f in range(FH):
                        act.wait_ge(hidden_ps, at(i, h, FH, f + 1))
                        act.wait_ge(los, at(i, h, FH, f + 1))
                        act.activation(hidden[f % 2][:, :], hid[f % 2][:, :], ACT.Gelu,
                                       bias=b1[:, f:f + 1]).then_inc(activated, 1)
                        act.wait_ge(activated, at(i, h, FH, f + 1) + 2)
                        act.wait_ge(used, at(i, h, FH, f + 1))
                        act.activation(hidden_hi[f % 2][:, :], hidden[f % 2][:, :], ACT.Copy).then_inc(his, 1)
                    if not last:
                        for j in range(NJ):
                            turn_hi(i, h + 1, j)

                act.sem_inc(activated, 2)
                for j in range(NJ):
                    turn_hi(0, 0, j)
                all_sequences(act, main)

            @block.tensor
            def _(pe):
                def product(ps, lhs, rhs, steps):
                    count = 0
                    for a, b in steps:
                        for x_, y_ in ((0, 0), (0, 1), (1, 0)):
                            count += 1
                            last = pe.matmul(ps, a[x_], b[y_], start=lhs and count == 1,
                                             stop=rhs and count == 3 * len(steps))
                    return last

                def turn_tile(i, h, j):
                    pe.wait_ge(normed, at(i, h, NJ, j + 1))
                    pe.wait_ge(turned_lo, at(i, h, NJ, j + 1))
                    for c_ in range(ND):
                        last = pe.transpose(turn[j % 2][:, c_ * P:(c_ + 1) * P],
                                            normed_x[:, j, c_ * P:(c_ + 1) * P], ident[:, :])
                    last.then_inc(turned, 1)

                def first_layer(i, h, f):
                    if f == 0:
                        pe.wait_ge(turned_lo, at(i, h, NJ, NJ) + 2)
                    pe.wait_ge(activated, at(i, h, FH, f + 1))
                    cols = slice(f * P, (f + 1) * P)
                    product(hid[f % 2][:, :], True, True,
                            [((w1_hi[:, c_, cols], w1_lo[:, c_, cols]), (xt_hi[:, c_, :], xt_lo[:, c_, :]))
                             for c_ in range(ND)]).then_inc(hidden_ps, 1)

                def second_layer(i, h, f):
                    pe.wait_ge(los, at(i, h, FH, f + 1) + 2)
                    if f == 0:
                        pe.wait_ge(mixed, at(i, h, NJ, NJ))
                    for j in range(NJ):
                        cols = slice(j * P, (j + 1) * P)
                        last = product(outs[j][:, :], f == 0, f == FH - 1,
                                       [((hidden_hi[f % 2][:, cols], hidden_lo[f % 2][:, cols]),
                                         (w2_hi[:, f, :], w2_lo[:, f, :]))])
                    last.then_inc(used, 1)

                def main(i, h, first, last):
                    for f in range(FH + 2):
                        if f < FH:
                            first_layer(i, h, f)
                        if not last and FH - 1 <= f <= FH:
                            for j in ((0, 1), (2, 3))[f - (FH - 1)]:
                                turn_tile(i, h + 1, j)
                        if f >= 2:
                            second_layer(i, h, f - 2)

                pe.sem_inc(used, 2)
                for j in range(NJ):
                    turn_tile(0, 0, j)
                all_sequences(pe, main)

            @block.vector
            def _(dve):
                def index(i, h):
                    dve.tensor_scalar(rows[h % 2][:, :], listed[:, bass.ds((i * 2 + h) * NJ, NJ)], 0.0, None,
                                      ALU.add).then_inc(indexed, 1)

                def stats_in(i, h):
                    mine = both[h % 2]
                    gate(dve, gathered[h % 2], i * (16 * NJ) + 16 * NJ * (h // 2 + 1))
                    for j in range(NJ):
                        dve.bn_stats(stats[:, j, :], mine[:, j, 0:D]).then_inc(stats_done, 1)
                    gate(dve, stats_done, at(i, h, NJ, NJ))
                    for j in range(NJ):
                        dve.bn_aggr(moments[:, j, :], stats[:, j, :]).then_inc(moments_done, 1)
                    dve.wait_ge(moments_done, at(i, h, NJ, NJ))
                    dve.tensor_scalar(var_eps[:, :], moments[:, :, 1], LN_EPS, None, ALU.add).then_inc(var_done, 1)

                def prepare(i, h):
                    mine = both[h % 2]
                    links = [0]

                    def link(ins):
                        links[0] += 1
                        ins.then_inc(chain, 1)
                        dve.wait_ge(chain, at(i, h, 4, links[0]))

                    dve.wait_ge(pow_done, at(i, h, 2, 2))
                    link(dve.scalar_tensor_tensor(out=norm[:, :], in0=std[:, :], scalar=SQRT_D, in1=rstd[:, :],
                                                  op0=ALU.mult, op1=ALU.mult))
                    link(dve.tensor_scalar(norm[:, :], norm[:, :], NORM_EPS, 1.0 / SQRT_D, ALU.max, ALU.mult))
                    link(dve.reciprocal(rnorm[:, :], norm[:, :]))
                    dve.tensor_tensor(scale[:, :], rstd[:, :], rnorm[:, :], ALU.mult).then_inc(scaled, 1)
                    dve.wait_ge(scaled, at(i, h, 1, 1))
                    for j in range(NJ):
                        dve.tensor_scalar(normed_x[:, j, :], mine[:, j, 0:D], moments[:, j, 0:1],
                                          scale[:, j:j + 1], ALU.subtract, ALU.mult).then_inc(normed, 1)
                    link(dve.tensor_scalar(weight[h % 2][:, :], weights[:, bass.ds((i * 2 + h) * NJ, NJ)], 0.0, None,
                                           ALU.add))
                    for j in range(NJ):
                        dve.scalar_tensor_tensor(out=mine[:, j, D:2 * D], in0=b2[:, :],
                                                 scalar=weight[h % 2][:, j:j + 1], in1=mine[:, j, D:2 * D],
                                                 op0=ALU.mult, op1=ALU.add).then_inc(based, 1)

                def turn_lo(i, h, j):
                    dve.wait_ge(turned_hi, at(i, h, NJ, j + 1))
                    dve.tensor_tensor(xt_lo[:, :, j * P:(j + 1) * P],
                                      turn[j % 2][:, :].rearrange("p (c q) -> p c q", c=ND),
                                      xt_hi[:, :, j * P:(j + 1) * P], ALU.subtract).then_inc(turned_lo, 1)

                def mix(i, h):
                    n = (h + 1) % 2
                    dve.wait_ge(based, at(i, h, NJ, 0))
                    dve.wait_ge(used, at(i, h, FH, 0) + 2)
                    for j in range(NJ):
                        dve.scalar_tensor_tensor(out=both[n][:, j, D:2 * D], in0=outs[j][:, :],
                                                 scalar=weight[n][:, j:j + 1], in1=both[n][:, j, D:2 * D],
                                                 op0=ALU.mult, op1=ALU.add).then_inc(mixed, 1)

                def stats_out(i, h):
                    n = (h + 1) % 2
                    gate(dve, mixed, at(i, h, NJ, NJ))
                    for j in range(NJ):
                        dve.bn_stats(o_stats[:, j, :], both[n][:, j, D:2 * D]).then_inc(o_stats_done, 1)
                    gate(dve, o_stats_done, at(i, h, NJ, 0))
                    for j in range(NJ):
                        dve.bn_aggr(o_moments[:, j, :], o_stats[:, j, :]).then_inc(o_moments_done, 1)
                    dve.wait_ge(o_moments_done, at(i, h, NJ, 0))
                    dve.tensor_scalar(o_var_eps[:, :], o_moments[:, :, 1], LN_EPS, None, ALU.add).then_inc(o_var_done, 1)

                def finish(i, h):
                    n = (h + 1) % 2
                    dve.wait_ge(o_pow_done, at(i, h, 1, 0))
                    for j in range(NJ):
                        dve.tensor_scalar(both[n][:, j, D:2 * D], both[n][:, j, D:2 * D], o_moments[:, j, 0:1],
                                          o_rstd[:, j:j + 1], ALU.subtract, ALU.mult).then_inc(out_n, 1)
                    for j in range(NJ):
                        dve.wait_ge(out_n, at(i, h, NJ, j + 1 - NJ))
                        dve.tensor_tensor(both[n][:, j, D:2 * D], both[n][:, j, D:2 * D], both[n][:, j, 0:D],
                                          ALU.add).then_inc(out_ready, 1)

                def main(i, h, first, last):
                    if not first:
                        mix(i, h)
                    for f in range(FH):
                        dve.wait_ge(his, at(i, h, FH, f + 1))
                        dve.tensor_tensor(hidden_lo[f % 2][:, :], hidden[f % 2][:, :], hidden_hi[f % 2][:, :],
                                          ALU.subtract).then_inc(los, 1)
                        if f == STATS_OUT and not first:
                            stats_out(i, h)
                        if f == FINISH and not first:
                            finish(i, h)
                        if f == INDEX and not last:
                            if not first:
                                n = (h + 1) % 2
                                dve.wait_ge(scattered[n], i * (16 * NJ) + 16 * NJ * ((h + 1) // 2))
                            index(i, h + 1)
                        if f == STATS_IN and not last:
                            stats_in(i, h + 1)
                        if f == PREPARE and not last:
                            prepare(i, h + 1)
                    if not last:
                        for j in range(NJ):
                            turn_lo(i, h + 1, j)
                    else:
                        mix(i, h + 1)
                        stats_out(i, h + 1)
                        finish(i, h + 1)

                dve.sem_inc(turned_lo, 2)
                dve.sem_inc(los, 2)
                dve.sem_inc(mixed, NJ)
                index(0, 0)
                stats_in(0, 0)
                dve.wait_ge(small, 32)
                prepare(0, 0)
                for j in range(NJ):
                    turn_lo(0, 0, j)
                all_sequences(dve, main)


def kernel(**inputs):
    import numpy as np
    import concourse.bacc as bacc
    from concourse.bass_utils import run_bass_kernel_spmd as run

    g = {k: np.asarray(v) for k, v in inputs.items()}
    x = g["L0_attn_x"]
    rank = g["L0_attn_dt_projs_weight"].shape[1]
    states = g["L0_attn_A_logs"].shape[1]
    proj = g["L0_attn_x_proj_weight"].T
    w_x = np.zeros((proj.shape[0], P), proj.dtype)
    for n in range(3):
        w_x[:, 32 * n:32 * n + states] = proj[:, rank:rank + states]
    w_x[:, 64 + states:64 + 2 * states] = proj[:, rank + states:]
    w_x[:, 96:96 + rank] = proj[:, :rank]
    arrays = {
        "x": x, "means": g["L0_attn_means"], "means_t": g["L0_attn_means"].T,
        "prompt_t": g["L0_attn_prompt_weight"].T, "w_x": w_x,
        "w_dt_t": g["L0_attn_dt_projs_weight"].T, "dt_bias": g["L0_attn_dt_projs_bias"],
        "a_logs": g["L0_attn_A_logs"], "ds": g["L0_attn_Ds"],
        "routing": g["L0_ffn_routing_token"],
    }
    for side in ("light", "heavy"):
        for part in ("gamma", "w1", "b1", "w2", "b2"):
            arrays[f"{side[0]}_{part}"] = g[f"L0_ffn_{side}_{part}"]
    arrays = {k: np.ascontiguousarray(v) for k, v in arrays.items()}
    nc = bacc.Bacc("TRN2", target_bir_lowering=False, num_devices=1)
    args = {k: nc.dram_tensor(f"in_{k}", v.shape, mybir.dt.from_np(v.dtype), kind="ExternalInput").ap()
            for k, v in arrays.items()}
    out = nc.dram_tensor("out", x.shape, F32, kind="ExternalOutput").ap()
    build(nc, out=out, **args)
    result = run(nc, [{f"in_{k}": v for k, v in arrays.items()}], core_ids=[0])
    return result.results[0]["out"]
```
